# Optimizing a Trainium2 kernel written in Bass

```python
import numpy as np
import jax
import jax.numpy as jnp

def _softmax(x, axis=-1):
    return jax.nn.softmax(x, axis=axis)

def _gelu(x):
    return jax.nn.gelu(x, approximate=True)

def _silu(x):
    return jax.nn.silu(x)

def _sigmoid(x):
    return jax.nn.sigmoid(x)

def _layernorm(x, axis=-1, eps=1e-05):
    m = jnp.mean(x, axis=axis, keepdims=True)
    v = jnp.var(x, axis=axis, keepdims=True)
    return (x - m) / jnp.sqrt(v + eps)

def _scatter_add(tgt, idx, src, axis=0):
    return tgt.at[idx].add(src)

def _segment_sum(src, seg, n):
    return jax.ops.segment_sum(src, seg, n)
kernel_name = 'mk_gnn_ffn_d1_gnn_r8_1608e5'

def setup_inputs(seed: int=0):
    np.random.seed(seed)
    _w = jnp.asarray

    def _rec_inputs():
        import jax
        import jax.numpy as jnp
        _gk = jax.random.key(seed)
        x = -0.0003929 + 0.9999 * jax.random.normal(jax.random.fold_in(_gk, 1), (4096, 512), jnp.float32)
        _s = jax.random.randint(jax.random.fold_in(_gk, 2), (32768,), 0, 4096, jnp.int32)
        _d = jax.random.randint(jax.random.fold_in(_gk, 3), (32768,), 0, 4096, jnp.int32)
        _loop = jnp.arange(4096, dtype=jnp.int32)
        src = jnp.concatenate([_s, _d, _loop])
        dst = jnp.concatenate([_d, _s, _loop])
        _o = jnp.argsort(dst, stable=True)
        src = src[_o]
        dst = dst[_o]
        edge_attr_8 = -4.48278e-06 + 1.00019 * jax.random.normal(jax.random.fold_in(_gk, 12), (69632, 8), jnp.float32)
        return (x, src, dst, edge_attr_8)
    x, src, dst, edge_attr_8 = _rec_inputs()

    def _L0_gnn_setup():
        import jax, jax.numpy as jnp
        import numpy as np
        L, C, H, E = (4096, 512, 8, 131072)
        D = C // H
        HID = 1024
        EPS = 1e-05

        def _ln(x, g, b):
            mu = jnp.mean(x, axis=-1, keepdims=True)
            var = jnp.var(x, axis=-1, keepdims=True)
            return (x - mu) * jax.lax.rsqrt(var + EPS) * g + b

        def _sparse_attention(z, row, col, bias, Wq, bq, Wk, bk, Wv, bv, Wo, bo):
            q = (z @ Wq + bq).reshape(L, H, D)
            k = (z @ Wk + bk).reshape(L, H, D)
            v = (z @ Wv + bv).reshape(L, H, D)
            scale = 1.0 / jnp.sqrt(jnp.asarray(D, z.dtype))
            scores = jnp.einsum('ehd,ehd->eh', q[row], k[col]) * scale + bias
            m = jax.ops.segment_max(scores, row, num_segments=L)
            p = jnp.exp(scores - m[row])
            ssum = jax.ops.segment_sum(p, row, num_segments=L)
            alpha = p / ssum[row]
            out = jax.ops.segment_sum(alpha[:, :, None] * v[col], row, num_segments=L)
            return out.reshape(L, C) @ Wo + bo
        key = jax.random.key(seed)
        ks = jax.random.split(key, 12)
        s = 0.02
        inp = {'x': jax.random.normal(ks[0], (L, C), jnp.float32), 'row_index': jnp.sort(jax.random.randint(ks[1], (E,), 0, L)), 'col_index': jax.random.randint(ks[2], (E,), 0, L), 'att_bias': jax.random.normal(ks[3], (E, H), jnp.float32), 'Wq': jax.random.normal(ks[4], (C, C), jnp.float32) * s, 'bq': jnp.zeros((C,), jnp.float32), 'Wk': jax.random.normal(ks[5], (C, C), jnp.float32) * s, 'bk': jnp.zeros((C,), jnp.float32), 'Wv': jax.random.normal(ks[6], (C, C), jnp.float32) * s, 'bv': jnp.zeros((C,), jnp.float32), 'Wo': jax.random.normal(ks[7], (C, C), jnp.float32) * s, 'bo': jnp.zeros((C,), jnp.float32), 'ln1_g': jnp.ones((C,), jnp.float32), 'ln1_b': jnp.zeros((C,), jnp.float32), 'ln2_g': jnp.ones((C,), jnp.float32), 'ln2_b': jnp.zeros((C,), jnp.float32), 'W1': jax.random.normal(ks[8], (C, HID), jnp.float32) * s, 'b1': jnp.zeros((HID,), jnp.float32), 'W2': jax.random.normal(ks[9], (HID, C), jnp.float32) * s, 'b2': jnp.zeros((C,), jnp.float32)}
        return inp
    _L0_gnn_all = _L0_gnn_setup()
    _L0_gnn_in = {k: v for k, v in _L0_gnn_all.items() if k in ('Wq', 'bq', 'Wk', 'bk', 'Wv', 'bv', 'Wo', 'bo', 'ln1_g', 'ln1_b', 'ln2_g', 'ln2_b', 'W1', 'b1', 'W2', 'b2')}
    del _L0_gnn_all

    def _L0_ffn_setup():
        import jax, jax.numpy as jnp
        import numpy as np
        K = 2
        EPS = 1e-06

        def _layernorm(x, gamma, beta):
            mu = jnp.mean(x, axis=-1, keepdims=True)
            var = jnp.mean(jnp.square(x - mu), axis=-1, keepdims=True)
            return (x - mu) * jax.lax.rsqrt(var + EPS) * gamma + beta
        key = jax.random.key(seed)
        ks = jax.random.split(key, 5)
        B, S, D, F, E = (8, 256, 512, 256, 8)
        x = jax.random.normal(ks[0], (B, S, D), dtype=jnp.float32)
        router_w = jax.random.normal(ks[1], (D, E), dtype=jnp.float32) * 0.02
        w1 = jax.random.normal(ks[2], (E, D, F), dtype=jnp.float32) * 0.02
        b1 = jnp.zeros((E, F), dtype=jnp.float32)
        w2 = jax.random.normal(ks[3], (E, F, D), dtype=jnp.float32) * 0.02
        b2 = jnp.zeros((E, D), dtype=jnp.float32)
        gamma = jnp.ones((E, D), dtype=jnp.float32)
        beta = jnp.zeros((E, D), dtype=jnp.float32)
        return {'x': x, 'router_w': router_w, 'w1': w1, 'b1': b1, 'w2': w2, 'b2': b2, 'gamma': gamma, 'beta': beta}
    _L0_ffn_all = _L0_ffn_setup()
    _L0_ffn_in = {k: v for k, v in _L0_ffn_all.items() if k in ('router_w', 'w1', 'b1', 'w2', 'b2', 'gamma', 'beta')}
    del _L0_ffn_all
    return {'x': x, 'src': src, 'dst': dst, 'edge_attr_8': edge_attr_8, 'L0_gnn_Wq': _L0_gnn_in['Wq'], 'L0_gnn_bq': _L0_gnn_in['bq'], 'L0_gnn_Wk': _L0_gnn_in['Wk'], 'L0_gnn_bk': _L0_gnn_in['bk'], 'L0_gnn_Wv': _L0_gnn_in['Wv'], 'L0_gnn_bv': _L0_gnn_in['bv'], 'L0_gnn_Wo': _L0_gnn_in['Wo'], 'L0_gnn_bo': _L0_gnn_in['bo'], 'L0_gnn_ln1_g': _L0_gnn_in['ln1_g'], 'L0_gnn_ln1_b': _L0_gnn_in['ln1_b'], 'L0_gnn_ln2_g': _L0_gnn_in['ln2_g'], 'L0_gnn_ln2_b': _L0_gnn_in['ln2_b'], 'L0_gnn_W1': _L0_gnn_in['W1'], 'L0_gnn_b1': _L0_gnn_in['b1'], 'L0_gnn_W2': _L0_gnn_in['W2'], 'L0_gnn_b2': _L0_gnn_in['b2'], 'L0_ffn_router_w': _L0_ffn_in['router_w'], 'L0_ffn_w1': _L0_ffn_in['w1'], 'L0_ffn_b1': _L0_ffn_in['b1'], 'L0_ffn_w2': _L0_ffn_in['w2'], 'L0_ffn_b2': _L0_ffn_in['b2'], 'L0_ffn_gamma': _L0_ffn_in['gamma'], 'L0_ffn_beta': _L0_ffn_in['beta']}

def reference(x, src, dst, edge_attr_8, L0_gnn_Wq, L0_gnn_bq, L0_gnn_Wk, L0_gnn_bk, L0_gnn_Wv, L0_gnn_bv, L0_gnn_Wo, L0_gnn_bo, L0_gnn_ln1_g, L0_gnn_ln1_b, L0_gnn_ln2_g, L0_gnn_ln2_b, L0_gnn_W1, L0_gnn_b1, L0_gnn_W2, L0_gnn_b2, L0_ffn_router_w, L0_ffn_w1, L0_ffn_b1, L0_ffn_w2, L0_ffn_b2, L0_ffn_gamma, L0_ffn_beta):
    import jax
    import jax.numpy as jnp

    def _L0_gnn_ref(x, att_bias, Wq, bq, Wk, bk, Wv, bv, Wo, bo, ln1_g, ln1_b, ln2_g, ln2_b, W1, b1, W2, b2, row_index, col_index):
        import jax, jax.numpy as jnp
        import numpy as np
        L, C, H, E = (4096, 512, 8, 131072)
        D = C // H
        HID = 1024
        EPS = 1e-05

        def _ln(x, g, b):
            mu = jnp.mean(x, axis=-1, keepdims=True)
            var = jnp.var(x, axis=-1, keepdims=True)
            return (x - mu) * jax.lax.rsqrt(var + EPS) * g + b

        def _sparse_attention(z, row, col, bias, Wq, bq, Wk, bk, Wv, bv, Wo, bo):
            q = (z @ Wq + bq).reshape(L, H, D)
            k = (z @ Wk + bk).reshape(L, H, D)
            v = (z @ Wv + bv).reshape(L, H, D)
            scale = 1.0 / jnp.sqrt(jnp.asarray(D, z.dtype))
            scores = jnp.einsum('ehd,ehd->eh', q[row], k[col]) * scale + bias
            m = jax.ops.segment_max(scores, row, num_segments=L)
            p = jnp.exp(scores - m[row])
            ssum = jax.ops.segment_sum(p, row, num_segments=L)
            alpha = p / ssum[row]
            out = jax.ops.segment_sum(alpha[:, :, None] * v[col], row, num_segments=L)
            return out.reshape(L, C) @ Wo + bo
        z = _ln(x, ln1_g, ln1_b)
        att = _sparse_attention(z, row_index, col_index, att_bias, Wq, bq, Wk, bk, Wv, bv, Wo, bo)
        x = x + att
        z = _ln(x, ln2_g, ln2_b)
        ff = jax.nn.silu(z @ W1 + b1) @ W2 + b2
        return x + ff

    def _L0_ffn_ref(x, router_w, w1, b1, w2, b2, gamma, beta):
        import jax, jax.numpy as jnp
        import numpy as np
        K = 2
        EPS = 1e-06

        def _layernorm(x, gamma, beta):
            mu = jnp.mean(x, axis=-1, keepdims=True)
            var = jnp.mean(jnp.square(x - mu), axis=-1, keepdims=True)
            return (x - mu) * jax.lax.rsqrt(var + EPS) * gamma + beta
        B, S, D = x.shape
        E = w1.shape[0]
        xf = x.reshape(-1, D)
        logits = xf @ router_w
        gate_vals, idx = jax.lax.top_k(logits, K)
        gates = jax.nn.softmax(gate_vals, axis=-1)
        out = jnp.zeros_like(xf)
        for e in range(E):
            h = jax.nn.relu(xf @ w1[e] + b1[e]) @ w2[e] + b2[e]
            y = _layernorm(xf + h, gamma[e], beta[e])
            w = jnp.sum(jnp.where(idx == e, gates, 0.0), axis=-1)
            out = out + w[:, None] * y
        return out.reshape(B, S, D)
    x = x + _L0_gnn_ref(_layernorm(x, axis=-1), edge_attr_8, L0_gnn_Wq, L0_gnn_bq, L0_gnn_Wk, L0_gnn_bk, L0_gnn_Wv, L0_gnn_bv, L0_gnn_Wo, L0_gnn_bo, L0_gnn_ln1_g, L0_gnn_ln1_b, L0_gnn_ln2_g, L0_gnn_ln2_b, L0_gnn_W1, L0_gnn_b1, L0_gnn_W2, L0_gnn_b2, src, dst)
    x = x + _L0_ffn_ref(_layernorm(x, axis=-1)[None], L0_ffn_router_w, L0_ffn_w1, L0_ffn_b1, L0_ffn_w2, L0_ffn_b2, L0_ffn_gamma, L0_ffn_beta)[0]
    return x

_drawn_inputs = setup_inputs


def setup_inputs(seed=0):
    import zlib

    import numpy as np

    out = dict(_drawn_inputs(seed))
    spreads = {'L0_gnn_bq': (0.0, 0.8),
     'L0_gnn_bk': (0.0, 0.8),
     'L0_gnn_bv': (0.0, 0.314),
     'L0_gnn_bo': (0.0, 0.1),
     'L0_gnn_ln1_g': (1.0, 0.6),
     'L0_gnn_ln1_b': (0.0, 0.668),
     'L0_gnn_ln2_g': (1.0, 0.6),
     'L0_gnn_ln2_b': (0.0, 0.8),
     'L0_gnn_b1': (0.0, 0.423),
     'L0_gnn_b2': (0.0, 0.1),
     'L0_ffn_b1': (0.0, 0.8),
     'L0_ffn_b2': (0.0, 0.324),
     'L0_ffn_gamma': (1.0, 0.2),
     'L0_ffn_beta': (0.0, 0.338)}
    factors = {'L0_gnn_Wq': 6.564, 'L0_gnn_Wk': 6.496, 'L0_ffn_w1': 2.721}
    for name, (base, spread) in spreads.items():
        noise = np.random.default_rng([zlib.crc32(name.encode()), seed]).standard_normal(out[name].shape)
        drawn = base * np.exp(spread * noise) if base else spread * noise
        out[name] = jnp.asarray(drawn.astype(out[name].dtype))
    for name, factor in factors.items():
        out[name] = (out[name] * factor).astype(out[name].dtype)
    return out
```

```python
import concourse.bass as bass
import concourse.mybir as mybir
from contextlib import ExitStack

F32, BF16, I32 = mybir.dt.float32, mybir.dt.bfloat16, mybir.dt.int32
ALU = mybir.AluOpType
ACT = mybir.ActivationFunctionType
AX = mybir.AxisListType

P = 128
NODES, C, HEADS = 4096, 512, 8
D = C // HEADS
EDGES = 69632
BLOCKS = NODES // P
IN_TILES = EDGES // P
GROUP = 2
SPAN = GROUP * P
GROUPS = -(-EDGES // SPAN) + BLOCKS
TILES = GROUPS * GROUP
RANGES = 16
RANGE_TILES = TILES // RANGES
REC = 2 + HEADS
PAD_ROW = -1.0


class Steps:

    def __init__(self, eng, sem, turn=None, per=0, base=0):
        self.eng, self.sem, self.turn, self.per, self.base, self.n = eng, sem, turn, per, base, 0

    def value(self):
        n = self.base + self.n
        return n if self.turn is None else self.turn * self.per + n

    def link(self, ins):
        self.n += 1
        ins.then_inc(self.sem, 1)
        self.eng.wait_ge(self.sem, self.value())


MOVES = 32


def open_block(nc, ctx, used):
    def clear():
        for s in used:
            nc.gpsimd.sem_clear(s)
        nc.all_engine_barrier()

    ctx.callback(clear)
    return ctx.enter_context(nc.Block())


def sort_edges(nc, moved, src_t, src_row, dst_t, bias_t, records, group_block):
    B = 16
    BATCHES = IN_TILES // B
    GC = -(-GROUPS // P)
    with ExitStack() as ctx:
        def sb(name, shape, dt):
            return ctx.enter_context(nc.sbuf_tensor(name, shape, dt))

        def ps(name, shape, dt=F32):
            return ctx.enter_context(nc.psum_tensor(name, shape, dt))

        used = []

        def sem(name):
            used.append(ctx.enter_context(nc.semaphore(name)))
            return used[-1]

        row_i = sb("row_i", [P, IN_TILES], I32)
        col_i = sb("col_i", [P, IN_TILES], I32)
        bias_in = sb("bias_in", [P, IN_TILES * HEADS], F32)
        row_f = sb("row_f", [P, IN_TILES], F32)
        blk_i = sb("blk_i", [P, IN_TILES], I32)
        low_i = sb("low_i", [P, IN_TILES], I32)
        blk_b = sb("blk_b", [P, IN_TILES], BF16)
        low_b = sb("low_b", [P, IN_TILES], BF16)
        iota_b = sb("iota_b", [P, P], BF16)
        iota_p = sb("iota_p", [P, 1], F32)
        earlier = sb("earlier", [P, P], F32)
        earlier_b = sb("earlier_b", [P, P], BF16)
        ones_f = sb("ones_f", [P, P], F32)
        ones_b = sb("ones_b", [P, 1], BF16)
        zeros_f = sb("zeros_f", [P, IN_TILES], F32)
        counts = sb("counts", [P, BLOCKS, IN_TILES + 1], F32)
        start = sb("start", [P, BLOCKS], F32)
        total = sb("total", [P, BLOCKS], F32)
        fill_i = sb("fill_i", [P, BLOCKS], I32)
        fill_s = sb("fill_s", [P, BLOCKS], I32)
        fill_f = sb("fill_f", [P, BLOCKS], F32)
        ends = sb("ends", [P, BLOCKS], F32)
        group_at = sb("group_at", [P, GC], F32)
        passed = sb("passed", [P, GC, BLOCKS], F32)
        group_f = sb("group_f", [P, GC], F32)
        group_i = sb("group_i", [P, GC], I32)
        low_hot = sb("low_hot", [P, 2, B, P], BF16)
        blk_hot = sb("blk_hot", [P, 2, B, BLOCKS], BF16)
        row_bc = sb("row_bc", [P, 2, B * P], I32)
        low_bc = sb("low_bc", [P, B * P], I32)
        low_hot_t = sb("low_hot_t", [P, 2, B * P], F32)
        same = sb("same", [P, 2, B, P], BF16)
        picked = sb("picked", [P, B, BLOCKS], F32)
        before = sb("before", [P, B], F32)
        place = sb("place", [P, B], I32)
        tile_of = sb("tile_of", [P, B], I32)
        part_of = sb("part_of", [P, B], I32)
        address = sb("address", [P, 2, B], I32)
        record = sb("record", [P, IN_TILES, REC], F32)
        staged = sb("staged", [P, 2, B, REC], F32)
        blank = sb("blank", [P, TILES // 4, REC], F32)

        hist = [ps(f"hist{b}", [P, B * BLOCKS]) for b in range(2)]
        ranks = [ps(f"ranks{b}", [P, B * BLOCKS]) for b in range(2)]
        within = [ps(f"within{b}", [P, B]) for b in range(2)]
        small = ps("small", [P, 2 * BLOCKS])

        s_rows, s_cols, s_bias, s_blank = sem("s_rows"), sem("s_cols"), sem("s_bias"), sem("s_blank")
        s_blanked, s_group = sem("s_blanked"), sem("s_group")
        s_iota, s_const, s_cut, s_dve, s_act = sem("s_iota"), sem("s_const"), sem("s_cut"), sem("s_dve"), sem("s_act")
        s_hot, s_hist, s_kept, s_hot2, s_ranks, s_addr, s_staged = (
            [sem(f"{n}{b}") for b in range(2)] for n in ("s_hot", "s_hist", "s_kept", "s_hot2", "s_ranks", "s_addr",
                                                       "s_staged"))
        s_total, s_small, s_start, s_groups = sem("s_total"), sem("s_small"), sem("s_start"), sem("s_groups")
        s_bc = [sem(f"s_bc{b}") for b in range(2)]
        s_record, s_passed = sem("s_record"), sem("s_passed")
        s_put = [moved[b * B:(b + 1) * B] for b in range(2)]
        block = open_block(nc, ctx, used)

        @block.sync
        def _(eng):
            eng.dma_start(row_i[:, :], src_t).then_inc(s_rows, 16)
            eng.dma_start(col_i[:, :], dst_t).then_inc(s_cols, 16)
            eng.dma_start(bias_in[:, :], bias_t).then_inc(s_bias, 16)
            eng.wait_ge(s_blank, 2)
            for q in range(4):
                eng.dma_start(records.rearrange("(p q t) w -> p q (t w)", p=P, q=4)[:, q, :],
                              blank[:, :, :].rearrange("p t w -> p (t w)")).then_inc(s_blanked, 16)
            rows = src_row.rearrange("(n w) -> n w", w=B * P)

            with eng.Fori(0, BATCHES // 2) as i:
                for b in range(2):
                    eng.wait_ge(s_addr[b], i)
                    eng.dma_start(row_bc[:, b, :],
                                  rows[bass.ds(i * 2 + b, 1), :].rearrange("a w -> (a w)").partition_broadcast(P)
                                  ).then_inc(s_bc[b], 16)
            eng.wait_ge(s_groups, 1)
            eng.dma_start(group_block.rearrange("(c p) -> p c", p=P), group_i[:, :],
                          allow_slow_non_contiguous=True).then_inc(s_group, 16)
            eng.wait_ge(s_group, 16)

        @block.gpsimd
        def _(eng):
            eng.iota(iota_b[:, :], pattern=[[1, P]], base=0, channel_multiplier=0,
                     allow_small_or_imprecise_dtypes=True).then_inc(s_iota, 1)
            eng.iota(iota_p[:, :], pattern=[[1, 1]], base=0, channel_multiplier=1,
                     allow_small_or_imprecise_dtypes=True).then_inc(s_iota, 1)
            eng.iota(group_at[:, :], pattern=[[P, GC]], base=0, channel_multiplier=1,
                     allow_small_or_imprecise_dtypes=True).then_inc(s_iota, 1)
            eng.memset(ones_f[:, :], 1.0).then_inc(s_const, 1)
            eng.memset(ones_b[:, :], 1.0).then_inc(s_const, 1)
            eng.memset(zeros_f[:, :], 0.0).then_inc(s_const, 1)
            eng.memset(blank[:, :, :], 0.0).then_inc(s_blank, 1)
            eng.wait_ge(s_blank, 1)
            eng.memset(blank[:, :, 1:2], PAD_ROW).then_inc(s_blank, 1)
            eng.wait_ge(s_const, 3)
            eng.affine_select(out=earlier[:, :], in_=ones_f[:, :], compare_op=ALU.is_gt, fill=0.0, base=0,
                              pattern=[[1, P]], channel_multiplier=-1).then_inc(s_cut, 1)
            eng.affine_select(out=earlier_b[:, :], in_=ones_f[:, :], compare_op=ALU.is_gt, fill=0.0, base=0,
                              pattern=[[1, P]], channel_multiplier=-1).then_inc(s_cut, 1)
            eng.wait_ge(s_blanked, 64)
            with eng.Fori(0, BATCHES // 2) as i:
                for b in range(2):
                    eng.wait_ge(s_addr[b], i + 1)
                    eng.wait_ge(s_staged[b], i + 1)
                    for u in range(B):
                        eng.sem_inc(s_passed, 1)
                        eng.indirect_dma_start(
                            records, bass.IndirectOffsetOnAxis(address[:, b, u:u + 1], 0),
                            staged[:, b, u, :], None,
                        ).then_inc(s_put[b][u], 16)
            for b in range(2):
                for u in range(B):
                    eng.wait_ge(s_put[b][u], 16 * (BATCHES // 2))

        @block.scalar
        def _(eng):
            eng.wait_ge(s_bias, 16)
            nc.scalar.copy(record[:, :, 2:REC], bias_in[:, :].rearrange("p (t h) -> p t h", h=HEADS)).then_inc(s_record, 1)
            with eng.Fori(0, BATCHES // 2) as i:
                for b in range(2):
                    eng.wait_ge(s_hist[b], i + 1)
                    nc.scalar.copy(counts[:, :, bass.ds(i * 2 * B + b * B + 1, B)].rearrange("p h t -> p t h"),
                                   hist[b][:, :].rearrange("p (t h) -> p t h", h=BLOCKS)).then_inc(s_kept[b], 1)

            eng.wait_ge(s_record, 3)
            with eng.Fori(0, BATCHES // 2) as i:
                for b in range(2):
                    for u in range(B):
                        eng.wait_ge(s_put[b][u], i * 16)
                    nc.scalar.copy(staged[:, b, :, :], record[:, bass.ds(i * 2 * B + b * B, B), :]).then_inc(s_staged[b], 1)

        @block.vector
        def _(eng):
            st = Steps(eng, s_dve)
            eng.wait_ge(s_rows, 16)
            nc.vector.tensor_copy(row_f[:, :], row_i[:, :]).then_inc(s_record, 1)
            st.link(nc.vector.tensor_scalar(blk_i[:, :], row_i[:, :], 7, None, ALU.arith_shift_right))
            st.link(nc.vector.tensor_scalar(low_i[:, :], row_i[:, :], P - 1, None, ALU.bitwise_and))
            st.link(nc.vector.tensor_copy(blk_b[:, :], blk_i[:, :]))
            st.link(nc.vector.tensor_copy(low_b[:, :], low_i[:, :]))
            st.link(nc.vector.tensor_copy(record[:, :, 1], row_f[:, :]))
            eng.wait_ge(s_cols, 16)
            nc.vector.tensor_copy(record[:, :, 0], col_i[:, :]).then_inc(s_record, 1)
            eng.wait_ge(s_iota, 3)

            def hot_block(i, b):
                return nc.vector.tensor_tensor(
                    blk_hot[:, b, :, :],
                    iota_b[:, 0:BLOCKS].unsqueeze(1).broadcast_to([P, B, BLOCKS]),
                    blk_b[:, bass.ds(i * 2 * B + b * B, B)].unsqueeze(2).broadcast_to([P, B, BLOCKS]), ALU.is_equal)

            with eng.Fori(0, BATCHES // 2) as i:
                for b in range(2):
                    eng.wait_ge(s_hist[b], i)
                    hot_block(i, b).then_inc(s_hot[b], 1)
                    nc.vector.tensor_tensor(
                        low_hot[:, b, :, :],
                        iota_b[:, :].unsqueeze(1).broadcast_to([P, B, P]),
                        low_b[:, bass.ds(i * 2 * B + b * B, B)].unsqueeze(2).broadcast_to([P, B, P]),
                        ALU.is_equal).then_inc(s_hot[b], 1)
            for b in range(2):
                eng.wait_ge(s_kept[b], BATCHES // 2)
            eng.wait_ge(s_const, 3)
            st.link(nc.vector.memset(counts[:, :, 0:1], 0.0))
            for h in range(BLOCKS):
                last = nc.vector.tensor_tensor_scan(counts[:, h, 1:], zeros_f[:, :], counts[:, h, 1:], 0.0,
                                                    ALU.add, ALU.add)
            st.link(last)
            nc.vector.tensor_copy(total[:, :], counts[:, :, IN_TILES]).then_inc(s_total, 1)
            eng.wait_ge(s_small, 1)
            st.link(nc.vector.tensor_scalar(fill_i[:, :], small[:, 0:BLOCKS], float(SPAN - 1), None, ALU.add))
            st.link(nc.vector.tensor_scalar(fill_s[:, :], fill_i[:, :], SPAN.bit_length() - 1, None, ALU.arith_shift_right))
            st.link(nc.vector.tensor_scalar(fill_f[:, :], fill_s[:, :], float(SPAN), None, ALU.mult))
            st.link(nc.vector.tensor_tensor_scan(ends[:, :], zeros_f[:, 0:BLOCKS], fill_f[:, :], 0.0, ALU.add, ALU.add))
            st.link(nc.vector.tensor_tensor(start[:, :], ends[:, :], fill_f[:, :], ALU.subtract))
            st.link(nc.vector.tensor_tensor(start[:, :], small[:, BLOCKS:], start[:, :], ALU.add))
            nc.vector.tensor_tensor(counts[:, :, 0:IN_TILES], counts[:, :, 0:IN_TILES],
                                    start[:, :].unsqueeze(2).broadcast_to([P, BLOCKS, IN_TILES]),
                                    ALU.add).then_inc(s_start, 1)
            st.link(nc.vector.tensor_scalar(group_at[:, :], group_at[:, :], float(SPAN), None, ALU.mult))
            st.link(nc.vector.tensor_tensor(passed[:, :, :], group_at[:, :].unsqueeze(2).broadcast_to([P, GC, BLOCKS]),
                                            ends[:, :].unsqueeze(1).broadcast_to([P, GC, BLOCKS]), ALU.is_ge))
            st.link(nc.vector.tensor_reduce(group_f[:, :], passed[:, :, :], AX.X, ALU.add))
            nc.vector.tensor_scalar(group_i[:, :], group_f[:, :], float(BLOCKS - 1), None, ALU.min).then_inc(s_groups, 1)
            eng.wait_ge(s_cut, 2)
            done = st.n

            with eng.Fori(0, BATCHES // 2) as i:
                st2 = Steps(eng, s_act, i, 14)
                for b in range(2):
                    eng.wait_ge(s_bc[b], i * 16 + 16)
                    st2.link(nc.vector.tensor_scalar(low_bc[:, :], row_bc[:, b, :], P - 1, None, ALU.bitwise_and))
                    nc.vector.tensor_scalar(low_hot_t[:, b, :], low_bc[:, :], iota_p[:, :], None,
                                            ALU.is_equal).then_inc(s_hot2[b], 1)
                    for u in range(B):
                        last = nc.vector.scalar_tensor_tensor(
                            same[:, b, u, :], row_bc[:, b, u * P:(u + 1) * P],
                            row_f[:, bass.ds(i * 2 * B + b * B + u, 1)], earlier_b[:, :], ALU.is_equal, ALU.mult)
                    last.then_inc(s_hot2[b], 1)
                    st2.link(hot_block(i, b))
                    eng.wait_ge(s_ranks[b], i + 1)
                    st2.link(nc.vector.tensor_tensor(picked[:, :, :],
                                                     ranks[b][:, :].rearrange("p (t h) -> p t h", h=BLOCKS),
                                                     blk_hot[:, b, :, :], ALU.mult))
                    st2.link(nc.vector.tensor_reduce(before[:, :], picked[:, :, :], AX.X, ALU.add))
                    st2.link(nc.vector.tensor_tensor(place[:, :], within[b][:, :], before[:, :], ALU.add))
                    st2.link(nc.vector.tensor_scalar(tile_of[:, :], place[:, :], 7, None, ALU.arith_shift_right))
                    st2.link(nc.vector.tensor_scalar(part_of[:, :], place[:, :], P - 1, None, ALU.bitwise_and))
                    for u in range(B):
                        eng.wait_ge(s_put[b][u], i * 16)
                    nc.vector.scalar_tensor_tensor(address[:, b, :], part_of[:, :], float(TILES),
                                                   tile_of[:, :], ALU.mult, ALU.add).then_inc(s_addr[b], 1)

        @block.tensor
        def _(eng):
            with eng.Fori(0, BATCHES // 2) as i:
                for b in range(2):
                    eng.wait_ge(s_hot[b], i * 2 + 2)
                    eng.wait_ge(s_kept[b], i)
                    for u in range(B):
                        last = nc.tensor.matmul(hist[b][:, u * BLOCKS:(u + 1) * BLOCKS], low_hot[:, b, u, :],
                                                blk_hot[:, b, u, :], start=True, stop=True)
                    last.then_inc(s_hist[b], 1)
            eng.wait_ge(s_total, 1)
            eng.wait_ge(s_cut, 2)
            nc.tensor.matmul(small[:, 0:BLOCKS], ones_f[:, :], total[:, :], start=True, stop=True)
            nc.tensor.matmul(small[:, BLOCKS:], earlier[:, :], total[:, :], start=True, stop=True).then_inc(s_small, 1)
            eng.wait_ge(s_start, 1)
            with eng.Fori(0, BATCHES // 2) as i:
                for b in range(2):
                    eng.wait_ge(s_hot2[b], i * 2 + 2)
                    eng.wait_ge(s_addr[b], i)
                    for u in range(B):
                        nc.tensor.matmul(ranks[b][:, u * BLOCKS:(u + 1) * BLOCKS], low_hot_t[:, b, u * P:(u + 1) * P],
                                         counts[:, :, bass.ds(i * 2 * B + b * B + u, 1)].rearrange("p h a -> p (h a)"),
                                         start=True, stop=True)
                    for u in range(B):
                        last = nc.tensor.matmul(within[b][:, u:u + 1], same[:, b, u, :], ones_b[:, :],
                                                start=True, stop=True)
                    last.then_inc(s_ranks[b], 1)


NORM_STEPS = 5


def norm_scale(nc, eng, st, passed, s_var, s_root, value, x, stats, mean_var, root, out):
    st.link(nc.vector.bn_stats(stats, x))
    eng.sem_inc(passed, 1)
    nc.vector.bn_aggr(mean_var, stats).then_inc(s_var, 1)
    eng.wait_ge(s_root, value)
    st.link(nc.vector.reciprocal(root, root))
    return nc.vector.tensor_scalar(out, x, mean_var[:, 0:1], root, ALU.subtract, ALU.mult)


def project_qkv(nc, x, ln_g, ln_b, wq, bq, wk, bk, wv, bv, z0, q, k, v):
    EPS = 1e-5
    KC = C // P
    ROWS = NODES // P
    with ExitStack() as ctx:
        def sb(name, shape, dt=F32):
            return ctx.enter_context(nc.sbuf_tensor(name, shape, dt))

        def ps(name, shape, dt=F32):
            return ctx.enter_context(nc.psum_tensor(name, shape, dt))

        used = []

        def sem(name):
            used.append(ctx.enter_context(nc.semaphore(name)))
            return used[-1]

        def sem2(name):
            return [sem(f"{name}{b}") for b in range(2)]

        w = sb("qkv_w", [P, 3, KC, C])
        bias = sb("qkv_bias", [P, 3, C])
        gain, shift = sb("qkv_gain", [P, C]), sb("qkv_shift", [P, C])
        ones, ident = sb("qkv_ones", [P, P]), sb("qkv_ident", [P, P])
        eps = sb("qkv_eps", [P, 1])
        xt = sb("qkv_x", [P, 2, C])
        z0t = sb("qkv_z0", [P, 2, C])
        zn = sb("qkv_zn", [P, C])
        zt = sb("qkv_z", [P, 2, C])
        zT = sb("qkv_zT", [P, 2, C])
        out = sb("qkv_out", [P, 2, 3, C])
        stats, mean_var, root = sb("qkv_stats", [P, 6]), sb("qkv_mv", [P, 2]), sb("qkv_root", [P, 1])
        turned = [ps(f"qkv_turned{b}", [P, C]) for b in range(2)]
        prod = [ps(f"qkv_prod{n}", [P, C]) for n in range(6)]

        s_w, s_c, s_cut, s_b, s_dve, s_passed, s_var, s_root = (
            sem(f"qkv_s_{n}") for n in ("w", "c", "cut", "b", "dve", "passed", "var", "root"))
        s_x, s_z0, s_z, s_turn, s_zT, s_stored_z0 = (
            sem2(f"qkv_s_{n}") for n in ("x", "z0", "z", "turn", "zT", "stored_z0"))
        s_prod, s_out, s_stored = ([sem(f"qkv_s_{n}{m}") for m in range(6)] for n in ("prod", "out", "stored"))
        block = open_block(nc, ctx, used)

        def tile_rows(a, j, c):
            return a.rearrange("(n p) c -> n p c", p=P)[bass.ds(j * 2 + c, 1), :, :].rearrange("a p c -> (a p) c")

        @block.sync
        def _(eng):
            def load_x(j, c):
                b, k_ = c % 2, j + c // 2
                eng.wait_ge(s_z0[b], k_)
                eng.dma_start(xt[:, b, :], tile_rows(x, j, c)).then_inc(s_x[b], 16)

            eng.dma_start(xt[:, 0, :], x[0:P, :]).then_inc(s_x[0], 16)
            eng.dma_start(xt[:, 1, :], x[P:2 * P, :]).then_inc(s_x[1], 16)
            for dst, a in ((gain, ln_g), (shift, ln_b)):
                eng.dma_start(dst[:, :], a.partition_broadcast(P)).then_inc(s_b, 16)
            for n, a in enumerate((wq, wk, wv)):
                eng.dma_start(w[:, n, :, :], a.rearrange("(k p) n -> p k n", p=P)).then_inc(s_w, 16)
            for n, a in enumerate((bq, bk, bv)):
                eng.dma_start(bias[:, n, :], a.partition_broadcast(P)).then_inc(s_b, 16)

            def store(j, c):
                b, k_ = c % 2, j + c // 2
                eng.wait_ge(s_z0[b], k_ + 1)
                eng.dma_start(tile_rows(z0, j, c), z0t[:, b, :]).then_inc(s_stored_z0[b], 16)
                for n, a in enumerate((q, k, v)):
                    eng.wait_ge(s_out[b * 3 + n], k_ + 1)
                    eng.dma_start(tile_rows(a, j, c), out[:, b, n, :]).then_inc(s_stored[b * 3 + n], 16)

            with eng.Fori(0, ROWS // 2 - 1) as j:
                for c in range(2):
                    load_x(j, c + 2)
                    store(j, c)
            for c in range(2):
                store(ROWS // 2 - 1, c)
            for b in range(2):
                eng.wait_ge(s_stored_z0[b], 16 * (ROWS // 2))
            for m in range(6):
                eng.wait_ge(s_stored[m], 16 * (ROWS // 2))

        @block.gpsimd
        def _(eng):
            eng.memset(ones[:, :], 1.0).then_inc(s_c, 1)
            eng.memset(eps[:, :], EPS).then_inc(s_c, 1)
            eng.wait_ge(s_c, 2)
            eng.affine_select(out=ident[:, :], in_=ones[:, :], compare_op=ALU.is_equal, fill=0.0, base=0,
                              pattern=[[1, P]], channel_multiplier=-1).then_inc(s_cut, 1)

        @block.vector
        def _(eng):
            def norms(st, j, c, done):
                b, k_ = c % 2, j + c // 2
                eng.wait_ge(s_x[b], k_ * 16 + 16)
                eng.wait_ge(s_stored_z0[b], k_ * 16)
                norm_scale(nc, eng, st, s_passed, s_var, s_root, done + 1, xt[:, b, :], stats[:, :], mean_var[:, :], root[:, :],
                           z0t[:, b, :]).then_inc(s_z0[b], 1)
                eng.wait_ge(s_z0[b], k_ + 1)
                st.link(norm_scale(nc, eng, st, s_passed, s_var, s_root, done + 2, z0t[:, b, :], stats[:, :], mean_var[:, :],
                                   root[:, :], zn[:, :]))
                st.link(nc.vector.tensor_tensor(zn[:, :], zn[:, :], gain[:, :], ALU.mult))
                eng.wait_ge(s_turn[b], k_)
                nc.vector.tensor_tensor(zt[:, b, :], zn[:, :], shift[:, :], ALU.add).then_inc(s_z[b], 1)

            def leave(j, c):
                b, k_ = c % 2, j + c // 2
                for n in range(3):
                    m = b * 3 + n
                    eng.wait_ge(s_prod[m], k_ + 1)
                    eng.wait_ge(s_stored[m], k_ * 16)
                    nc.vector.scalar_tensor_tensor(out[:, b, n, :], prod[m][:, :], float(D) ** -0.5 if n == 0 else 1.0,
                                                   bias[:, n, :], ALU.mult, ALU.add).then_inc(s_out[m], 1)

            STEPS = 6
            pre = Steps(eng, s_dve)
            eng.wait_ge(s_b, 80)
            pre.link(nc.vector.tensor_scalar(bias[:, 0, :], bias[:, 0, :], float(D) ** -0.5, None, ALU.mult))
            norms(pre, 0, 0, 0)
            assert pre.n == STEPS + 1
            with eng.Fori(0, ROWS // 2 - 1) as j:
                st = Steps(eng, s_dve, j, 2 * STEPS, STEPS + 1)
                for c in range(2):
                    norms(st, j, c + 1, j * 4 + 2 * (c + 1))
                    leave(j, c)
            post = Steps(eng, s_dve, None, 0, STEPS + 1 + (ROWS // 2 - 1) * 2 * STEPS)
            last = ROWS // 2 - 1
            norms(post, last, 1, last * 4 + 2)
            for c in range(2):
                leave(last, c)

        @block.scalar
        def _(eng):
            eng.wait_ge(s_c, 2)

            def roots(done):
                for n in range(2):
                    eng.wait_ge(s_var, done + n + 1)
                    nc.scalar.activation(root[:, :], mean_var[:, 1:2], ACT.Sqrt, bias=eps[:, :]).then_inc(s_root, 1)

            def keep(j, c):
                b, k_ = c % 2, j + c // 2
                eng.wait_ge(s_turn[b], k_ + 1)
                eng.wait_ge(s_prod[b * 3 + 2], k_)
                nc.scalar.copy(zT[:, b, :], turned[b][:, :]).then_inc(s_zT[b], 1)

            roots(0)
            with eng.Fori(0, ROWS // 2 - 1) as j:
                for c in range(2):
                    keep(j, c)
                    roots(j * 4 + 2 * (c + 1))
            last = ROWS // 2 - 1
            keep(last, 0)
            roots(last * 4 + 2)
            keep(last, 1)

        @block.tensor
        def _(eng):
            eng.wait_ge(s_cut, 1)
            eng.wait_ge(s_w, 48)
            with eng.Fori(0, ROWS // 2) as j:
                for b in range(2):
                    eng.wait_ge(s_z[b], j + 1)
                    eng.wait_ge(s_zT[b], j)
                    for n in range(KC):
                        last = nc.tensor.transpose(turned[b][:, n * P:(n + 1) * P], zt[:, b, n * P:(n + 1) * P], ident[:, :])
                    last.then_inc(s_turn[b], 1)
                    eng.wait_ge(s_zT[b], j + 1)
                    for n in range(3):
                        m = b * 3 + n
                        eng.wait_ge(s_out[m], j)
                        for kc in range(KC):
                            last = nc.tensor.matmul(prod[m][:, :], zT[:, b, kc * P:(kc + 1) * P], w[:, n, kc, :],
                                                    start=(kc == 0), stop=(kc == KC - 1))
                        last.then_inc(s_prod[m], 1)


def attention(nc, moved, count, records, group_block, q, k, v, mixed):
    U = 8
    TURN = 2 * U
    TURNS = TILES // TURN
    assert TILES % TURN == 0
    BIG = 3.0e38
    k_from = count
    v_from = count + 16 * TURNS
    LANE = RANGE_TILES * P
    with ExitStack() as ctx:
        def sb(name, shape, dt, on=ctx):
            return on.enter_context(nc.sbuf_tensor(name, shape, dt))

        def ps(name, shape, dt=F32, on=ctx):
            return on.enter_context(nc.psum_tensor(name, shape, dt))

        def sem(name, on=ctx):
            used.append(on.enter_context(nc.semaphore(name)))
            return used[-1]

        rec = sb("at_rec", [P, TILES, REC], F32)
        groups = sb("groups", [1, GROUPS], I32)
        low_neg = sb("low_neg", [P, TILES], F32)
        weight = sb("weight", [P, TILES, HEADS], F32)
        iota_f = sb("iota_f", [P, P], F32)
        ident = sb("ident", [P, P], F32)
        ident_b = sb("ident_b", [P, P], BF16)
        ones = sb("ones", [P, P], F32)

        used = []
        with ExitStack() as part:
            q_sb = sb("q_sb", [P, BLOCKS, C], F32, part)
            row_i = sb("at_row_i", [P, TILES], I32, part)
            low_f = sb("at_low_f", [P, TILES], F32, part)
            padded = sb("padded", [P, TILES], F32, part)
            index = sb("k_index", [P, 2, U], I32, part)
            k_sb = sb("k_sb", [P, TURN, C], F32, part)
            away = sb("away", [P, 2, P], F32, part)
            hot = sb("hot", [P, 2, P], BF16, part)
            hot_t = sb("hot_t", [P, 2, P], F32, part)
            product = sb("product", [P, 2, C], F32, part)
            turned = [ps(f"turned{b}", [P, P], BF16, part) for b in range(2)]
            q_edge = [ps(f"q_edge{b}", [P, C], F32, part) for b in range(2)]
            s_const, s_cut = sem("a_const", part), sem("a_cut", part)
            s_rec, s_grp, s_q = sem("a_rec", part), sem("a_grp", part), sem("a_q", part)
            s_dve, s_low, s_index = sem("a_dve", part), sem("a_low", part), sem("a_index", part)
            s_k = moved[:TURN]
            s_act, s_passed = sem("a_act", part), sem("a_passed", part)
            s_hot, s_turned, s_hot_t, s_qe, s_prod, s_score = (
                [sem(f"{n}{b}", part) for b in range(2)]
                for n in ("a_hot", "a_turned", "a_hot_t", "a_qe", "a_prod", "a_score"))
            block = open_block(nc, part, used)

            @block.sync
            def _(eng):
                eng.dma_start(rec[:, :, :], records.rearrange("(p t) w -> p t w", p=P)).then_inc(s_rec, 16)
                eng.dma_start(groups[0:1, :], group_block[0:GROUPS].unsqueeze(0)).then_inc(s_grp, 16)
                eng.dma_start(q_sb[:, :, :], q.rearrange("(b p) c -> p b c", p=P)).then_inc(s_q, 16)

            @block.gpsimd
            def _(eng):
                eng.memset(ones[:, :], 1.0).then_inc(s_const, 1)
                eng.iota(iota_f[:, :], pattern=[[1, P]], base=0, channel_multiplier=0,
                         allow_small_or_imprecise_dtypes=True).then_inc(s_const, 1)
                eng.wait_ge(s_const, 2)
                for m in (ident, ident_b):
                    eng.affine_select(out=m[:, :], in_=ones[:, :], compare_op=ALU.is_equal, fill=0.0, base=0,
                                      pattern=[[1, P]], channel_multiplier=-1).then_inc(s_cut, 1)
                eng.wait_ge(s_rec, 16)
                with eng.Fori(0, TURNS) as i:
                    for half in range(2):
                        for n in range(U):
                            eng.wait_ge(s_k[half * U + n], i * 16 + k_from)
                        eng.tensor_copy(index[:, half, :], rec[:, bass.ds(i * TURN + half * U, U), 0]
                                        ).then_inc(s_index, 1)
                        eng.wait_ge(s_index, i * 2 + half + 1)
                        for n in range(U):
                            u = half * U + n
                            eng.wait_ge(s_score[half], i * U)
                            eng.sem_inc(s_passed, 1)
                            eng.indirect_dma_start(k_sb[:, u, :], None, k,
                                                   bass.IndirectOffsetOnAxis(index[:, half, n:n + 1], 0)
                                                   ).then_inc(s_k[u], 16)

            @block.vector
            def _(eng):
                st = Steps(eng, s_dve)
                eng.wait_ge(s_rec, 16)
                row = rec[:, :, 1]
                st.link(nc.vector.tensor_copy(row_i[:, :], row))
                st.link(nc.vector.tensor_scalar(row_i[:, :], row_i[:, :], P - 1, None, ALU.bitwise_and))
                st.link(nc.vector.tensor_copy(low_f[:, :], row_i[:, :]))
                st.link(nc.vector.tensor_scalar(padded[:, :], row, 0.0, float(4 * P), ALU.is_lt, ALU.mult))
                st.link(nc.vector.tensor_tensor(low_f[:, :], low_f[:, :], padded[:, :], ALU.add))
                nc.vector.tensor_scalar(low_neg[:, :], low_f[:, :], -1.0, None, ALU.mult).then_inc(s_low, 1)
                with eng.Fori(0, TURNS) as i:
                    for half in range(2):
                        for n in range(U):
                            u = half * U + n
                            b = u % 2
                            eng.wait_ge(s_k[u], i * 16 + k_from + 16)
                            eng.wait_ge(s_qe[b], i * U + u // 2 + 1)
                            nc.vector.tensor_tensor(product[:, b, :], q_edge[b][:, :], k_sb[:, u, :],
                                                    ALU.mult).then_inc(s_prod[b], 1)
                            eng.wait_ge(s_prod[b], i * U + u // 2 + 1)
                            nc.vector.tensor_reduce(weight[:, bass.ds(i * TURN + u, 1), :].rearrange("p a h -> p (a h)"),
                                                    product[:, b, :].rearrange("p (h d) -> p h d", d=D), AX.X,
                                                    ALU.add).then_inc(s_score[half], 1)

            @block.scalar
            def _(eng):
                eng.wait_ge(s_low, 1)
                eng.wait_ge(s_const, 2)
                with eng.Fori(0, TURNS) as i:
                    st = Steps(eng, s_act, i, TURN)
                    for u in range(TURN):
                        b = u % 2
                        at = low_neg[:, bass.ds(i * TURN + u, 1)]
                        st.link(nc.scalar.activation(away[:, b, :], iota_f[:, :], ACT.Abs, bias=at))
                        eng.wait_ge(s_turned[b], i * U + u // 2)
                        nc.scalar.activation(hot[:, b, :], away[:, b, :], ACT.Relu, bias=1.0, scale=-1.0
                                             ).then_inc(s_hot[b], 1)
                        eng.wait_ge(s_turned[b], i * U + u // 2 + 1)
                        eng.wait_ge(s_qe[b], i * U + u // 2)
                        nc.scalar.copy(hot_t[:, b, :], turned[b][:, :]).then_inc(s_hot_t[b], 1)

            @block.tensor
            def _(eng):
                eng.wait_ge(s_cut, 2)
                eng.wait_ge(s_grp, 16)
                eng.wait_ge(s_q, 16)

                with eng.Fori(0, TURNS) as i:
                    for u in range(TURN):
                        b = u % 2
                        if u % GROUP == 0:
                            at = eng.value_load(groups[0:1, bass.ds(i * (TURN // GROUP) + u // GROUP, 1)],
                                                min_val=0, max_val=BLOCKS - 1)
                        eng.wait_ge(s_hot[b], i * U + u // 2 + 1)
                        eng.wait_ge(s_hot_t[b], i * U + u // 2)
                        nc.tensor.transpose(turned[b][:, :], hot[:, b, :], ident_b[:, :]).then_inc(s_turned[b], 1)
                        eng.wait_ge(s_hot_t[b], i * U + u // 2 + 1)
                        eng.wait_ge(s_prod[b], i * U + u // 2)
                        nc.tensor.matmul(q_edge[b][:, :], hot_t[:, b, :],
                                         q_sb[:, bass.ds(at, 1), :].rearrange("p a c -> p (a c)"),
                                         start=True, stop=True).then_inc(s_qe[b], 1)

        used = []
        with ExitStack() as part:
            stage_s = sb("stage_s", [P, 2, RANGES, HEADS], F32, part)
            stage_k = sb("stage_k", [P, 2, RANGES, HEADS], F32, part)
            stage_p = sb("stage_p", [P, 2, P], F32, part)
            keys = sb("keys", [P, LANE], F32, part)
            score = sb("score", [P, LANE], F32, part)
            cont = sb("cont", [P, LANE + 1], F32, part)
            ahead = sb("ahead", [P, LANE], F32, part)
            back = sb("back", [P, LANE], F32, part)
            row4 = sb("row4", [1, 4, HEADS, RANGES], F32, part)
            linked = sb("linked", [1, HEADS, RANGES + 1], F32, part)
            whole = sb("whole", [1, HEADS, RANGES], F32, part)
            pass_f = sb("pass_f", [1, HEADS, RANGES], F32, part)
            pass_b = sb("pass_b", [1, HEADS, RANGES], F32, part)
            state = sb("state", [1, 2, HEADS, RANGES], F32, part)
            carry = sb("carry", [1, 2, RANGES, HEADS], F32, part)
            carried = sb("carried", [P, 2], F32, part)
            turn_s = [ps(f"turn_s{b}", [P, P], F32, part) for b in range(2)]
            turn_k = [ps(f"turn_k{b}", [P, P], F32, part) for b in range(2)]
            ends4 = ps("ends4", [1, 4 * P], F32, part)
            carry_ps = ps("carry_ps", [P, 2], F32, part)
            s_dve, s_loc, s_ends, s_carry, s_carried, s_sub = (
                sem(n, part) for n in ("m_dve", "m_loc", "m_ends", "m_carry", "m_carried", "m_sub"))
            s_sum, s_row, s_turn, s_keep_s, s_keep_k, s_exp, s_back, s_keep = (
                [sem(f"{n}{b}", part) for b in range(2)]
                for n in ("m_sum", "m_row", "m_turn", "m_keep_s", "m_keep_k", "m_exp", "m_back", "m_keep"))
            block = open_block(nc, part, used)
            HALF = RANGE_TILES // 2

            def by_range(x):
                return x.rearrange("p (c j) h -> p c j h", c=RANGES)

            rec_range = by_range(rec[:, :, :])

            @block.tensor
            def _(eng):
                with eng.Fori(0, HALF) as i:
                    for b in range(2):
                        eng.wait_ge(s_sum[b], i + 1)
                        eng.wait_ge(s_row[b], i + 1)
                        eng.wait_ge(s_keep_s[b], i)
                        eng.wait_ge(s_keep_k[b], i)
                        nc.tensor.transpose(turn_s[b][:, :], stage_s[:, b, :, :].rearrange("p c h -> p (c h)"), ident[:, :])
                        nc.tensor.transpose(turn_k[b][:, :], stage_k[:, b, :, :].rearrange("p c h -> p (c h)"),
                                            ident[:, :]).then_inc(s_turn[b], 1)
                eng.wait_ge(s_loc, 2)
                for n, x in enumerate((ahead[:, LANE - 1:LANE], back[:, 0:1], keys[:, 0:1], keys[:, LANE - 1:LANE])):
                    last = nc.tensor.transpose(ends4[0:1, n * P:(n + 1) * P], x, ident[:, :])
                last.then_inc(s_ends, 1)
                eng.wait_ge(s_carry, 1)
                for n in range(2):
                    last = nc.tensor.matmul(carry_ps[:, n:n + 1], carry[0:1, n, :, :].rearrange("p c h -> p (c h)"),
                                            ones[0:1, 0:1], start=True, stop=True)
                last.then_inc(s_carried, 1)
                with eng.Fori(0, HALF) as i:
                    for b in range(2):
                        eng.wait_ge(s_exp[b], i + 1)
                        eng.wait_ge(s_keep[b], i)
                        nc.tensor.transpose(turn_s[b][:, :], stage_p[:, b, :], ident[:, :]).then_inc(s_back[b], 1)

            @block.scalar
            def _(eng):
                with eng.Fori(0, HALF) as i:
                    for b in range(2):
                        eng.wait_ge(s_turn[b], i)
                        nc.scalar.copy(stage_k[:, b, :, :],
                                       rec_range[:, :, bass.ds(i * 2 + b, 1), 1].broadcast_to([P, RANGES, HEADS])
                                       ).then_inc(s_row[b], 1)
                        eng.wait_ge(s_turn[b], i + 1)
                        nc.scalar.copy(keys[:, bass.ds((i * 2 + b) * P, P)], turn_k[b][:, :]).then_inc(s_keep_k[b], 1)
                eng.wait_ge(s_sub, 1)
                with eng.Fori(0, HALF) as i:
                    for b in range(2):
                        eng.wait_ge(s_back[b], i)
                        nc.scalar.activation(stage_p[:, b, :], score[:, bass.ds((i * 2 + b) * P, P)], ACT.Exp
                                             ).then_inc(s_exp[b], 1)

            @block.vector
            def _(eng):
                st = Steps(eng, s_dve)
                with eng.Fori(0, HALF) as i:
                    for b in range(2):
                        eng.wait_ge(s_turn[b], i)
                        j = bass.ds(i * 2 + b, 1)
                        nc.vector.tensor_tensor(stage_s[:, b, :, :],
                                                by_range(weight[:, :, :])[:, :, j, :].rearrange("p c a h -> p c (a h)"),
                                                rec_range[:, :, j, 2:REC].rearrange("p c a h -> p c (a h)"),
                                                ALU.add).then_inc(s_sum[b], 1)
                        eng.wait_ge(s_turn[b], i + 1)
                        nc.vector.tensor_copy(score[:, bass.ds((i * 2 + b) * P, P)], turn_s[b][:, :]).then_inc(s_keep_s[b], 1)
                for b in range(2):
                    eng.wait_ge(s_keep_k[b], HALF)
                    eng.wait_ge(s_keep_s[b], HALF)
                st.link(nc.vector.memset(cont[:, :], 1.0))
                st.link(nc.vector.tensor_tensor(cont[:, 1:LANE], keys[:, 1:], keys[:, 0:LANE - 1], ALU.is_equal))
                st.link(nc.vector.tensor_scalar(cont[:, :], cont[:, :], 1.0, BIG, ALU.subtract, ALU.mult))
                nc.vector.tensor_tensor_scan(ahead[:, :], cont[:, 0:LANE], score[:, :], -BIG, ALU.add, ALU.max).then_inc(s_loc, 1)
                nc.vector.tensor_tensor_scan(back[:, ::-1], cont[:, LANE:0:-1], score[:, ::-1], -BIG, ALU.add, ALU.max).then_inc(s_loc, 1)
                eng.wait_ge(s_ends, 1)
                st.link(nc.vector.tensor_copy(row4[:, :, :, :], ends4[0:1, :].rearrange("p (n c h) -> p n h c", n=4, c=RANGES)))
                first, last = row4[0:1, 2, :, :], row4[0:1, 3, :, :]
                st.link(nc.vector.memset(linked[:, :, :], 0.0))
                st.link(nc.vector.tensor_tensor(linked[:, :, 1:RANGES], first[:, :, 1:], last[:, :, 0:RANGES - 1], ALU.is_equal))
                st.link(nc.vector.tensor_tensor(whole[:, :, :], first, last, ALU.is_equal))
                for to, at in ((pass_f, linked[:, :, 0:RANGES]), (pass_b, linked[:, :, 1:])):
                    st.link(nc.vector.tensor_tensor(to[:, :, :], whole[:, :, :], at, ALU.mult))
                    st.link(nc.vector.tensor_scalar(to[:, :, :], to[:, :, :], 1.0, BIG, ALU.subtract, ALU.mult))
                st.link(nc.vector.tensor_scalar(linked[:, :, :], linked[:, :, :], 1.0, BIG, ALU.subtract, ALU.mult))

                def flat(x):
                    return x.rearrange("p h c -> p (h c)")

                st.link(nc.vector.tensor_tensor_scan(flat(state[:, 0, :, :]), flat(pass_f[:, :, :]),
                                                     flat(row4[:, 0, :, :]), 0.0, ALU.add, ALU.max))
                st.link(nc.vector.tensor_tensor_scan(flat(state[:, 1, :, :])[:, ::-1], flat(pass_b[:, :, :])[:, ::-1],
                                                     flat(row4[:, 1, :, :])[:, ::-1], 0.0, ALU.add, ALU.max))
                st.link(nc.vector.memset(carry[:, :, :, :], -BIG))
                st.link(nc.vector.tensor_tensor(carry[:, 0, 1:, :].rearrange("p c h -> p h c"), state[:, 0, :, 0:RANGES - 1],
                                                linked[:, :, 1:RANGES], ALU.add))
                nc.vector.tensor_tensor(carry[:, 1, 0:RANGES - 1, :].rearrange("p c h -> p h c"), state[:, 1, :, 1:],
                                        linked[:, :, 1:RANGES], ALU.add).then_inc(s_carry, 1)
                eng.wait_ge(s_carried, 1)
                st.link(nc.vector.tensor_copy(carried[:, :], carry_ps[:, :]))
                st.link(nc.vector.tensor_tensor_scan(ahead[:, :], cont[:, 0:LANE], score[:, :], carried[:, 0:1], ALU.add, ALU.max))
                st.link(nc.vector.tensor_tensor_scan(back[:, ::-1], cont[:, LANE:0:-1], score[:, ::-1], carried[:, 1:2],
                                                     ALU.add, ALU.max))
                st.link(nc.vector.tensor_tensor(ahead[:, :], ahead[:, :], back[:, :], ALU.max))
                nc.vector.tensor_tensor(score[:, :], score[:, :], ahead[:, :], ALU.subtract).then_inc(s_sub, 1)
                with eng.Fori(0, HALF) as i:
                    for b in range(2):
                        eng.wait_ge(s_back[b], i + 1)
                        nc.vector.tensor_copy(
                            by_range(weight[:, :, :])[:, :, bass.ds(i * 2 + b, 1), :].rearrange("p c a h -> p c (a h)"),
                            turn_s[b][:, :].rearrange("p (c h) -> p c h", c=RANGES)).then_inc(s_keep[b], 1)

        used = []
        with ExitStack() as part:
            total = sb("mix_total", [P, BLOCKS, C], F32, part)
            mass = sb("mix_mass", [P, BLOCKS, HEADS], F32, part)
            index = sb("v_index", [P, 2, U], I32, part)
            v_sb = sb("v_sb", [P, TURN, C], F32, part)
            scaled = sb("scaled", [P, 2, C], F32, part)
            away = sb("v_away", [P, 2, P], F32, part)
            hot = sb("v_hot", [P, 2, P], F32, part)
            mix = [ps(f"mix{b}", [P, C], F32, part) for b in range(2)]
            mass_ps = [ps(f"mass{b}", [P, HEADS], F32, part) for b in range(2)]
            s_passed, s_act, s_dve, s_index, s_norm, s_out = (sem(n, part) for n in ("v_passed", "v_act", "v_dve", "v_index", "v_norm", "v_out"))
            s_v = moved[:TURN]
            s_hot, s_tile, s_added = (
                [sem(f"{n}{b}", part) for b in range(2)] for n in ("v_hot", "v_tile", "v_added"))
            s_scaled = [[sem(f"v_scaled{h}{b}", part) for b in range(2)] for h in range(2)]
            block = open_block(nc, part, used)
            G2 = TURN // GROUP

            @block.gpsimd
            def _(eng):
                with eng.Fori(0, TURNS) as i:
                    for half in range(2):
                        for n in range(U):
                            eng.wait_ge(s_v[half * U + n], i * 16 + v_from)
                        eng.tensor_copy(index[:, half, :], rec[:, bass.ds(i * TURN + half * U, U), 0]
                                        ).then_inc(s_index, 1)
                        eng.wait_ge(s_index, i * 2 + half + 1)
                        for n in range(U):
                            u = half * U + n
                            for b in range(2):
                                eng.wait_ge(s_scaled[half][b], i * (U // 2))
                            eng.sem_inc(s_passed, 1)
                            eng.indirect_dma_start(v_sb[:, u, :], None, v,
                                                   bass.IndirectOffsetOnAxis(index[:, half, n:n + 1], 0)
                                                   ).then_inc(s_v[u], 16)

            @block.scalar
            def _(eng):
                with eng.Fori(0, TURNS) as i:
                    st = Steps(eng, s_act, i, TURN)
                    for u in range(TURN):
                        b = u % 2
                        at = low_neg[:, bass.ds(i * TURN + u, 1)]
                        st.link(nc.scalar.activation(away[:, b, :], iota_f[:, :], ACT.Abs, bias=at))
                        eng.wait_ge(s_tile[b], i * U + u // 2)
                        nc.scalar.activation(hot[:, b, :], away[:, b, :], ACT.Relu, bias=1.0, scale=-1.0
                                             ).then_inc(s_hot[b], 1)

            @block.vector
            def _(eng):
                st = Steps(eng, s_dve)
                st.link(nc.vector.memset(total[:, :, :], 0.0))
                st.link(nc.vector.memset(mass[:, :, :], 0.0))
                first = st.n
                with eng.Fori(0, TURNS) as i:
                    for half in range(2):
                        for n in range(U):
                            u = half * U + n
                            b = u % 2
                            eng.wait_ge(s_v[u], i * 16 + v_from + 16)
                            eng.wait_ge(s_tile[b], i * U + u // 2)
                            nc.vector.tensor_tensor(
                                scaled[:, b, :].rearrange("p (h d) -> p h d", d=D),
                                v_sb[:, u, :].rearrange("p (h d) -> p h d", d=D),
                                weight[:, bass.ds(i * TURN + u, 1), :].rearrange("p a h -> p (a h)").unsqueeze(2)
                                .broadcast_to([P, HEADS, D]), ALU.mult).then_inc(s_scaled[half][b], 1)
                            if u % GROUP == GROUP - 1:
                                g = u // GROUP
                                at = eng.value_load(groups[0:1, bass.ds(i * G2 + g, 1)], min_val=0, max_val=BLOCKS - 1)
                                m = g % 2
                                eng.wait_ge(s_tile[1], i * U + g + 1)
                                if g == 0:
                                    eng.wait_ge(s_added[1], i * G2)
                                else:
                                    eng.wait_ge(s_added[1 - m], i * G2 + 2 * ((g + 1) // 2))
                                t = total[:, bass.ds(at, 1), :].rearrange("p a c -> p (a c)")
                                nc.vector.tensor_tensor(t, mix[m][:, :], t, ALU.add).then_inc(s_added[m], 1)
                                t = mass[:, bass.ds(at, 1), :].rearrange("p a c -> p (a c)")
                                nc.vector.tensor_tensor(t, mass_ps[m][:, :], t, ALU.add).then_inc(s_added[m], 1)
                for m in range(2):
                    eng.wait_ge(s_added[m], TURNS * G2)
                st.link(nc.vector.tensor_scalar(mass[:, :, :], mass[:, :, :], 1e-30, None, ALU.max))
                st.link(nc.vector.reciprocal(mass[:, :, :], mass[:, :, :]))
                for n in range(4):
                    bl = slice(n * BLOCKS // 4, (n + 1) * BLOCKS // 4)
                    t = total[:, bl, :].rearrange("p b (h d) -> p (b h) d", d=D)
                    nc.vector.tensor_tensor(
                        t, t, mass[:, bl, :].rearrange("p b h -> p (b h)").unsqueeze(2)
                        .broadcast_to([P, BLOCKS // 4 * HEADS, D]), ALU.mult).then_inc(s_norm, 1)

            @block.tensor
            def _(eng):
                with eng.Fori(0, TURNS) as i:
                    for u in range(TURN):
                        b, g = u % 2, u // GROUP
                        m = g % 2
                        eng.wait_ge(s_hot[b], i * U + u // 2 + 1)
                        eng.wait_ge(s_scaled[u // U][b], i * (U // 2) + u % U // 2 + 1)
                        if u % GROUP == 0:
                            eng.wait_ge(s_added[m], i * G2 + 2 * (g // 2))
                        nc.tensor.matmul(mass_ps[m][:, :], hot[:, b, :],
                                         weight[:, bass.ds(i * TURN + u, 1), :].rearrange("p a h -> p (a h)"),
                                         start=(u % GROUP == 0), stop=(u % GROUP == GROUP - 1))
                        nc.tensor.matmul(mix[m][:, :], hot[:, b, :], scaled[:, b, :],
                                         start=(u % GROUP == 0), stop=(u % GROUP == GROUP - 1)).then_inc(s_tile[b], 1)

            @block.sync
            def _(eng):
                for n in range(4):
                    eng.wait_ge(s_norm, n + 1)
                    bl = slice(n * BLOCKS // 4, (n + 1) * BLOCKS // 4)
                    eng.dma_start(mixed.rearrange("(b p) c -> p b c", p=P)[:, bl, :], total[:, bl, :]).then_inc(s_out, 16)
                eng.wait_ge(s_out, 64)


def out_and_ffn(nc, mixed, z0, x, wo, bo, ln_g, ln_b, w1, b1, w2, b2, x3, z3):
    EPS = 1e-5
    KC = C // P
    M = 4
    TURNS = NODES // (M * P)
    HIDDEN = w1.shape[1]
    FC = HIDDEN // P
    with ExitStack() as ctx:
        def sb(name, shape, dt=F32):
            return ctx.enter_context(nc.sbuf_tensor("f_" + name, shape, dt))

        def ps(name, shape, dt=F32):
            return ctx.enter_context(nc.psum_tensor("f_" + name, shape, dt))

        used = []

        def sem(name):
            used.append(ctx.enter_context(nc.semaphore("fs_" + name)))
            return used[-1]

        def sems(n, *names):
            return [[sem(f"{name}{i}") for i in range(n)] for name in names]

        wo_sb, w1_sb, w2_sb = sb("wo", [P, KC, C]), sb("w1", [P, KC, HIDDEN]), sb("w2", [P, FC, C])
        bo_sb, b2_sb, gain, shift = sb("bo", [P, C]), sb("b2", [P, C]), sb("gain", [P, C]), sb("shift", [P, C])
        b1_sb = sb("b1", [P, FC])
        ones, ident, eps = sb("ones", [P, P]), sb("ident", [P, P]), sb("eps", [P, 1])
        mixt, z0t, xt = sb("mix", [P, M, C]), sb("z0", [P, M, C]), sb("x", [P, M, C])
        mixT = sb("mixT", [P, 2, C])
        x1 = sb("x1", [P, M, C])
        zn = sb("zn", [P, C])
        z = sb("z", [P, M, C])
        zT = sb("zT", [P, 2, KC, M * P])
        base = sb("base", [P, 2, M, C])
        hT = sb("hT", [P, FC, M * P])
        x3t, z3t = sb("x3", [P, M, C]), sb("z3", [P, M, C])
        stats, mean_var, root = sb("stats", [P, 2, 6]), sb("mv", [P, 2, 2]), sb("root", [P, 2])
        turned = [ps(f"turned{b}", [P, C]) for b in range(2)]
        o_ps = [ps(f"o{b}", [P, C]) for b in range(2)]
        up_ps = [ps(f"up{b}", [P, M * P]) for b in range(2)]
        down_ps = [ps(f"down{b}", [P, C]) for b in range(2)]

        s_w, s_b, s_c, s_cut, s_a, s_e, s_passed = (sem(n) for n in ("w", "b", "c", "cut", "a", "e", "passed"))
        s_var_a, s_root_a, s_var_e, s_root_e = (sem(n) for n in ("var_a", "root_a", "var_e", "root_e"))
        (s_mix, s_z0, s_x, s_res, s_mixturn, s_mixT, s_o, s_x1, s_z, s_zturn, s_zT, s_part, s_base, s_down, s_x3, s_z3,
         s_put_x3, s_put_z3) = sems(M, "mix", "z0", "x", "res", "mixturn", "mixT", "o", "x1", "z", "zturn", "zT", "part",
                                    "base", "down", "x3", "z3", "put_x3", "put_z3")
        s_up, s_h = sems(FC, "up", "h")
        block = open_block(nc, ctx, used)

        def rows(a, t, m):
            n = t * M + m
            v = a.rearrange("(n p) c -> n p c", p=P)
            return v[n, :, :] if isinstance(n, int) else v[bass.ds(n, 1), :, :].rearrange("a p c -> (a p) c")

        def turns(eng, begin, body, end):
            begin()
            with eng.Fori(0, (TURNS - 2) // 2) as j:
                for c in range(2):
                    body(j * 2 + c, c)
            body(TURNS - 2, 0)
            end(TURNS - 1, 1)

        @block.sync
        def _(eng):
            def load(t, m):
                eng.wait_ge(s_mixturn[m], t)
                eng.dma_start(mixt[:, m, :], rows(mixed, t, m)).then_inc(s_mix[m], 16)
                eng.wait_ge(s_x1[m], t)
                eng.dma_start(z0t[:, m, :], rows(z0, t, m)).then_inc(s_z0[m], 16)
                eng.wait_ge(s_part[m], t)
                eng.dma_start(xt[:, m, :], rows(x, t, m)).then_inc(s_x[m], 16)

            def store(t, m):
                eng.wait_ge(s_x3[m], t + 1)
                eng.dma_start(rows(x3, t, m), x3t[:, m, :]).then_inc(s_put_x3[m], 16)
                eng.wait_ge(s_z3[m], t + 1)
                eng.dma_start(rows(z3, t, m), z3t[:, m, :]).then_inc(s_put_z3[m], 16)

            def begin():
                for m in range(M):
                    load(0, m)
                eng.dma_start(wo_sb[:, :, :], wo.rearrange("(k p) n -> p k n", p=P)).then_inc(s_w, 16)
                for dst, a in ((bo_sb, bo), (b2_sb, b2), (gain, ln_g), (shift, ln_b)):
                    eng.dma_start(dst[:, :], a.partition_broadcast(P)).then_inc(s_b, 16)
                eng.dma_start(b1_sb[:, :], b1).then_inc(s_b, 16)
                eng.dma_start(w1_sb[:, :, :], w1.rearrange("(k p) n -> p k n", p=P)).then_inc(s_w, 16)
                eng.dma_start(w2_sb[:, :, :], w2.rearrange("(k p) n -> p k n", p=P)).then_inc(s_w, 16)
                for m in range(M):
                    load(1, m)

            def body(t, c):
                if not (isinstance(t, int) and t == TURNS - 2):
                    for m in range(M):
                        load(t + 2, m)
                for m in range(M):
                    store(t, m)

            def end(t, c):
                for m in range(M):
                    store(t, m)

            turns(eng, begin, body, end)
            for m in range(M):
                eng.wait_ge(s_put_x3[m], 16 * TURNS)
                eng.wait_ge(s_put_z3[m], 16 * TURNS)

        @block.gpsimd
        def _(eng):
            eng.memset(ones[:, :], 1.0).then_inc(s_c, 1)
            eng.memset(eps[:, :], EPS).then_inc(s_c, 1)
            eng.wait_ge(s_c, 2)
            eng.affine_select(out=ident[:, :], in_=ones[:, :], compare_op=ALU.is_equal, fill=0.0, base=0,
                              pattern=[[1, P]], channel_multiplier=-1).then_inc(s_cut, 1)
            eng.wait_ge(s_b, 80)

            def sums(t, c):
                for m in range(M):
                    eng.wait_ge(s_z0[m], t * 16 + 16)
                    eng.tensor_tensor(z0t[:, m, :], z0t[:, m, :], bo_sb[:, :], ALU.add).then_inc(s_res[m], 1)
                for m in range(M):
                    eng.wait_ge(s_x1[m], t + 1)
                    eng.wait_ge(s_x[m], t * 16 + 16)
                    eng.tensor_tensor(base[:, c, m, :], x1[:, m, :], xt[:, m, :], ALU.add).then_inc(s_part[m], 1)
                    eng.wait_ge(s_part[m], t + 1)
                    eng.tensor_tensor(base[:, c, m, :], base[:, c, m, :], b2_sb[:, :], ALU.add).then_inc(s_base[m], 1)

            turns(eng, lambda: sums(0, 0), lambda t, c: sums(t + 1, 1 - c), lambda t, c: None)

        @block.vector
        def _(eng):
            eng.wait_ge(s_b, 80)

            def attended(t, c):
                st = Steps(eng, s_a, t, 4 * M)
                for m in range(M):
                    eng.wait_ge(s_o[m], t + 1)
                    eng.wait_ge(s_res[m], t + 1)
                    eng.wait_ge(s_base[m], t)
                    nc.vector.tensor_tensor(x1[:, m, :], o_ps[m % 2][:, :], z0t[:, m, :], ALU.add).then_inc(s_x1[m], 1)
                    eng.wait_ge(s_x1[m], t + 1)
                    st.link(norm_scale(nc, eng, st, s_passed, s_var_a, s_root_a, t * M + m + 1, x1[:, m, :], stats[:, 0, :],
                                       mean_var[:, 0, :], root[:, 0:1], zn[:, :]))
                    st.link(nc.vector.tensor_tensor(zn[:, :], zn[:, :], gain[:, :], ALU.mult))
                    eng.wait_ge(s_zturn[m], t)
                    nc.vector.tensor_tensor(z[:, m, :], zn[:, :], shift[:, :], ALU.add).then_inc(s_z[m], 1)
                assert st.n == 4 * M

            def ended(t, c):
                st = Steps(eng, s_e, t, 2 * M)
                for m in range(M):
                    eng.wait_ge(s_down[m], t + 1)
                    eng.wait_ge(s_base[m], t + 1)
                    eng.wait_ge(s_put_x3[m], t * 16)
                    nc.vector.tensor_tensor(x3t[:, m, :], down_ps[m % 2][:, :], base[:, c, m, :], ALU.add).then_inc(s_x3[m], 1)
                    eng.wait_ge(s_x3[m], t + 1)
                    eng.wait_ge(s_put_z3[m], t * 16)
                    norm_scale(nc, eng, st, s_passed, s_var_e, s_root_e, t * M + m + 1, x3t[:, m, :], stats[:, 1, :],
                               mean_var[:, 1, :], root[:, 1:2], z3t[:, m, :]).then_inc(s_z3[m], 1)
                assert st.n == 2 * M

            turns(eng, lambda: attended(0, 0),
                  lambda t, c: (attended(t + 1, 1 - c), ended(t, c)), ended)

        @block.scalar
        def _(eng):
            eng.wait_ge(s_c, 2)
            eng.wait_ge(s_b, 80)

            def attended(t):
                def keep(m):
                    eng.wait_ge(s_mixturn[m], t + 1)
                    eng.wait_ge(s_o[(m + 2) % M], t + (m >= 2))
                    nc.scalar.copy(mixT[:, m % 2, :], turned[m % 2][:, :]).then_inc(s_mixT[m], 1)

                def root_of(m):
                    eng.wait_ge(s_var_a, t * M + m + 1)
                    nc.scalar.activation(root[:, 0:1], mean_var[:, 0, 1:2], ACT.Sqrt, bias=eps[:, :]).then_inc(s_root_a, 1)

                keep(0)
                for m in range(1, M):
                    keep(m)
                    root_of(m - 1)
                root_of(M - 1)

            def hidden(t):
                for f in range(FC):
                    eng.wait_ge(s_up[f], t + 1)
                    nc.scalar.activation(hT[:, f, :], up_ps[f % 2][:, :], ACT.Silu, bias=b1_sb[:, f:f + 1]).then_inc(s_h[f], 1)

            def columns(t, c):
                for m in range(M):
                    eng.wait_ge(s_zturn[m], t + 1)
                    nc.scalar.copy(zT[:, c, :, m * P:(m + 1) * P],
                                   turned[m % 2][:, :].rearrange("p (k r) -> p k r", r=P)).then_inc(s_zT[m], 1)

            def ended(t):
                for m in range(M):
                    eng.wait_ge(s_var_e, t * M + m + 1)
                    nc.scalar.activation(root[:, 1:2], mean_var[:, 1, 1:2], ACT.Sqrt, bias=eps[:, :]).then_inc(s_root_e, 1)

            turns(eng, lambda: (attended(0), columns(0, 0)),
                  lambda t, c: (attended(t + 1), hidden(t), columns(t + 1, 1 - c), ended(t)),
                  lambda t, c: (hidden(t), ended(t)))

        @block.tensor
        def _(eng):
            eng.wait_ge(s_cut, 1)

            def attended(t):
                def turn(m):
                    eng.wait_ge(s_mix[m], t * 16 + 16)
                    if m >= 2:
                        eng.wait_ge(s_mixT[m - 2], t + 1)
                    else:
                        eng.wait_ge(s_zT[m + 2], t)
                    for kc in range(KC):
                        last = nc.tensor.transpose(turned[m % 2][:, kc * P:(kc + 1) * P], mixt[:, m, kc * P:(kc + 1) * P],
                                                   ident[:, :])
                    last.then_inc(s_mixturn[m], 1)

                def product(m):
                    eng.wait_ge(s_mixT[m], t + 1)
                    eng.wait_ge(s_x1[(m + 2) % M], t + (m >= 2))
                    for kc in range(KC):
                        last = nc.tensor.matmul(o_ps[m % 2][:, :], mixT[:, m % 2, kc * P:(kc + 1) * P], wo_sb[:, kc, :],
                                                start=(kc == 0), stop=(kc == KC - 1))
                    last.then_inc(s_o[m], 1)

                turn(0)
                for m in range(1, M):
                    turn(m)
                    product(m - 1)
                product(M - 1)

            def up(t, c):
                for m in range(M):
                    eng.wait_ge(s_zT[m], t + 1)
                for f in range(FC):
                    eng.wait_ge(s_h[(f - 2) % FC], t + (f >= 2))
                    for kc in range(KC):
                        last = nc.tensor.matmul(up_ps[f % 2][:, :], w1_sb[:, kc, f * P:(f + 1) * P], zT[:, c, kc, :],
                                                start=(kc == 0), stop=(kc == KC - 1))
                    last.then_inc(s_up[f], 1)

            def turn_z(t):
                for m in range(M):
                    eng.wait_ge(s_z[m], t + 1)
                    if m >= 2:
                        eng.wait_ge(s_zT[m - 2], t + 1)
                    else:
                        eng.wait_ge(s_mixT[m + 2], t + 1)
                    for kc in range(KC):
                        last = nc.tensor.transpose(turned[m % 2][:, kc * P:(kc + 1) * P], z[:, m, kc * P:(kc + 1) * P],
                                                   ident[:, :])
                    last.then_inc(s_zturn[m], 1)

            def down(t):
                for f in range(FC):
                    eng.wait_ge(s_h[f], t + 1)
                for m in range(M):
                    eng.wait_ge(s_x3[(m + 2) % M], t + (m >= 2))
                    for f in range(FC):
                        last = nc.tensor.matmul(down_ps[m % 2][:, :], hT[:, f, m * P:(m + 1) * P], w2_sb[:, f, :],
                                                start=(f == 0), stop=(f == FC - 1))
                    last.then_inc(s_down[m], 1)

            def begin():
                eng.wait_ge(s_w, 48)
                attended(0)
                turn_z(0)

            turns(eng, begin, lambda t, c: (attended(t + 1), up(t, c), turn_z(t + 1), down(t)),
                  lambda t, c: (up(t, c), down(t)))


def experts(nc, x3, z3, router, w1, b1, w2, b2, gamma, beta, out):
    EPS = 1e-6
    KC = C // P
    M = 4
    TURNS = NODES // (M * P)
    E, _, F = w1.shape
    FC = F // P
    with ExitStack() as ctx:
        def sb(name, shape, dt=F32):
            return ctx.enter_context(nc.sbuf_tensor("m_" + name, shape, dt))

        def ps(name, shape, dt=F32):
            return ctx.enter_context(nc.psum_tensor("m_" + name, shape, dt))

        used = []

        def sem(name):
            used.append(ctx.enter_context(nc.semaphore("ms_" + name)))
            return used[-1]

        def sems(n, *names):
            return [[sem(f"{name}_{i}") for i in range(n)] for name in names]

        w1_sb, w2_sb = sb("w1", [P, E, KC, F]), sb("w2", [P, E, FC, C])
        gamma_sb, b2_sb = sb("gamma", [P, E, C]), sb("b2", [P, E, C])
        b1_sb, beta_sb, router_sb = sb("b1", [P, E, FC]), sb("beta", [E, C]), sb("router", [P, KC, E])
        ones, ident, eps, iota_e = sb("ones", [P, P]), sb("ident", [P, P]), sb("eps", [P, 1]), sb("iota_e", [P, E])
        z3t = sb("z3", [P, 2, M, C])
        acc = sb("acc", [P, 2, M, C])
        zT = sb("zT", [P, 2, KC, M * P])
        hT = sb("hT", [P, 2, FC, M * P])
        res = sb("res", [P, M, C])
        y = sb("y", [P, 2, M, C])
        logits = sb("logits", [P, M, E])
        top = sb("top", [P, M, 8])
        top_i = sb("top_i", [P, M, 8], mybir.dt.uint32)
        top_f = sb("top_f", [P, M, 2])
        below, ratio, g1, g2 = (sb(n, [P, M]) for n in ("below", "ratio", "g1", "g2"))
        pick = sb("pick", [P, 2, M, E])
        gate = sb("gate", [P, 2, M, E])
        gateT = sb("gateT", [E, M * P])
        stats, mean_var = sb("stats", [P, M, 6]), sb("mv", [P, M, 2])
        root = sb("root", [P, M])
        slope, offset = sb("slope", [P, 2, M]), sb("offset", [P, 2, M])
        turned = [ps(f"turned{b}", [P, C]) for b in range(2)]
        up_ps = [ps(f"up{b}", [P, M * P]) for b in range(2)]
        down_ps = [ps(f"down{b}", [P, C]) for b in range(2)]
        route_ps = ps("route", [P, M * E])

        s_w, s_c, s_cut, s_r, s_e, s_passed = (sem(n) for n in ("w", "c", "cut", "r", "e", "passed"))
        s_logits, s_low, s_ratio, s_gate, s_gateturn, s_gateT, s_var, s_root, s_line = (
            sem(n) for n in ("logits", "low", "ratio", "gate", "gateturn", "gateT", "var", "root", "line"))
        s_z, s_x, s_put = ([[sem(f"{n}{b}_{m}") for m in range(M)] for b in range(2)] for n in ("z", "x", "put"))
        s_turn, s_zT, s_beta, s_acc = sems(M, "turn", "zT", "beta", "acc")
        s_res, s_down, s_y, s_norm, s_gain, s_add = sems(M, "res", "down", "y", "norm", "gain", "add")
        s_up, s_h = sems(FC, "up", "h")
        block = open_block(nc, ctx, used)

        def rows(a, t, m):
            n = t * M + m
            v = a.rearrange("(n p) c -> n p c", p=P)
            return v[n, :, :] if isinstance(n, int) else v[bass.ds(n, 1), :, :].rearrange("a p c -> (a p) c")

        def turns(eng, begin, body):
            begin()
            with eng.Fori(0, TURNS // 2 - 1) as j:
                for c in range(2):
                    body(j * 2 + c, c, j, True)
            body(TURNS - 2, 0, TURNS // 2 - 1, True)
            body(TURNS - 1, 1, TURNS // 2 - 1, False)

        @block.sync
        def _(eng):
            def load(t, b, k):
                for m in range(M):
                    eng.wait_ge(s_put[b][m], k * 16)
                    eng.dma_start(z3t[:, b, m, :], rows(z3, t, m)).then_inc(s_z[b][m], 16)
                    eng.dma_start(acc[:, b, m, :], rows(x3, t, m)).then_inc(s_x[b][m], 16)

            def begin():
                load(0, 0, 0)
                eng.dma_start(router_sb[:, :, :], router.rearrange("(k p) e -> p k e", p=P)).then_inc(s_c, 16)
                eng.dma_start(beta_sb[:, :], beta).then_inc(s_c, 16)
                eng.dma_start(b1_sb[:, :, :], b1).then_inc(s_c, 16)
                eng.dma_start(w1_sb[:, :, :, :], w1.rearrange("e (k p) f -> p e k f", p=P)).then_inc(s_w, 16)
                eng.dma_start(b2_sb[:, :, :].rearrange("p e c -> p (e c)"),
                              b2.rearrange("e c -> (e c)").partition_broadcast(P)).then_inc(s_w, 16)
                eng.dma_start(w2_sb[:, :, :, :], w2.rearrange("e (k p) c -> p e k c", p=P)).then_inc(s_w, 16)
                eng.dma_start(gamma_sb[:, :, :].rearrange("p e c -> p (e c)"),
                              gamma.rearrange("e c -> (e c)").partition_broadcast(P)).then_inc(s_w, 16)

            def body(t, b, k, more):
                if more:
                    load(t + 1, 1 - b, k + b)
                for m in range(M):
                    eng.wait_ge(s_acc[m], t + 1)
                    eng.dma_start(rows(out, t, m), acc[:, b, m, :]).then_inc(s_put[b][m], 16)

            turns(eng, begin, body)
            for b in range(2):
                for m in range(M):
                    eng.wait_ge(s_put[b][m], 16 * (TURNS // 2))

        @block.gpsimd
        def _(eng):
            eng.memset(ones[:, :], 1.0).then_inc(s_cut, 1)
            eng.memset(eps[:, :], EPS).then_inc(s_cut, 1)
            eng.iota(iota_e[:, :], pattern=[[1, E]], base=0, channel_multiplier=0,
                     allow_small_or_imprecise_dtypes=True).then_inc(s_cut, 1)
            eng.wait_ge(s_cut, 3)
            eng.affine_select(out=ident[:, :], in_=ones[:, :], compare_op=ALU.is_equal, fill=0.0, base=0,
                              pattern=[[1, P]], channel_multiplier=-1).then_inc(s_cut, 1)
            eng.wait_ge(s_w, 64)

            def body(t, b, k, more):
                def residual(e):
                    n = t * E + e
                    for m in range(M):
                        if e == 0:
                            eng.wait_ge(s_z[b][m], k * 16 + 16)
                        eng.wait_ge(s_y[m], n)
                        eng.tensor_tensor(res[:, m, :], z3t[:, b, m, :], b2_sb[:, e, :], ALU.add).then_inc(s_res[m], 1)

                def gain(e):
                    n = t * E + e
                    for m in range(M):
                        eng.wait_ge(s_norm[m], n + 1)
                        eng.tensor_tensor(y[:, e % 2, m, :], y[:, e % 2, m, :], gamma_sb[:, e, :], ALU.mult
                                          ).then_inc(s_gain[m], 1)

                residual(0)
                for e in range(1, E):
                    residual(e)
                    gain(e - 1)
                gain(E - 1)

            turns(eng, lambda: None, body)

        @block.vector
        def _(eng):
            def route(t, b, k):
                st = Steps(eng, s_r, t, 2 * M + 9)
                eng.wait_ge(s_logits, t + 1)
                st.link(nc.vector.tensor_copy(logits[:, :, :], route_ps[:, :].rearrange("p (m e) -> p m e", e=E)))
                for m in range(M):
                    eng.sem_inc(s_passed, 1)
                    st.link(nc.vector.max(top[:, m, :], logits[:, m, :]))
                    eng.sem_inc(s_passed, 1)
                    st.link(nc.vector.max_index(top_i[:, m, :], top[:, m, :], logits[:, m, :]))
                st.link(nc.vector.tensor_copy(top_f[:, :, :], top_i[:, :, 0:2]))
                nc.vector.tensor_tensor(below[:, :], top[:, :, 1], top[:, :, 0], ALU.subtract).then_inc(s_low, 1)
                eng.wait_ge(s_ratio, t + 1)
                st.link(nc.vector.tensor_scalar(g1[:, :], ratio[:, :], 1.0, None, ALU.add))
                st.link(nc.vector.reciprocal(g1[:, :], g1[:, :]))
                st.link(nc.vector.tensor_tensor(g2[:, :], g1[:, :], ratio[:, :], ALU.mult))
                for n, g in ((0, g1), (1, g2)):
                    st.link(nc.vector.tensor_tensor(pick[:, n, :, :], iota_e[:, :].unsqueeze(1).broadcast_to([P, M, E]),
                                                    top_f[:, :, n:n + 1].broadcast_to([P, M, E]), ALU.is_equal))
                    st.link(nc.vector.tensor_tensor(pick[:, n, :, :], pick[:, n, :, :],
                                                    g[:, :].unsqueeze(2).broadcast_to([P, M, E]), ALU.mult))
                nc.vector.tensor_tensor(gate[:, b, :, :], pick[:, 0, :, :], pick[:, 1, :, :], ALU.add).then_inc(s_gate, 1)
                assert st.n == 2 * M + 9

            def start_sum(t, b, k):
                for m in range(M):
                    eng.wait_ge(s_beta[m], t + 1)
                    eng.wait_ge(s_x[b][m], k * 16 + 16)
                    nc.vector.tensor_tensor(acc[:, b, m, :], down_ps[m % 2][:, :], acc[:, b, m, :], ALU.add
                                            ).then_inc(s_add[m], 1)

            def body(t, b, k, more):
                def norm(e):
                    st = Steps(eng, s_e, t * E + e, M + 2)
                    n = t * E + e
                    for m in range(M):
                        eng.wait_ge(s_down[m], n + 1)
                        eng.wait_ge(s_res[m], n + 1)
                        if e == 1:
                            eng.wait_ge(s_acc[m], t)
                        else:
                            eng.wait_ge(s_add[m], n)
                        nc.vector.tensor_tensor(y[:, e % 2, m, :], down_ps[m % 2][:, :], res[:, m, :], ALU.add
                                                ).then_inc(s_y[m], 1)
                        eng.wait_ge(s_y[m], n + 1)
                        st.link(nc.vector.bn_stats(stats[:, m, :], y[:, e % 2, m, :]))
                        eng.sem_inc(s_passed, 1)
                        last = nc.vector.bn_aggr(mean_var[:, m, :], stats[:, m, :])
                    last.then_inc(s_var, 1)
                    eng.wait_ge(s_root, n + 1)
                    st.link(nc.vector.reciprocal(root[:, :], root[:, :]))
                    st.link(nc.vector.tensor_tensor(slope[:, e % 2, :], root[:, :], gate[:, b, :, e], ALU.mult))
                    nc.vector.scalar_tensor_tensor(offset[:, e % 2, :], mean_var[:, :, 0], -1.0, slope[:, e % 2, :],
                                                   ALU.mult, ALU.mult).then_inc(s_line, 1)
                    assert st.n == M + 2

                def add(e):
                    n = t * E + e
                    for m in range(M):
                        eng.wait_ge(s_gain[m], n + 1)
                        eng.wait_ge(s_add[m], t * E + e + 1)
                        last = nc.vector.tensor_tensor(acc[:, b, m, :], acc[:, b, m, :], y[:, e % 2, m, :], ALU.add)
                        last.then_inc(s_add[m], 1) if e < E - 1 else last.then_inc(s_acc[m], 1)

                norm(0)
                for e in range(1, E):
                    norm(e)
                    add(e - 1)
                    if e == E // 2 and more:
                        route(t + 1, 1 - b, k + b)
                add(E - 1)
                if more:
                    start_sum(t + 1, 1 - b, k + b)

            eng.wait_ge(s_cut, 3)
            turns(eng, lambda: (route(0, 0, 0), start_sum(0, 0, 0)), body)

        @block.scalar
        def _(eng):
            eng.wait_ge(s_cut, 3)
            eng.wait_ge(s_c, 48)

            def columns(t, b):
                for m in range(M):
                    eng.wait_ge(s_turn[m], t + 1)
                    nc.scalar.copy(zT[:, b, :, m * P:(m + 1) * P],
                                   turned[m % 2][:, :].rearrange("p (k r) -> p k r", r=P)).then_inc(s_zT[m], 1)

            def second_gate(t):
                eng.wait_ge(s_low, t + 1)
                nc.scalar.activation(ratio[:, :], below[:, :], ACT.Exp).then_inc(s_ratio, 1)

            def gate_columns(t):
                eng.wait_ge(s_gateturn, t + 1)
                nc.scalar.copy(gateT[:, :], turned[0][0:E, :]).then_inc(s_gateT, 1)

            def body(t, b, k, more):
                def hidden(e):
                    n = t * E + e
                    for f in range(FC):
                        eng.wait_ge(s_up[f], n + 1)
                        nc.scalar.activation(hT[:, e % 2, f, :], up_ps[f][:, :], ACT.Relu, bias=b1_sb[:, e, f:f + 1]
                                             ).then_inc(s_h[f], 1)

                def norm(e):
                    n = t * E + e
                    eng.wait_ge(s_var, n + 1)
                    nc.scalar.activation(root[:, :], mean_var[:, :, 1], ACT.Sqrt, bias=eps[:, :]).then_inc(s_root, 1)
                    eng.wait_ge(s_line, n + 1)
                    for m in range(M):
                        nc.scalar.activation(y[:, e % 2, m, :], y[:, e % 2, m, :], ACT.Identity,
                                             bias=offset[:, e % 2, m:m + 1], scale=slope[:, e % 2, m:m + 1]
                                             ).then_inc(s_norm[m], 1)

                hidden(0)
                for e in range(1, E):
                    hidden(e)
                    norm(e - 1)
                    if e == E // 2 and more:
                        columns(t + 1, 1 - b)
                    if e == E // 2 + 1 and more:
                        second_gate(t + 1)
                    if e == E // 2 + 2 and more:
                        gate_columns(t + 1)
                norm(E - 1)

            turns(eng, lambda: (columns(0, 0), second_gate(0), gate_columns(0)), body)

        @block.tensor
        def _(eng):
            eng.wait_ge(s_cut, 4)
            eng.wait_ge(s_c, 48)

            def route(t, b, k):
                for m in range(M):
                    eng.wait_ge(s_z[b][m], k * 16 + 16)
                    if m >= 2:
                        eng.wait_ge(s_zT[m - 2], t + 1)
                    else:
                        eng.wait_ge(s_zT[m + 2], t)
                    if m == 0:
                        eng.wait_ge(s_gateT, t)
                    for kc in range(KC):
                        last = nc.tensor.transpose(turned[m % 2][:, kc * P:(kc + 1) * P],
                                                   z3t[:, b, m, kc * P:(kc + 1) * P], ident[:, :])
                    last.then_inc(s_turn[m], 1)
                for m in range(M):
                    eng.wait_ge(s_zT[m], t + 1)
                    for kc in range(KC):
                        last = nc.tensor.matmul(route_ps[:, m * E:(m + 1) * E], zT[:, b, kc, m * P:(m + 1) * P],
                                                router_sb[:, kc, :], start=(kc == 0), stop=(kc == KC - 1))
                last.then_inc(s_logits, 1)

            def turn_gates(t, b):
                eng.wait_ge(s_gate, t + 1)
                for m in range(M):
                    last = nc.tensor.transpose(turned[0][0:E, m * P:(m + 1) * P], gate[:, b, m, :], ident[:, :])
                last.then_inc(s_gateturn, 1)

            def start_sum(t):
                eng.wait_ge(s_gateT, t + 1)
                for m in range(M):
                    if m >= 2:
                        eng.wait_ge(s_add[m - 2], t * E + 1)
                    else:
                        eng.wait_ge(s_y[m + 2], t * E)
                    nc.tensor.matmul(down_ps[m % 2][:, :], gateT[:, m * P:(m + 1) * P], beta_sb[:, :],
                                     start=True, stop=True).then_inc(s_beta[m], 1)

            def body(t, b, k, more):
                def up(e):
                    n = t * E + e
                    for f in range(FC):
                        eng.wait_ge(s_h[f], n)
                        for kc in range(KC):
                            last = nc.tensor.matmul(up_ps[f][:, :], w1_sb[:, e, kc, f * P:(f + 1) * P], zT[:, b, kc, :],
                                                    start=(kc == 0), stop=(kc == KC - 1))
                        last.then_inc(s_up[f], 1)

                def down(e):
                    n = t * E + e
                    for f in range(FC):
                        eng.wait_ge(s_h[f], n + 1)
                    for m in range(M):
                        if m >= 2:
                            eng.wait_ge(s_y[m - 2], n + 1)
                        elif e == 0:
                            eng.wait_ge(s_add[m + 2], n + 1)
                        else:
                            eng.wait_ge(s_y[m + 2], n)
                        for f in range(FC):
                            last = nc.tensor.matmul(down_ps[m % 2][:, :], hT[:, e % 2, f, m * P:(m + 1) * P],
                                                    w2_sb[:, e, f, :], start=(f == 0), stop=(f == FC - 1))
                        last.then_inc(s_down[m], 1)

                up(0)
                for e in range(1, E):
                    up(e)
                    down(e - 1)
                    if e == E // 2 and more:
                        route(t + 1, 1 - b, k + b)
                    if e == E // 2 + 2 and more:
                        turn_gates(t + 1, 1 - b)
                down(E - 1)
                if more:
                    start_sum(t + 1)

            def begin():
                route(0, 0, 0)
                turn_gates(0, 0)
                start_sum(0)
                eng.wait_ge(s_w, 64)

            turns(eng, begin, body)


def graph_layer(nc, a, out):

    def scratch(name, shape, dt=F32):
        return nc.dram_tensor(name, shape, dt, kind="Internal").ap()

    with ExitStack() as ctx:
        moved = [ctx.enter_context(nc.semaphore(f"moved{n}")) for n in range(MOVES)]
        stages(nc, a, out, moved, scratch)


def stages(nc, a, out, moved, scratch):
    records = scratch("records", (P * TILES, REC))
    group_block = scratch("group_block", (-(-GROUPS // P) * P,), I32)
    z0, q, k, v, mixed, x3, z3 = (scratch(f"t_{n}", (NODES, C)) for n in ("z0", "q", "k", "v", "mixed", "x3", "z3"))
    project_qkv(nc, a["x"], a["L0_gnn_ln1_g"], a["L0_gnn_ln1_b"], a["L0_gnn_Wq"], a["L0_gnn_bq"], a["L0_gnn_Wk"],
                a["L0_gnn_bk"], a["L0_gnn_Wv"], a["L0_gnn_bv"], z0, q, k, v)
    sort_edges(nc, moved, a["src_t"], a["src"], a["dst_t"], a["bias_t"], records, group_block)
    attention(nc, moved, 16 * (EDGES // P) // MOVES, records, group_block, q, k, v, mixed)
    out_and_ffn(nc, mixed, z0, a["x"], a["L0_gnn_Wo"], a["L0_gnn_bo"], a["L0_gnn_ln2_g"], a["L0_gnn_ln2_b"],
                a["L0_gnn_W1"], a["b1_t"], a["L0_gnn_W2"], a["L0_gnn_b2"], x3, z3)
    experts(nc, x3, z3, a["L0_ffn_router_w"], a["L0_ffn_w1"], a["moe_b1_t"], a["L0_ffn_w2"], a["L0_ffn_b2"],
            a["L0_ffn_gamma"], a["L0_ffn_beta"], out)


_PLAIN = ["x", "src", "L0_gnn_Wq", "L0_gnn_bq", "L0_gnn_Wk", "L0_gnn_bk", "L0_gnn_Wv", "L0_gnn_bv", "L0_gnn_Wo",
          "L0_gnn_bo", "L0_gnn_ln1_g", "L0_gnn_ln1_b", "L0_gnn_ln2_g", "L0_gnn_ln2_b", "L0_gnn_W1", "L0_gnn_W2",
          "L0_gnn_b2", "L0_ffn_router_w", "L0_ffn_w1", "L0_ffn_w2", "L0_ffn_b2", "L0_ffn_gamma", "L0_ffn_beta"]


def kernel(**inputs):
    import numpy as _np
    import concourse.bacc as _bacc
    from concourse import mybir as _mybir
    from concourse.bass_utils import run_bass_kernel_spmd as _run

    given = {name: _np.asarray(inputs[name]) for name in inputs}
    laid = {name: given[name] for name in _PLAIN}
    laid["src_t"] = given["src"].reshape(IN_TILES, P).T
    laid["dst_t"] = given["dst"].reshape(IN_TILES, P).T
    laid["bias_t"] = given["edge_attr_8"].reshape(IN_TILES, P, HEADS).transpose(1, 0, 2).reshape(P, IN_TILES * HEADS)
    laid["b1_t"] = given["L0_gnn_b1"].reshape(-1, P).T
    laid["moe_b1_t"] = given["L0_ffn_b1"].reshape(given["L0_ffn_b1"].shape[0], -1, P).transpose(2, 0, 1)

    nc = _bacc.Bacc("TRN2", target_bir_lowering=False, num_devices=1)
    arrays, args = {}, {}
    for name, a in laid.items():
        arrays[f"in_{name}"] = _np.ascontiguousarray(a)
        args[name] = nc.dram_tensor(f"in_{name}", a.shape, _mybir.dt.from_np(a.dtype), kind="ExternalInput").ap()
    out = nc.dram_tensor("out", (NODES, C), F32, kind="ExternalOutput").ap()
    graph_layer(nc, args, out)
    r = _run(nc, [arrays], core_ids=[0])
    return r.results[0]["out"]
```

```python
import concourse.bass as bass
import concourse.mybir as mybir
from contextlib import ExitStack

F32, BF16, I32 = mybir.dt.float32, mybir.dt.bfloat16, mybir.dt.int32
ALU = mybir.AluOpType
ACT = mybir.ActivationFunctionType
AX = mybir.AxisListType

P = 128
NODES, C, HEADS = 4096, 512, 8
D = C // HEADS
EDGES = 69632
BLOCKS = NODES // P
IN_TILES = EDGES // P
GROUP = 2
SPAN = GROUP * P
GROUPS = -(-EDGES // SPAN) + BLOCKS
TILES = GROUPS * GROUP
RANGES = 16
RANGE_TILES = TILES // RANGES
REC = 2 + HEADS
PAD_ROW = -1.0


class Steps:

    def __init__(self, eng, sem, turn=None, per=0, base=0):
        self.eng, self.sem, self.turn, self.per, self.base, self.n = eng, sem, turn, per, base, 0

    def value(self):
        n = self.base + self.n
        return n if self.turn is None else self.turn * self.per + n

    def link(self, ins):
        self.n += 1
        ins.then_inc(self.sem, 1)
        self.eng.wait_ge(self.sem, self.value())


class Ring:

    def __init__(self, sems, tiles):
        self.sems, self.n, self.per = sems, len(sems), tiles // len(sems)

    def start(self, eng):
        for s in self.sems:
            eng.sem_inc(s, self.per)

    def sem(self, u):
        return self.sems[u % self.n]

    def value(self, i, u):
        return i * self.per + (self.per + u // self.n + 1)

    def wait(self, eng, i, u):
        eng.wait_ge(self.sem(u), self.value(i, u))


MOVES = 32


def open_block(nc, ctx, used):
    def clear():
        for s in used:
            nc.gpsimd.sem_clear(s)
        nc.all_engine_barrier()

    ctx.callback(clear)
    return ctx.enter_context(nc.Block())


def sort_edges(nc, moved, src_t, src_row, dst_t, bias_t, records, group_block):
    B = 16
    BATCHES = IN_TILES // B
    GC = -(-GROUPS // P)
    with ExitStack() as ctx:
        def sb(name, shape, dt):
            return ctx.enter_context(nc.sbuf_tensor(name, shape, dt))

        def ps(name, shape, dt=F32):
            return ctx.enter_context(nc.psum_tensor(name, shape, dt))

        used = []

        def sem(name):
            used.append(ctx.enter_context(nc.semaphore(name)))
            return used[-1]

        row_i = sb("row_i", [P, IN_TILES], I32)
        col_i = sb("col_i", [P, IN_TILES], I32)
        bias_in = sb("bias_in", [P, IN_TILES * HEADS], F32)
        row_f = sb("row_f", [P, IN_TILES], F32)
        blk_i = sb("blk_i", [P, IN_TILES], I32)
        low_i = sb("low_i", [P, IN_TILES], I32)
        blk_b = sb("blk_b", [P, IN_TILES], BF16)
        low_b = sb("low_b", [P, IN_TILES], BF16)
        iota_b = sb("iota_b", [P, P], BF16)
        iota_p = sb("iota_p", [P, 1], F32)
        earlier = sb("earlier", [P, P], F32)
        earlier_b = sb("earlier_b", [P, P], BF16)
        ones_f = sb("ones_f", [P, P], F32)
        ones_b = sb("ones_b", [P, 1], BF16)
        zeros_f = sb("zeros_f", [P, IN_TILES], F32)
        counts = sb("counts", [P, BLOCKS, IN_TILES + 1], F32)
        start = sb("start", [P, BLOCKS], F32)
        total = sb("total", [P, BLOCKS], F32)
        fill_i = sb("fill_i", [P, BLOCKS], I32)
        fill_s = sb("fill_s", [P, BLOCKS], I32)
        fill_f = sb("fill_f", [P, BLOCKS], F32)
        ends = sb("ends", [P, BLOCKS], F32)
        group_at = sb("group_at", [P, GC], F32)
        passed = sb("passed", [P, GC, BLOCKS], F32)
        group_f = sb("group_f", [P, GC], F32)
        group_i = sb("group_i", [P, GC], I32)
        low_hot = sb("low_hot", [P, 2, B, P], BF16)
        blk_hot = sb("blk_hot", [P, 2, B, BLOCKS], BF16)
        row_bc = sb("row_bc", [P, 2, B * P], I32)
        low_bc = sb("low_bc", [P, B * P], I32)
        low_hot_t = sb("low_hot_t", [P, 2, B * P], F32)
        same = sb("same", [P, 2, B, P], BF16)
        picked = sb("picked", [P, B, BLOCKS], F32)
        before = sb("before", [P, B], F32)
        place = sb("place", [P, B], I32)
        tile_of = sb("tile_of", [P, B], I32)
        part_of = sb("part_of", [P, B], I32)
        address = sb("address", [P, 2, B], I32)
        record = sb("record", [P, IN_TILES, REC], F32)
        staged = sb("staged", [P, 2, B, REC], F32)
        blank = sb("blank", [P, TILES // 4, REC], F32)

        hist = [ps(f"hist{b}", [P, B * BLOCKS]) for b in range(2)]
        ranks = [ps(f"ranks{b}", [P, B * BLOCKS]) for b in range(2)]
        within = [ps(f"within{b}", [P, B]) for b in range(2)]
        small = ps("small", [P, 2 * BLOCKS])

        s_rows, s_cols, s_bias, s_blank = sem("s_rows"), sem("s_cols"), sem("s_bias"), sem("s_blank")
        s_blanked, s_group = sem("s_blanked"), sem("s_group")
        s_iota, s_const, s_cut, s_dve, s_act = sem("s_iota"), sem("s_const"), sem("s_cut"), sem("s_dve"), sem("s_act")
        s_hot, s_hist, s_kept, s_hot2, s_ranks, s_addr, s_staged = (
            [sem(f"{n}{b}") for b in range(2)] for n in ("s_hot", "s_hist", "s_kept", "s_hot2", "s_ranks", "s_addr",
                                                       "s_staged"))
        s_total, s_small, s_start, s_groups = sem("s_total"), sem("s_small"), sem("s_start"), sem("s_groups")
        s_bc = [sem(f"s_bc{b}") for b in range(2)]
        s_record, s_passed = sem("s_record"), sem("s_passed")
        s_put = [moved[b * B:(b + 1) * B] for b in range(2)]
        block = open_block(nc, ctx, used)

        @block.sync
        def _(eng):
            eng.dma_start(row_i[:, :], src_t).then_inc(s_rows, 16)
            eng.dma_start(col_i[:, :], dst_t).then_inc(s_cols, 16)
            eng.dma_start(bias_in[:, :], bias_t).then_inc(s_bias, 16)
            eng.wait_ge(s_blank, 2)
            for q in range(4):
                eng.dma_start(records.rearrange("(p q t) w -> p q (t w)", p=P, q=4)[:, q, :],
                              blank[:, :, :].rearrange("p t w -> p (t w)")).then_inc(s_blanked, 16)
            rows = src_row.rearrange("(n w) -> n w", w=B * P)

            with eng.Fori(0, BATCHES // 2) as i:
                for b in range(2):
                    eng.wait_ge(s_addr[b], i)
                    eng.dma_start(row_bc[:, b, :],
                                  rows[bass.ds(i * 2 + b, 1), :].rearrange("a w -> (a w)").partition_broadcast(P)
                                  ).then_inc(s_bc[b], 16)
            eng.wait_ge(s_groups, 1)
            eng.dma_start(group_block.rearrange("(c p) -> p c", p=P), group_i[:, :],
                          allow_slow_non_contiguous=True).then_inc(s_group, 16)
            eng.wait_ge(s_group, 16)

        @block.gpsimd
        def _(eng):
            eng.iota(iota_b[:, :], pattern=[[1, P]], base=0, channel_multiplier=0,
                     allow_small_or_imprecise_dtypes=True).then_inc(s_iota, 1)
            eng.iota(iota_p[:, :], pattern=[[1, 1]], base=0, channel_multiplier=1,
                     allow_small_or_imprecise_dtypes=True).then_inc(s_iota, 1)
            eng.iota(group_at[:, :], pattern=[[P, GC]], base=0, channel_multiplier=1,
                     allow_small_or_imprecise_dtypes=True).then_inc(s_iota, 1)
            eng.memset(ones_f[:, :], 1.0).then_inc(s_const, 1)
            eng.memset(ones_b[:, :], 1.0).then_inc(s_const, 1)
            eng.memset(zeros_f[:, :], 0.0).then_inc(s_const, 1)
            eng.memset(blank[:, :, :], 0.0).then_inc(s_blank, 1)
            eng.wait_ge(s_blank, 1)
            eng.memset(blank[:, :, 1:2], PAD_ROW).then_inc(s_blank, 1)
            eng.wait_ge(s_const, 3)
            eng.affine_select(out=earlier[:, :], in_=ones_f[:, :], compare_op=ALU.is_gt, fill=0.0, base=0,
                              pattern=[[1, P]], channel_multiplier=-1).then_inc(s_cut, 1)
            eng.affine_select(out=earlier_b[:, :], in_=ones_f[:, :], compare_op=ALU.is_gt, fill=0.0, base=0,
                              pattern=[[1, P]], channel_multiplier=-1).then_inc(s_cut, 1)
            eng.wait_ge(s_blanked, 64)
            with eng.Fori(0, BATCHES // 2) as i:
                for b in range(2):
                    eng.wait_ge(s_addr[b], i + 1)
                    eng.wait_ge(s_staged[b], i + 1)
                    for u in range(B):
                        eng.sem_inc(s_passed, 1)
                        eng.indirect_dma_start(
                            records, bass.IndirectOffsetOnAxis(address[:, b, u:u + 1], 0),
                            staged[:, b, u, :], None,
                        ).then_inc(s_put[b][u], 16)
            for b in range(2):
                for u in range(B):
                    eng.wait_ge(s_put[b][u], 16 * (BATCHES // 2))

        @block.scalar
        def _(eng):
            eng.wait_ge(s_bias, 16)
            nc.scalar.copy(record[:, :, 2:REC], bias_in[:, :].rearrange("p (t h) -> p t h", h=HEADS)).then_inc(s_record, 1)
            with eng.Fori(0, BATCHES // 2) as i:
                for b in range(2):
                    eng.wait_ge(s_hist[b], i + 1)
                    nc.scalar.copy(counts[:, :, bass.ds(i * 2 * B + b * B + 1, B)].rearrange("p h t -> p t h"),
                                   hist[b][:, :].rearrange("p (t h) -> p t h", h=BLOCKS)).then_inc(s_kept[b], 1)

            eng.wait_ge(s_record, 3)
            with eng.Fori(0, BATCHES // 2) as i:
                for b in range(2):
                    for u in range(B):
                        eng.wait_ge(s_put[b][u], i * 16)
                    nc.scalar.copy(staged[:, b, :, :], record[:, bass.ds(i * 2 * B + b * B, B), :]).then_inc(s_staged[b], 1)

        @block.vector
        def _(eng):
            st = Steps(eng, s_dve)
            eng.wait_ge(s_rows, 16)
            nc.vector.tensor_copy(row_f[:, :], row_i[:, :]).then_inc(s_record, 1)
            st.link(nc.vector.tensor_scalar(blk_i[:, :], row_i[:, :], 7, None, ALU.arith_shift_right))
            st.link(nc.vector.tensor_scalar(low_i[:, :], row_i[:, :], P - 1, None, ALU.bitwise_and))
            st.link(nc.vector.tensor_copy(blk_b[:, :], blk_i[:, :]))
            st.link(nc.vector.tensor_copy(low_b[:, :], low_i[:, :]))
            st.link(nc.vector.tensor_copy(record[:, :, 1], row_f[:, :]))
            eng.wait_ge(s_cols, 16)
            nc.vector.tensor_copy(record[:, :, 0], col_i[:, :]).then_inc(s_record, 1)
            eng.wait_ge(s_iota, 3)

            def hot_block(i, b):
                return nc.vector.tensor_tensor(
                    blk_hot[:, b, :, :],
                    iota_b[:, 0:BLOCKS].unsqueeze(1).broadcast_to([P, B, BLOCKS]),
                    blk_b[:, bass.ds(i * 2 * B + b * B, B)].unsqueeze(2).broadcast_to([P, B, BLOCKS]), ALU.is_equal)

            with eng.Fori(0, BATCHES // 2) as i:
                for b in range(2):
                    eng.wait_ge(s_hist[b], i)
                    hot_block(i, b).then_inc(s_hot[b], 1)
                    nc.vector.tensor_tensor(
                        low_hot[:, b, :, :],
                        iota_b[:, :].unsqueeze(1).broadcast_to([P, B, P]),
                        low_b[:, bass.ds(i * 2 * B + b * B, B)].unsqueeze(2).broadcast_to([P, B, P]),
                        ALU.is_equal).then_inc(s_hot[b], 1)
            for b in range(2):
                eng.wait_ge(s_kept[b], BATCHES // 2)
            eng.wait_ge(s_const, 3)
            st.link(nc.vector.memset(counts[:, :, 0:1], 0.0))
            for h in range(BLOCKS):
                last = nc.vector.tensor_tensor_scan(counts[:, h, 1:], zeros_f[:, :], counts[:, h, 1:], 0.0,
                                                    ALU.add, ALU.add)
            st.link(last)
            nc.vector.tensor_copy(total[:, :], counts[:, :, IN_TILES]).then_inc(s_total, 1)
            eng.wait_ge(s_small, 1)
            st.link(nc.vector.tensor_scalar(fill_i[:, :], small[:, 0:BLOCKS], float(SPAN - 1), None, ALU.add))
            st.link(nc.vector.tensor_scalar(fill_s[:, :], fill_i[:, :], SPAN.bit_length() - 1, None, ALU.arith_shift_right))
            st.link(nc.vector.tensor_scalar(fill_f[:, :], fill_s[:, :], float(SPAN), None, ALU.mult))
            st.link(nc.vector.tensor_tensor_scan(ends[:, :], zeros_f[:, 0:BLOCKS], fill_f[:, :], 0.0, ALU.add, ALU.add))
            st.link(nc.vector.tensor_tensor(start[:, :], ends[:, :], fill_f[:, :], ALU.subtract))
            st.link(nc.vector.tensor_tensor(start[:, :], small[:, BLOCKS:], start[:, :], ALU.add))
            nc.vector.tensor_tensor(counts[:, :, 0:IN_TILES], counts[:, :, 0:IN_TILES],
                                    start[:, :].unsqueeze(2).broadcast_to([P, BLOCKS, IN_TILES]),
                                    ALU.add).then_inc(s_start, 1)
            st.link(nc.vector.tensor_scalar(group_at[:, :], group_at[:, :], float(SPAN), None, ALU.mult))
            st.link(nc.vector.tensor_tensor(passed[:, :, :], group_at[:, :].unsqueeze(2).broadcast_to([P, GC, BLOCKS]),
                                            ends[:, :].unsqueeze(1).broadcast_to([P, GC, BLOCKS]), ALU.is_ge))
            st.link(nc.vector.tensor_reduce(group_f[:, :], passed[:, :, :], AX.X, ALU.add))
            nc.vector.tensor_scalar(group_i[:, :], group_f[:, :], float(BLOCKS - 1), None, ALU.min).then_inc(s_groups, 1)
            eng.wait_ge(s_cut, 2)
            done = st.n

            with eng.Fori(0, BATCHES // 2) as i:
                st2 = Steps(eng, s_act, i, 14)
                for b in range(2):
                    eng.wait_ge(s_bc[b], i * 16 + 16)
                    st2.link(nc.vector.tensor_scalar(low_bc[:, :], row_bc[:, b, :], P - 1, None, ALU.bitwise_and))
                    nc.vector.tensor_scalar(low_hot_t[:, b, :], low_bc[:, :], iota_p[:, :], None,
                                            ALU.is_equal).then_inc(s_hot2[b], 1)
                    for u in range(B):
                        last = nc.vector.scalar_tensor_tensor(
                            same[:, b, u, :], row_bc[:, b, u * P:(u + 1) * P],
                            row_f[:, bass.ds(i * 2 * B + b * B + u, 1)], earlier_b[:, :], ALU.is_equal, ALU.mult)
                    last.then_inc(s_hot2[b], 1)
                    st2.link(hot_block(i, b))
                    eng.wait_ge(s_ranks[b], i + 1)
                    st2.link(nc.vector.tensor_tensor(picked[:, :, :],
                                                     ranks[b][:, :].rearrange("p (t h) -> p t h", h=BLOCKS),
                                                     blk_hot[:, b, :, :], ALU.mult))
                    st2.link(nc.vector.tensor_reduce(before[:, :], picked[:, :, :], AX.X, ALU.add))
                    st2.link(nc.vector.tensor_tensor(place[:, :], within[b][:, :], before[:, :], ALU.add))
                    st2.link(nc.vector.tensor_scalar(tile_of[:, :], place[:, :], 7, None, ALU.arith_shift_right))
                    st2.link(nc.vector.tensor_scalar(part_of[:, :], place[:, :], P - 1, None, ALU.bitwise_and))
                    for u in range(B):
                        eng.wait_ge(s_put[b][u], i * 16)
                    nc.vector.scalar_tensor_tensor(address[:, b, :], part_of[:, :], float(TILES),
                                                   tile_of[:, :], ALU.mult, ALU.add).then_inc(s_addr[b], 1)

        @block.tensor
        def _(eng):
            with eng.Fori(0, BATCHES // 2) as i:
                for b in range(2):
                    eng.wait_ge(s_hot[b], i * 2 + 2)
                    eng.wait_ge(s_kept[b], i)
                    for u in range(B):
                        last = nc.tensor.matmul(hist[b][:, u * BLOCKS:(u + 1) * BLOCKS], low_hot[:, b, u, :],
                                                blk_hot[:, b, u, :], start=True, stop=True)
                    last.then_inc(s_hist[b], 1)
            eng.wait_ge(s_total, 1)
            eng.wait_ge(s_cut, 2)
            nc.tensor.matmul(small[:, 0:BLOCKS], ones_f[:, :], total[:, :], start=True, stop=True)
            nc.tensor.matmul(small[:, BLOCKS:], earlier[:, :], total[:, :], start=True, stop=True).then_inc(s_small, 1)
            eng.wait_ge(s_start, 1)
            with eng.Fori(0, BATCHES // 2) as i:
                for b in range(2):
                    eng.wait_ge(s_hot2[b], i * 2 + 2)
                    eng.wait_ge(s_addr[b], i)
                    for u in range(B):
                        nc.tensor.matmul(ranks[b][:, u * BLOCKS:(u + 1) * BLOCKS], low_hot_t[:, b, u * P:(u + 1) * P],
                                         counts[:, :, bass.ds(i * 2 * B + b * B + u, 1)].rearrange("p h a -> p (h a)"),
                                         start=True, stop=True)
                    for u in range(B):
                        last = nc.tensor.matmul(within[b][:, u:u + 1], same[:, b, u, :], ones_b[:, :],
                                                start=True, stop=True)
                    last.then_inc(s_ranks[b], 1)


NORM_STEPS = 5


def norm_scale(nc, eng, st, passed, s_var, s_root, value, x, stats, mean_var, root, out):
    st.link(nc.vector.bn_stats(stats, x))
    eng.sem_inc(passed, 1)
    nc.vector.bn_aggr(mean_var, stats).then_inc(s_var, 1)
    eng.wait_ge(s_root, value)
    st.link(nc.vector.reciprocal(root, root))
    return nc.vector.tensor_scalar(out, x, mean_var[:, 0:1], root, ALU.subtract, ALU.mult)


def project_qkv(nc, x, ln_g, ln_b, wq, bq, wk, bk, wv, bv, z0, q, k, v):
    EPS = 1e-5
    KC = C // P
    ROWS = NODES // P
    with ExitStack() as ctx:
        def sb(name, shape, dt=F32):
            return ctx.enter_context(nc.sbuf_tensor(name, shape, dt))

        def ps(name, shape, dt=F32):
            return ctx.enter_context(nc.psum_tensor(name, shape, dt))

        used = []

        def sem(name):
            used.append(ctx.enter_context(nc.semaphore(name)))
            return used[-1]

        def sem2(name):
            return [sem(f"{name}{b}") for b in range(2)]

        w = sb("qkv_w", [P, 3, KC, C])
        bias = sb("qkv_bias", [P, 3, C])
        gain, shift = sb("qkv_gain", [P, C]), sb("qkv_shift", [P, C])
        ones, ident = sb("qkv_ones", [P, P]), sb("qkv_ident", [P, P])
        eps = sb("qkv_eps", [P, 1])
        xt = sb("qkv_x", [P, 2, C])
        z0t = sb("qkv_z0", [P, 2, C])
        zn = sb("qkv_zn", [P, C])
        zt = sb("qkv_z", [P, 2, C])
        zT = sb("qkv_zT", [P, 2, C])
        out = sb("qkv_out", [P, 2, 3, C])
        stats, mean_var, root = sb("qkv_stats", [P, 6]), sb("qkv_mv", [P, 2]), sb("qkv_root", [P, 1])
        turned = [ps(f"qkv_turned{b}", [P, C]) for b in range(2)]
        prod = [ps(f"qkv_prod{n}", [P, C]) for n in range(6)]

        s_w, s_c, s_cut, s_b, s_dve, s_passed, s_var, s_root = (
            sem(f"qkv_s_{n}") for n in ("w", "c", "cut", "b", "dve", "passed", "var", "root"))
        s_x, s_z0, s_z, s_turn, s_zT, s_stored_z0 = (
            sem2(f"qkv_s_{n}") for n in ("x", "z0", "z", "turn", "zT", "stored_z0"))
        s_prod, s_out, s_stored = ([sem(f"qkv_s_{n}{m}") for m in range(6)] for n in ("prod", "out", "stored"))
        block = open_block(nc, ctx, used)

        def tile_rows(a, j, c):
            return a.rearrange("(n p) c -> n p c", p=P)[bass.ds(j * 2 + c, 1), :, :].rearrange("a p c -> (a p) c")

        @block.sync
        def _(eng):
            def load_x(j, c):
                b, k_ = c % 2, j + c // 2
                eng.wait_ge(s_z0[b], k_)
                eng.dma_start(xt[:, b, :], tile_rows(x, j, c)).then_inc(s_x[b], 16)

            eng.dma_start(xt[:, 0, :], x[0:P, :]).then_inc(s_x[0], 16)
            eng.dma_start(xt[:, 1, :], x[P:2 * P, :]).then_inc(s_x[1], 16)
            for dst, a in ((gain, ln_g), (shift, ln_b)):
                eng.dma_start(dst[:, :], a.partition_broadcast(P)).then_inc(s_b, 16)
            for n, a in enumerate((wq, wk, wv)):
                eng.dma_start(w[:, n, :, :], a.rearrange("(k p) n -> p k n", p=P)).then_inc(s_w, 16)
            for n, a in enumerate((bq, bk, bv)):
                eng.dma_start(bias[:, n, :], a.partition_broadcast(P)).then_inc(s_b, 16)

            def store(j, c):
                b, k_ = c % 2, j + c // 2
                eng.wait_ge(s_z0[b], k_ + 1)
                eng.dma_start(tile_rows(z0, j, c), z0t[:, b, :]).then_inc(s_stored_z0[b], 16)
                for n, a in enumerate((q, k, v)):
                    eng.wait_ge(s_out[b * 3 + n], k_ + 1)
                    eng.dma_start(tile_rows(a, j, c), out[:, b, n, :]).then_inc(s_stored[b * 3 + n], 16)

            with eng.Fori(0, ROWS // 2 - 1) as j:
                for c in range(2):
                    load_x(j, c + 2)
                    store(j, c)
            for c in range(2):
                store(ROWS // 2 - 1, c)
            for b in range(2):
                eng.wait_ge(s_stored_z0[b], 16 * (ROWS // 2))
            for m in range(6):
                eng.wait_ge(s_stored[m], 16 * (ROWS // 2))

        @block.gpsimd
        def _(eng):
            eng.memset(ones[:, :], 1.0).then_inc(s_c, 1)
            eng.memset(eps[:, :], EPS).then_inc(s_c, 1)
            eng.wait_ge(s_c, 2)
            eng.affine_select(out=ident[:, :], in_=ones[:, :], compare_op=ALU.is_equal, fill=0.0, base=0,
                              pattern=[[1, P]], channel_multiplier=-1).then_inc(s_cut, 1)

        @block.vector
        def _(eng):
            def norms(st, j, c, done):
                b, k_ = c % 2, j + c // 2
                eng.wait_ge(s_x[b], k_ * 16 + 16)
                eng.wait_ge(s_stored_z0[b], k_ * 16)
                norm_scale(nc, eng, st, s_passed, s_var, s_root, done + 1, xt[:, b, :], stats[:, :], mean_var[:, :], root[:, :],
                           z0t[:, b, :]).then_inc(s_z0[b], 1)
                eng.wait_ge(s_z0[b], k_ + 1)
                st.link(norm_scale(nc, eng, st, s_passed, s_var, s_root, done + 2, z0t[:, b, :], stats[:, :], mean_var[:, :],
                                   root[:, :], zn[:, :]))
                st.link(nc.vector.tensor_tensor(zn[:, :], zn[:, :], gain[:, :], ALU.mult))
                eng.wait_ge(s_turn[b], k_)
                nc.vector.tensor_tensor(zt[:, b, :], zn[:, :], shift[:, :], ALU.add).then_inc(s_z[b], 1)

            def leave(j, c):
                b, k_ = c % 2, j + c // 2
                for n in range(3):
                    m = b * 3 + n
                    eng.wait_ge(s_prod[m], k_ + 1)
                    eng.wait_ge(s_stored[m], k_ * 16)
                    nc.vector.scalar_tensor_tensor(out[:, b, n, :], prod[m][:, :], float(D) ** -0.5 if n == 0 else 1.0,
                                                   bias[:, n, :], ALU.mult, ALU.add).then_inc(s_out[m], 1)

            STEPS = 6
            pre = Steps(eng, s_dve)
            eng.wait_ge(s_b, 80)
            pre.link(nc.vector.tensor_scalar(bias[:, 0, :], bias[:, 0, :], float(D) ** -0.5, None, ALU.mult))
            norms(pre, 0, 0, 0)
            assert pre.n == STEPS + 1
            with eng.Fori(0, ROWS // 2 - 1) as j:
                st = Steps(eng, s_dve, j, 2 * STEPS, STEPS + 1)
                for c in range(2):
                    norms(st, j, c + 1, j * 4 + 2 * (c + 1))
                    leave(j, c)
            post = Steps(eng, s_dve, None, 0, STEPS + 1 + (ROWS // 2 - 1) * 2 * STEPS)
            last = ROWS // 2 - 1
            norms(post, last, 1, last * 4 + 2)
            for c in range(2):
                leave(last, c)

        @block.scalar
        def _(eng):
            eng.wait_ge(s_c, 2)

            def roots(done):
                for n in range(2):
                    eng.wait_ge(s_var, done + n + 1)
                    nc.scalar.activation(root[:, :], mean_var[:, 1:2], ACT.Sqrt, bias=eps[:, :]).then_inc(s_root, 1)

            def keep(j, c):
                b, k_ = c % 2, j + c // 2
                eng.wait_ge(s_turn[b], k_ + 1)
                eng.wait_ge(s_prod[b * 3 + 2], k_)
                nc.scalar.copy(zT[:, b, :], turned[b][:, :]).then_inc(s_zT[b], 1)

            roots(0)
            with eng.Fori(0, ROWS // 2 - 1) as j:
                for c in range(2):
                    keep(j, c)
                    roots(j * 4 + 2 * (c + 1))
            last = ROWS // 2 - 1
            keep(last, 0)
            roots(last * 4 + 2)
            keep(last, 1)

        @block.tensor
        def _(eng):
            eng.wait_ge(s_cut, 1)
            eng.wait_ge(s_w, 48)
            with eng.Fori(0, ROWS // 2) as j:
                for b in range(2):
                    eng.wait_ge(s_z[b], j + 1)
                    eng.wait_ge(s_zT[b], j)
                    for n in range(KC):
                        last = nc.tensor.transpose(turned[b][:, n * P:(n + 1) * P], zt[:, b, n * P:(n + 1) * P], ident[:, :])
                    last.then_inc(s_turn[b], 1)
                    eng.wait_ge(s_zT[b], j + 1)
                    for n in range(3):
                        m = b * 3 + n
                        eng.wait_ge(s_out[m], j)
                        for kc in range(KC):
                            last = nc.tensor.matmul(prod[m][:, :], zT[:, b, kc * P:(kc + 1) * P], w[:, n, kc, :],
                                                    start=(kc == 0), stop=(kc == KC - 1))
                        last.then_inc(s_prod[m], 1)


def attention(nc, moved, count, records, group_block, q, k, v, mixed):
    U = 8
    TURN = 2 * U
    TURNS = TILES // TURN
    assert TILES % TURN == 0
    BIG = 3.0e38
    k_from = count
    v_from = count + 16 * TURNS
    LANE = RANGE_TILES * P
    with ExitStack() as ctx:
        def sb(name, shape, dt, on=ctx):
            return on.enter_context(nc.sbuf_tensor(name, shape, dt))

        def ps(name, shape, dt=F32, on=ctx):
            return on.enter_context(nc.psum_tensor(name, shape, dt))

        def sem(name, on=ctx):
            used.append(on.enter_context(nc.semaphore(name)))
            return used[-1]

        rec = sb("at_rec", [P, TILES, REC], F32)
        groups = sb("groups", [1, GROUPS], I32)
        low_neg = sb("low_neg", [P, TILES + 3], F32)
        weight = sb("weight", [P, TILES, HEADS], F32)
        iota_f = sb("iota_f", [P, P], F32)
        ident = sb("ident", [P, P], F32)
        ident_b = sb("ident_b", [P, P], BF16)
        ones = sb("ones", [P, P], F32)

        used = []
        with ExitStack() as part:
            q_sb = sb("q_sb", [P, BLOCKS, C], F32, part)
            row_i = sb("at_row_i", [P, TILES], I32, part)
            low_f = sb("at_low_f", [P, TILES], F32, part)
            padded = sb("padded", [P, TILES], F32, part)
            index = sb("k_index", [P, 2, U], I32, part)
            k_sb = sb("k_sb", [P, TURN, C], F32, part)
            away = sb("away", [P, 4, P], F32, part)
            hot = sb("hot", [P, 4, P], BF16, part)
            hot_t = sb("hot_t", [P, 4, P], F32, part)
            product = sb("product", [P, 4, C], F32, part)
            turned = [ps(f"turned{b}", [P, P], BF16, part) for b in range(4)]
            q_edge = [ps(f"q_edge{b}", [P, C], F32, part) for b in range(4)]
            s_const, s_cut = sem("a_const", part), sem("a_cut", part)
            s_rec, s_grp, s_q = sem("a_rec", part), sem("a_grp", part), sem("a_q", part)
            s_dve, s_low, s_index, s_passed = (sem(n, part) for n in ("a_dve", "a_low", "a_index", "a_passed"))
            s_k = moved[:TURN]
            r_away, r_hot, r_turned, r_hot_t, r_edge, r_product, r_score = (
                Ring([sem(f"{n}{b}", part) for b in range(4)], TURN)
                for n in ("a_away", "a_hot", "a_turned", "a_hot_t", "a_edge", "a_product", "a_score"))
            block = open_block(nc, part, used)

            @block.sync
            def _(eng):
                eng.dma_start(rec[:, :, :], records.rearrange("(p t) w -> p t w", p=P)).then_inc(s_rec, 16)
                eng.dma_start(groups[0:1, :], group_block[0:GROUPS].unsqueeze(0)).then_inc(s_grp, 16)
                eng.dma_start(q_sb[:, :, :], q.rearrange("(b p) c -> p b c", p=P)).then_inc(s_q, 16)

            @block.gpsimd
            def _(eng):
                eng.memset(ones[:, :], 1.0).then_inc(s_const, 1)
                eng.iota(iota_f[:, :], pattern=[[1, P]], base=0, channel_multiplier=0,
                         allow_small_or_imprecise_dtypes=True).then_inc(s_const, 1)
                eng.memset(low_neg[:, TILES:], 0.0).then_inc(s_const, 1)
                eng.wait_ge(s_const, 3)
                for m in (ident, ident_b):
                    eng.affine_select(out=m[:, :], in_=ones[:, :], compare_op=ALU.is_equal, fill=0.0, base=0,
                                      pattern=[[1, P]], channel_multiplier=-1).then_inc(s_cut, 1)
                eng.wait_ge(s_rec, 16)
                with eng.Fori(0, TURNS) as i:
                    for half in range(2):
                        for n in range(U):
                            eng.wait_ge(s_k[half * U + n], i * 16 + k_from)
                        eng.tensor_copy(index[:, half, :], rec[:, bass.ds(i * TURN + half * U, U), 0]
                                        ).then_inc(s_index, 1)
                        eng.wait_ge(s_index, i * 2 + half + 1)
                        for n in range(U):
                            u = half * U + n
                            r_product.wait(eng, i, u - TURN)
                            eng.sem_inc(s_passed, 1)
                            eng.indirect_dma_start(k_sb[:, u, :], None, k,
                                                   bass.IndirectOffsetOnAxis(index[:, half, n:n + 1], 0)
                                                   ).then_inc(s_k[u], 16)

            @block.vector
            def _(eng):
                st = Steps(eng, s_dve)
                r_product.start(eng)
                r_score.start(eng)
                eng.wait_ge(s_rec, 16)
                row = rec[:, :, 1]
                st.link(nc.vector.tensor_copy(row_i[:, :], row))
                st.link(nc.vector.tensor_scalar(row_i[:, :], row_i[:, :], P - 1, None, ALU.bitwise_and))
                st.link(nc.vector.tensor_copy(low_f[:, :], row_i[:, :]))
                st.link(nc.vector.tensor_scalar(padded[:, :], row, 0.0, float(4 * P), ALU.is_lt, ALU.mult))
                st.link(nc.vector.tensor_tensor(low_f[:, :], low_f[:, :], padded[:, :], ALU.add))
                nc.vector.tensor_scalar(low_neg[:, 0:TILES], low_f[:, :], -1.0, None, ALU.mult).then_inc(s_low, 1)
                with eng.Fori(0, TURNS) as i:
                    def reduce(u):
                        r_product.wait(eng, i, u)
                        nc.vector.tensor_reduce(weight[:, bass.ds(i * TURN + u, 1), :].rearrange("p a h -> p (a h)"),
                                                product[:, u % 4, :].rearrange("p (h d) -> p h d", d=D), AX.X,
                                                ALU.add).then_inc(r_score.sem(u), 1)

                    for u in range(TURN):
                        eng.wait_ge(s_k[u], i * 16 + (k_from + 16))
                        r_edge.wait(eng, i, u)
                        r_score.wait(eng, i, u - 4)
                        nc.vector.tensor_tensor(product[:, u % 4, :], q_edge[u % 4][:, :], k_sb[:, u, :],
                                                ALU.mult).then_inc(r_product.sem(u), 1)
                        if u:
                            reduce(u - 1)
                    reduce(TURN - 1)

            @block.scalar
            def _(eng):
                for r in (r_away, r_hot, r_hot_t):
                    r.start(eng)
                eng.wait_ge(s_low, 1)
                eng.wait_ge(s_const, 3)

                def distance(i, u):
                    r_hot.wait(eng, i, u - 4)
                    nc.scalar.activation(away[:, u % 4, :], iota_f[:, :], ACT.Abs, bias=low_neg[:, bass.ds(i * TURN + u, 1)]
                                         ).then_inc(r_away.sem(u), 1)

                def one_hot(i, u):
                    r_away.wait(eng, i, u)
                    r_turned.wait(eng, i, u - 4)
                    nc.scalar.activation(hot[:, u % 4, :], away[:, u % 4, :], ACT.Relu, bias=1.0, scale=-1.0
                                         ).then_inc(r_hot.sem(u), 1)

                def transposed(i, u):
                    r_turned.wait(eng, i, u)
                    r_edge.wait(eng, i, u - 4)
                    nc.scalar.copy(hot_t[:, u % 4, :], turned[u % 4][:, :]).then_inc(r_hot_t.sem(u), 1)

                for u in range(3):
                    distance(0, u)
                for u in range(2):
                    one_hot(0, u)
                with eng.Fori(0, TURNS) as i:
                    for u in range(TURN):
                        distance(i, u + 3)
                        one_hot(i, u + 2)
                        transposed(i, u)

            @block.tensor
            def _(eng):
                r_turned.start(eng)
                r_edge.start(eng)
                eng.wait_ge(s_cut, 2)
                eng.wait_ge(s_grp, 16)
                eng.wait_ge(s_q, 16)

                def turn(i, u):
                    r_hot.wait(eng, i, u)
                    r_hot_t.wait(eng, i, u - 4)
                    nc.tensor.transpose(turned[u % 4][:, :], hot[:, u % 4, :], ident_b[:, :]).then_inc(r_turned.sem(u), 1)

                turn(0, 0)
                turn(0, 1)
                with eng.Fori(0, TURNS) as i:
                    for u in range(TURN):
                        if u % GROUP == 0:
                            at = eng.value_load(groups[0:1, bass.ds(i * (TURN // GROUP) + u // GROUP, 1)],
                                                min_val=0, max_val=BLOCKS - 1)
                        turn(i, u + 2)
                        r_hot_t.wait(eng, i, u)
                        r_product.wait(eng, i, u - 4)
                        nc.tensor.matmul(q_edge[u % 4][:, :], hot_t[:, u % 4, :],
                                         q_sb[:, bass.ds(at, 1), :].rearrange("p a c -> p (a c)"),
                                         start=True, stop=True).then_inc(r_edge.sem(u), 1)

        used = []
        with ExitStack() as part:
            stage_s = sb("stage_s", [P, 2, RANGES, HEADS], F32, part)
            stage_k = sb("stage_k", [P, 2, RANGES, HEADS], F32, part)
            stage_p = sb("stage_p", [P, 2, P], F32, part)
            keys = sb("keys", [P, LANE], F32, part)
            score = sb("score", [P, LANE], F32, part)
            cont = sb("cont", [P, LANE + 1], F32, part)
            ahead = sb("ahead", [P, LANE], F32, part)
            back = sb("back", [P, LANE], F32, part)
            row4 = sb("row4", [1, 4, HEADS, RANGES], F32, part)
            linked = sb("linked", [1, HEADS, RANGES + 1], F32, part)
            whole = sb("whole", [1, HEADS, RANGES], F32, part)
            pass_f = sb("pass_f", [1, HEADS, RANGES], F32, part)
            pass_b = sb("pass_b", [1, HEADS, RANGES], F32, part)
            state = sb("state", [1, 2, HEADS, RANGES], F32, part)
            carry = sb("carry", [1, 2, RANGES, HEADS], F32, part)
            carried = sb("carried", [P, 2], F32, part)
            turn_s = [ps(f"turn_s{b}", [P, P], F32, part) for b in range(2)]
            turn_k = [ps(f"turn_k{b}", [P, P], F32, part) for b in range(2)]
            ends4 = ps("ends4", [1, 4 * P], F32, part)
            carry_ps = ps("carry_ps", [P, 2], F32, part)
            s_dve, s_loc, s_ends, s_carry, s_carried, s_sub = (
                sem(n, part) for n in ("m_dve", "m_loc", "m_ends", "m_carry", "m_carried", "m_sub"))
            s_sum, s_row, s_turn, s_keep_s, s_keep_k, s_exp, s_back, s_keep = (
                [sem(f"{n}{b}", part) for b in range(2)]
                for n in ("m_sum", "m_row", "m_turn", "m_keep_s", "m_keep_k", "m_exp", "m_back", "m_keep"))
            block = open_block(nc, part, used)
            HALF = RANGE_TILES // 2

            def by_range(x):
                return x.rearrange("p (c j) h -> p c j h", c=RANGES)

            rec_range = by_range(rec[:, :, :])

            @block.tensor
            def _(eng):
                with eng.Fori(0, HALF) as i:
                    for b in range(2):
                        eng.wait_ge(s_sum[b], i + 1)
                        eng.wait_ge(s_row[b], i + 1)
                        eng.wait_ge(s_keep_s[b], i)
                        eng.wait_ge(s_keep_k[b], i)
                        nc.tensor.transpose(turn_s[b][:, :], stage_s[:, b, :, :].rearrange("p c h -> p (c h)"), ident[:, :])
                        nc.tensor.transpose(turn_k[b][:, :], stage_k[:, b, :, :].rearrange("p c h -> p (c h)"),
                                            ident[:, :]).then_inc(s_turn[b], 1)
                eng.wait_ge(s_loc, 2)
                for n, x in enumerate((ahead[:, LANE - 1:LANE], back[:, 0:1], keys[:, 0:1], keys[:, LANE - 1:LANE])):
                    last = nc.tensor.transpose(ends4[0:1, n * P:(n + 1) * P], x, ident[:, :])
                last.then_inc(s_ends, 1)
                eng.wait_ge(s_carry, 1)
                for n in range(2):
                    last = nc.tensor.matmul(carry_ps[:, n:n + 1], carry[0:1, n, :, :].rearrange("p c h -> p (c h)"),
                                            ones[0:1, 0:1], start=True, stop=True)
                last.then_inc(s_carried, 1)
                with eng.Fori(0, HALF) as i:
                    for b in range(2):
                        eng.wait_ge(s_exp[b], i + 1)
                        eng.wait_ge(s_keep[b], i)
                        nc.tensor.transpose(turn_s[b][:, :], stage_p[:, b, :], ident[:, :]).then_inc(s_back[b], 1)

            @block.scalar
            def _(eng):
                with eng.Fori(0, HALF) as i:
                    for b in range(2):
                        eng.wait_ge(s_turn[b], i)
                        nc.scalar.copy(stage_k[:, b, :, :],
                                       rec_range[:, :, bass.ds(i * 2 + b, 1), 1].broadcast_to([P, RANGES, HEADS])
                                       ).then_inc(s_row[b], 1)
                        eng.wait_ge(s_turn[b], i + 1)
                        nc.scalar.copy(keys[:, bass.ds((i * 2 + b) * P, P)], turn_k[b][:, :]).then_inc(s_keep_k[b], 1)
                eng.wait_ge(s_sub, 1)
                with eng.Fori(0, HALF) as i:
                    for b in range(2):
                        eng.wait_ge(s_back[b], i)
                        nc.scalar.activation(stage_p[:, b, :], score[:, bass.ds((i * 2 + b) * P, P)], ACT.Exp
                                             ).then_inc(s_exp[b], 1)

            @block.vector
            def _(eng):
                st = Steps(eng, s_dve)
                with eng.Fori(0, HALF) as i:
                    for b in range(2):
                        eng.wait_ge(s_turn[b], i)
                        j = bass.ds(i * 2 + b, 1)
                        nc.vector.tensor_tensor(stage_s[:, b, :, :],
                                                by_range(weight[:, :, :])[:, :, j, :].rearrange("p c a h -> p c (a h)"),
                                                rec_range[:, :, j, 2:REC].rearrange("p c a h -> p c (a h)"),
                                                ALU.add).then_inc(s_sum[b], 1)
                        eng.wait_ge(s_turn[b], i + 1)
                        nc.vector.tensor_copy(score[:, bass.ds((i * 2 + b) * P, P)], turn_s[b][:, :]).then_inc(s_keep_s[b], 1)
                for b in range(2):
                    eng.wait_ge(s_keep_k[b], HALF)
                    eng.wait_ge(s_keep_s[b], HALF)
                st.link(nc.vector.memset(cont[:, :], 1.0))
                st.link(nc.vector.tensor_tensor(cont[:, 1:LANE], keys[:, 1:], keys[:, 0:LANE - 1], ALU.is_equal))
                st.link(nc.vector.tensor_scalar(cont[:, :], cont[:, :], 1.0, BIG, ALU.subtract, ALU.mult))
                nc.vector.tensor_tensor_scan(ahead[:, :], cont[:, 0:LANE], score[:, :], -BIG, ALU.add, ALU.max).then_inc(s_loc, 1)
                nc.vector.tensor_tensor_scan(back[:, ::-1], cont[:, LANE:0:-1], score[:, ::-1], -BIG, ALU.add, ALU.max).then_inc(s_loc, 1)
                eng.wait_ge(s_ends, 1)
                st.link(nc.vector.tensor_copy(row4[:, :, :, :], ends4[0:1, :].rearrange("p (n c h) -> p n h c", n=4, c=RANGES)))
                first, last = row4[0:1, 2, :, :], row4[0:1, 3, :, :]
                st.link(nc.vector.memset(linked[:, :, :], 0.0))
                st.link(nc.vector.tensor_tensor(linked[:, :, 1:RANGES], first[:, :, 1:], last[:, :, 0:RANGES - 1], ALU.is_equal))
                st.link(nc.vector.tensor_tensor(whole[:, :, :], first, last, ALU.is_equal))
                for to, at in ((pass_f, linked[:, :, 0:RANGES]), (pass_b, linked[:, :, 1:])):
                    st.link(nc.vector.tensor_tensor(to[:, :, :], whole[:, :, :], at, ALU.mult))
                    st.link(nc.vector.tensor_scalar(to[:, :, :], to[:, :, :], 1.0, BIG, ALU.subtract, ALU.mult))
                st.link(nc.vector.tensor_scalar(linked[:, :, :], linked[:, :, :], 1.0, BIG, ALU.subtract, ALU.mult))

                def flat(x):
                    return x.rearrange("p h c -> p (h c)")

                st.link(nc.vector.tensor_tensor_scan(flat(state[:, 0, :, :]), flat(pass_f[:, :, :]),
                                                     flat(row4[:, 0, :, :]), 0.0, ALU.add, ALU.max))
                st.link(nc.vector.tensor_tensor_scan(flat(state[:, 1, :, :])[:, ::-1], flat(pass_b[:, :, :])[:, ::-1],
                                                     flat(row4[:, 1, :, :])[:, ::-1], 0.0, ALU.add, ALU.max))
                st.link(nc.vector.memset(carry[:, :, :, :], -BIG))
                st.link(nc.vector.tensor_tensor(carry[:, 0, 1:, :].rearrange("p c h -> p h c"), state[:, 0, :, 0:RANGES - 1],
                                                linked[:, :, 1:RANGES], ALU.add))
                nc.vector.tensor_tensor(carry[:, 1, 0:RANGES - 1, :].rearrange("p c h -> p h c"), state[:, 1, :, 1:],
                                        linked[:, :, 1:RANGES], ALU.add).then_inc(s_carry, 1)
                eng.wait_ge(s_carried, 1)
                st.link(nc.vector.tensor_copy(carried[:, :], carry_ps[:, :]))
                st.link(nc.vector.tensor_tensor_scan(ahead[:, :], cont[:, 0:LANE], score[:, :], carried[:, 0:1], ALU.add, ALU.max))
                st.link(nc.vector.tensor_tensor_scan(back[:, ::-1], cont[:, LANE:0:-1], score[:, ::-1], carried[:, 1:2],
                                                     ALU.add, ALU.max))
                st.link(nc.vector.tensor_tensor(ahead[:, :], ahead[:, :], back[:, :], ALU.max))
                nc.vector.tensor_tensor(score[:, :], score[:, :], ahead[:, :], ALU.subtract).then_inc(s_sub, 1)
                with eng.Fori(0, HALF) as i:
                    for b in range(2):
                        eng.wait_ge(s_back[b], i + 1)
                        nc.vector.tensor_copy(
                            by_range(weight[:, :, :])[:, :, bass.ds(i * 2 + b, 1), :].rearrange("p c a h -> p c (a h)"),
                            turn_s[b][:, :].rearrange("p (c h) -> p c h", c=RANGES)).then_inc(s_keep[b], 1)

        used = []
        with ExitStack() as part:
            total = sb("mix_total", [P, BLOCKS, C], F32, part)
            mass = sb("mix_mass", [P, BLOCKS, HEADS], F32, part)
            index = sb("v_index", [P, 2, U], I32, part)
            v_sb = sb("v_sb", [P, TURN, C], F32, part)
            scaled = sb("scaled", [P, 4, C], F32, part)
            away = sb("v_away", [P, 4, P], F32, part)
            hot = sb("v_hot", [P, 4, P], F32, part)
            mix = [ps(f"mix{b}", [P, C], F32, part) for b in range(4)]
            mass_ps = [ps(f"mass{b}", [P, HEADS], F32, part) for b in range(4)]
            s_passed, s_dve, s_index, s_norm, s_out = (sem(n, part) for n in ("v_passed", "v_dve", "v_index", "v_norm", "v_out"))
            s_v = moved[:TURN]
            r_away, r_hot, r_scaled, r_tile = (
                Ring([sem(f"{n}{b}", part) for b in range(4)], TURN) for n in ("v_away", "v_hot", "v_scaled", "v_tile"))
            G2 = TURN // GROUP
            r_total, r_mass = (
                Ring([sem(f"{n}{b}", part) for b in range(4)], G2) for n in ("v_total", "v_mass"))
            block = open_block(nc, part, used)

            @block.gpsimd
            def _(eng):
                with eng.Fori(0, TURNS) as i:
                    for half in range(2):
                        for n in range(U):
                            eng.wait_ge(s_v[half * U + n], i * 16 + v_from)
                        eng.tensor_copy(index[:, half, :], rec[:, bass.ds(i * TURN + half * U, U), 0]
                                        ).then_inc(s_index, 1)
                        eng.wait_ge(s_index, i * 2 + half + 1)
                        for n in range(U):
                            u = half * U + n
                            r_scaled.wait(eng, i, u - TURN)
                            eng.sem_inc(s_passed, 1)
                            eng.indirect_dma_start(v_sb[:, u, :], None, v,
                                                   bass.IndirectOffsetOnAxis(index[:, half, n:n + 1], 0)
                                                   ).then_inc(s_v[u], 16)

            @block.scalar
            def _(eng):
                r_away.start(eng)
                r_hot.start(eng)

                def distance(i, u):
                    r_hot.wait(eng, i, u - 4)
                    nc.scalar.activation(away[:, u % 4, :], iota_f[:, :], ACT.Abs, bias=low_neg[:, bass.ds(i * TURN + u, 1)]
                                         ).then_inc(r_away.sem(u), 1)

                distance(0, 0)
                with eng.Fori(0, TURNS) as i:
                    for u in range(TURN):
                        distance(i, u + 1)
                        r_away.wait(eng, i, u)
                        r_tile.wait(eng, i, u - 4)
                        nc.scalar.activation(hot[:, u % 4, :], away[:, u % 4, :], ACT.Relu, bias=1.0, scale=-1.0
                                             ).then_inc(r_hot.sem(u), 1)

            @block.vector
            def _(eng):
                r_scaled.start(eng)
                r_total.start(eng)
                r_mass.start(eng)
                st = Steps(eng, s_dve)
                st.link(nc.vector.memset(total[:, :, :], 0.0))
                st.link(nc.vector.memset(mass[:, :, :], 0.0))
                with eng.Fori(0, TURNS) as i:
                    def add(g):
                        at = eng.value_load(groups[0:1, bass.ds(i * G2 + g, 1)], min_val=0, max_val=BLOCKS - 1)
                        r_tile.wait(eng, i, (g + 1) * GROUP - 1)
                        for ring, to, of in ((r_mass, mass, mass_ps), (r_total, total, mix)):
                            ring.wait(eng, i, g - 1)
                            t = to[:, bass.ds(at, 1), :].rearrange("p a c -> p (a c)")
                            nc.vector.tensor_tensor(t, of[g % 4][:, :], t, ALU.add).then_inc(ring.sem(g), 1)

                    for u in range(TURN):
                        eng.wait_ge(s_v[u], i * 16 + (v_from + 16))
                        r_tile.wait(eng, i, u - 4)
                        nc.vector.tensor_tensor(
                            scaled[:, u % 4, :].rearrange("p (h d) -> p h d", d=D),
                            v_sb[:, u, :].rearrange("p (h d) -> p h d", d=D),
                            weight[:, bass.ds(i * TURN + u, 1), :].rearrange("p a h -> p (a h)").unsqueeze(2)
                            .broadcast_to([P, HEADS, D]), ALU.mult).then_inc(r_scaled.sem(u), 1)
                        if u % GROUP == GROUP - 1 and u > GROUP:
                            add(u // GROUP - 1)
                    add(G2 - 1)
                r_total.wait(eng, TURNS - 1, G2 - 1)
                r_mass.wait(eng, TURNS - 1, G2 - 1)
                st.link(nc.vector.tensor_scalar(mass[:, :, :], mass[:, :, :], 1e-30, None, ALU.max))
                st.link(nc.vector.reciprocal(mass[:, :, :], mass[:, :, :]))
                for n in range(4):
                    bl = slice(n * BLOCKS // 4, (n + 1) * BLOCKS // 4)
                    t = total[:, bl, :].rearrange("p b (h d) -> p (b h) d", d=D)
                    nc.vector.tensor_tensor(
                        t, t, mass[:, bl, :].rearrange("p b h -> p (b h)").unsqueeze(2)
                        .broadcast_to([P, BLOCKS // 4 * HEADS, D]), ALU.mult).then_inc(s_norm, 1)

            @block.tensor
            def _(eng):
                r_tile.start(eng)
                with eng.Fori(0, TURNS) as i:
                    for u in range(TURN):
                        g, first, last = u // GROUP, u % GROUP == 0, u % GROUP == GROUP - 1
                        r_hot.wait(eng, i, u)
                        if first:
                            r_mass.wait(eng, i, g - 4)
                            r_total.wait(eng, i, g - 4)
                        nc.tensor.matmul(mass_ps[g % 4][:, :], hot[:, u % 4, :],
                                         weight[:, bass.ds(i * TURN + u, 1), :].rearrange("p a h -> p (a h)"),
                                         start=first, stop=last)
                        r_scaled.wait(eng, i, u)
                        nc.tensor.matmul(mix[g % 4][:, :], hot[:, u % 4, :], scaled[:, u % 4, :],
                                         start=first, stop=last).then_inc(r_tile.sem(u), 1)

            @block.sync
            def _(eng):
                for n in range(4):
                    eng.wait_ge(s_norm, n + 1)
                    bl = slice(n * BLOCKS // 4, (n + 1) * BLOCKS // 4)
                    eng.dma_start(mixed.rearrange("(b p) c -> p b c", p=P)[:, bl, :], total[:, bl, :]).then_inc(s_out, 16)
                eng.wait_ge(s_out, 64)


def out_and_ffn(nc, mixed, z0, x, wo, bo, ln_g, ln_b, w1, b1, w2, b2, x3, z3):
    EPS = 1e-5
    KC = C // P
    M = 4
    TURNS = NODES // (M * P)
    HIDDEN = w1.shape[1]
    FC = HIDDEN // P
    with ExitStack() as ctx:
        def sb(name, shape, dt=F32):
            return ctx.enter_context(nc.sbuf_tensor("f_" + name, shape, dt))

        def ps(name, shape, dt=F32):
            return ctx.enter_context(nc.psum_tensor("f_" + name, shape, dt))

        used = []

        def sem(name):
            used.append(ctx.enter_context(nc.semaphore("fs_" + name)))
            return used[-1]

        def sems(n, *names):
            return [[sem(f"{name}{i}") for i in range(n)] for name in names]

        wo_sb, w1_sb, w2_sb = sb("wo", [P, KC, C]), sb("w1", [P, KC, HIDDEN]), sb("w2", [P, FC, C])
        bo_sb, b2_sb, gain, shift = sb("bo", [P, C]), sb("b2", [P, C]), sb("gain", [P, C]), sb("shift", [P, C])
        b1_sb = sb("b1", [P, FC])
        ones, ident, eps = sb("ones", [P, P]), sb("ident", [P, P]), sb("eps", [P, 1])
        mixt, z0t, xt = sb("mix", [P, M, C]), sb("z0", [P, M, C]), sb("x", [P, M, C])
        mixT = sb("mixT", [P, 2, C])
        x1 = sb("x1", [P, M, C])
        zn = sb("zn", [P, C])
        z = sb("z", [P, M, C])
        zT = sb("zT", [P, 2, KC, M * P])
        base = sb("base", [P, 2, M, C])
        hT = sb("hT", [P, FC, M * P])
        x3t, z3t = sb("x3", [P, M, C]), sb("z3", [P, M, C])
        stats, mean_var, root = sb("stats", [P, 2, 6]), sb("mv", [P, 2, 2]), sb("root", [P, 2])
        turned = [ps(f"turned{b}", [P, C]) for b in range(2)]
        o_ps = [ps(f"o{b}", [P, C]) for b in range(2)]
        up_ps = [ps(f"up{b}", [P, M * P]) for b in range(2)]
        down_ps = [ps(f"down{b}", [P, C]) for b in range(2)]

        s_w, s_b, s_c, s_cut, s_a, s_e, s_passed = (sem(n) for n in ("w", "b", "c", "cut", "a", "e", "passed"))
        s_var_a, s_root_a, s_var_e, s_root_e = (sem(n) for n in ("var_a", "root_a", "var_e", "root_e"))
        (s_mix, s_z0, s_x, s_res, s_mixturn, s_mixT, s_o, s_x1, s_z, s_zturn, s_zT, s_part, s_base, s_down, s_x3, s_z3,
         s_put_x3, s_put_z3) = sems(M, "mix", "z0", "x", "res", "mixturn", "mixT", "o", "x1", "z", "zturn", "zT", "part",
                                    "base", "down", "x3", "z3", "put_x3", "put_z3")
        s_up, s_h = sems(FC, "up", "h")
        block = open_block(nc, ctx, used)

        def rows(a, t, m):
            n = t * M + m
            v = a.rearrange("(n p) c -> n p c", p=P)
            return v[n, :, :] if isinstance(n, int) else v[bass.ds(n, 1), :, :].rearrange("a p c -> (a p) c")

        def turns(eng, begin, body, end):
            begin()
            with eng.Fori(0, (TURNS - 2) // 2) as j:
                for c in range(2):
                    body(j * 2 + c, c)
            body(TURNS - 2, 0)
            end(TURNS - 1, 1)

        @block.sync
        def _(eng):
            def load(t, m):
                eng.wait_ge(s_mixturn[m], t)
                eng.dma_start(mixt[:, m, :], rows(mixed, t, m)).then_inc(s_mix[m], 16)
                eng.wait_ge(s_x1[m], t)
                eng.dma_start(z0t[:, m, :], rows(z0, t, m)).then_inc(s_z0[m], 16)
                eng.wait_ge(s_part[m], t)
                eng.dma_start(xt[:, m, :], rows(x, t, m)).then_inc(s_x[m], 16)

            def store(t, m):
                eng.wait_ge(s_x3[m], t + 1)
                eng.dma_start(rows(x3, t, m), x3t[:, m, :]).then_inc(s_put_x3[m], 16)
                eng.wait_ge(s_z3[m], t + 1)
                eng.dma_start(rows(z3, t, m), z3t[:, m, :]).then_inc(s_put_z3[m], 16)

            def begin():
                for m in range(M):
                    load(0, m)
                eng.dma_start(wo_sb[:, :, :], wo.rearrange("(k p) n -> p k n", p=P)).then_inc(s_w, 16)
                for dst, a in ((bo_sb, bo), (b2_sb, b2), (gain, ln_g), (shift, ln_b)):
                    eng.dma_start(dst[:, :], a.partition_broadcast(P)).then_inc(s_b, 16)
                eng.dma_start(b1_sb[:, :], b1).then_inc(s_b, 16)
                eng.dma_start(w1_sb[:, :, :], w1.rearrange("(k p) n -> p k n", p=P)).then_inc(s_w, 16)
                eng.dma_start(w2_sb[:, :, :], w2.rearrange("(k p) n -> p k n", p=P)).then_inc(s_w, 16)
                for m in range(M):
                    load(1, m)

            def body(t, c):
                if not (isinstance(t, int) and t == TURNS - 2):
                    for m in range(M):
                        load(t + 2, m)
                for m in range(M):
                    store(t, m)

            def end(t, c):
                for m in range(M):
                    store(t, m)

            turns(eng, begin, body, end)
            for m in range(M):
                eng.wait_ge(s_put_x3[m], 16 * TURNS)
                eng.wait_ge(s_put_z3[m], 16 * TURNS)

        @block.gpsimd
        def _(eng):
            eng.memset(ones[:, :], 1.0).then_inc(s_c, 1)
            eng.memset(eps[:, :], EPS).then_inc(s_c, 1)
            eng.wait_ge(s_c, 2)
            eng.affine_select(out=ident[:, :], in_=ones[:, :], compare_op=ALU.is_equal, fill=0.0, base=0,
                              pattern=[[1, P]], channel_multiplier=-1).then_inc(s_cut, 1)
            eng.wait_ge(s_b, 80)

            def sums(t, c):
                for m in range(M):
                    eng.wait_ge(s_z0[m], t * 16 + 16)
                    eng.tensor_tensor(z0t[:, m, :], z0t[:, m, :], bo_sb[:, :], ALU.add).then_inc(s_res[m], 1)
                for m in range(M):
                    eng.wait_ge(s_x1[m], t + 1)
                    eng.wait_ge(s_x[m], t * 16 + 16)
                    eng.tensor_tensor(base[:, c, m, :], x1[:, m, :], xt[:, m, :], ALU.add).then_inc(s_part[m], 1)
                    eng.wait_ge(s_part[m], t + 1)
                    eng.tensor_tensor(base[:, c, m, :], base[:, c, m, :], b2_sb[:, :], ALU.add).then_inc(s_base[m], 1)

            turns(eng, lambda: sums(0, 0), lambda t, c: sums(t + 1, 1 - c), lambda t, c: None)

        @block.vector
        def _(eng):
            eng.wait_ge(s_b, 80)

            def attended(t, c):
                st = Steps(eng, s_a, t, 4 * M)
                for m in range(M):
                    eng.wait_ge(s_o[m], t + 1)
                    eng.wait_ge(s_res[m], t + 1)
                    eng.wait_ge(s_base[m], t)
                    nc.vector.tensor_tensor(x1[:, m, :], o_ps[m % 2][:, :], z0t[:, m, :], ALU.add).then_inc(s_x1[m], 1)
                    eng.wait_ge(s_x1[m], t + 1)
                    st.link(norm_scale(nc, eng, st, s_passed, s_var_a, s_root_a, t * M + m + 1, x1[:, m, :], stats[:, 0, :],
                                       mean_var[:, 0, :], root[:, 0:1], zn[:, :]))
                    st.link(nc.vector.tensor_tensor(zn[:, :], zn[:, :], gain[:, :], ALU.mult))
                    eng.wait_ge(s_zturn[m], t)
                    nc.vector.tensor_tensor(z[:, m, :], zn[:, :], shift[:, :], ALU.add).then_inc(s_z[m], 1)
                assert st.n == 4 * M

            def ended(t, c):
                st = Steps(eng, s_e, t, 2 * M)
                for m in range(M):
                    eng.wait_ge(s_down[m], t + 1)
                    eng.wait_ge(s_base[m], t + 1)
                    eng.wait_ge(s_put_x3[m], t * 16)
                    nc.vector.tensor_tensor(x3t[:, m, :], down_ps[m % 2][:, :], base[:, c, m, :], ALU.add).then_inc(s_x3[m], 1)
                    eng.wait_ge(s_x3[m], t + 1)
                    eng.wait_ge(s_put_z3[m], t * 16)
                    norm_scale(nc, eng, st, s_passed, s_var_e, s_root_e, t * M + m + 1, x3t[:, m, :], stats[:, 1, :],
                               mean_var[:, 1, :], root[:, 1:2], z3t[:, m, :]).then_inc(s_z3[m], 1)
                assert st.n == 2 * M

            turns(eng, lambda: attended(0, 0),
                  lambda t, c: (attended(t + 1, 1 - c), ended(t, c)), ended)

        @block.scalar
        def _(eng):
            eng.wait_ge(s_c, 2)
            eng.wait_ge(s_b, 80)

            def attended(t):
                def keep(m):
                    eng.wait_ge(s_mixturn[m], t + 1)
                    eng.wait_ge(s_o[(m + 2) % M], t + (m >= 2))
                    nc.scalar.copy(mixT[:, m % 2, :], turned[m % 2][:, :]).then_inc(s_mixT[m], 1)

                def root_of(m):
                    eng.wait_ge(s_var_a, t * M + m + 1)
                    nc.scalar.activation(root[:, 0:1], mean_var[:, 0, 1:2], ACT.Sqrt, bias=eps[:, :]).then_inc(s_root_a, 1)

                keep(0)
                for m in range(1, M):
                    keep(m)
                    root_of(m - 1)
                root_of(M - 1)

            def hidden(t):
                for f in range(FC):
                    eng.wait_ge(s_up[f], t + 1)
                    nc.scalar.activation(hT[:, f, :], up_ps[f % 2][:, :], ACT.Silu, bias=b1_sb[:, f:f + 1]).then_inc(s_h[f], 1)

            def columns(t, c):
                for m in range(M):
                    eng.wait_ge(s_zturn[m], t + 1)
                    nc.scalar.copy(zT[:, c, :, m * P:(m + 1) * P],
                                   turned[m % 2][:, :].rearrange("p (k r) -> p k r", r=P)).then_inc(s_zT[m], 1)

            def ended(t):
                for m in range(M):
                    eng.wait_ge(s_var_e, t * M + m + 1)
                    nc.scalar.activation(root[:, 1:2], mean_var[:, 1, 1:2], ACT.Sqrt, bias=eps[:, :]).then_inc(s_root_e, 1)

            turns(eng, lambda: (attended(0), columns(0, 0)),
                  lambda t, c: (attended(t + 1), hidden(t), columns(t + 1, 1 - c), ended(t)),
                  lambda t, c: (hidden(t), ended(t)))

        @block.tensor
        def _(eng):
            eng.wait_ge(s_cut, 1)

            def attended(t):
                def turn(m):
                    eng.wait_ge(s_mix[m], t * 16 + 16)
                    if m >= 2:
                        eng.wait_ge(s_mixT[m - 2], t + 1)
                    else:
                        eng.wait_ge(s_zT[m + 2], t)
                    for kc in range(KC):
                        last = nc.tensor.transpose(turned[m % 2][:, kc * P:(kc + 1) * P], mixt[:, m, kc * P:(kc + 1) * P],
                                                   ident[:, :])
                    last.then_inc(s_mixturn[m], 1)

                def product(m):
                    eng.wait_ge(s_mixT[m], t + 1)
                    eng.wait_ge(s_x1[(m + 2) % M], t + (m >= 2))
                    for kc in range(KC):
                        last = nc.tensor.matmul(o_ps[m % 2][:, :], mixT[:, m % 2, kc * P:(kc + 1) * P], wo_sb[:, kc, :],
                                                start=(kc == 0), stop=(kc == KC - 1))
                    last.then_inc(s_o[m], 1)

                turn(0)
                for m in range(1, M):
                    turn(m)
                    product(m - 1)
                product(M - 1)

            def up(t, c):
                for m in range(M):
                    eng.wait_ge(s_zT[m], t + 1)
                for f in range(FC):
                    eng.wait_ge(s_h[(f - 2) % FC], t + (f >= 2))
                    for kc in range(KC):
                        last = nc.tensor.matmul(up_ps[f % 2][:, :], w1_sb[:, kc, f * P:(f + 1) * P], zT[:, c, kc, :],
                                                start=(kc == 0), stop=(kc == KC - 1))
                    last.then_inc(s_up[f], 1)

            def turn_z(t):
                for m in range(M):
                    eng.wait_ge(s_z[m], t + 1)
                    if m >= 2:
                        eng.wait_ge(s_zT[m - 2], t + 1)
                    else:
                        eng.wait_ge(s_mixT[m + 2], t + 1)
                    for kc in range(KC):
                        last = nc.tensor.transpose(turned[m % 2][:, kc * P:(kc + 1) * P], z[:, m, kc * P:(kc + 1) * P],
                                                   ident[:, :])
                    last.then_inc(s_zturn[m], 1)

            def down(t):
                for f in range(FC):
                    eng.wait_ge(s_h[f], t + 1)
                for m in range(M):
                    eng.wait_ge(s_x3[(m + 2) % M], t + (m >= 2))
                    for f in range(FC):
                        last = nc.tensor.matmul(down_ps[m % 2][:, :], hT[:, f, m * P:(m + 1) * P], w2_sb[:, f, :],
                                                start=(f == 0), stop=(f == FC - 1))
                    last.then_inc(s_down[m], 1)

            def begin():
                eng.wait_ge(s_w, 48)
                attended(0)
                turn_z(0)

            turns(eng, begin, lambda t, c: (attended(t + 1), up(t, c), turn_z(t + 1), down(t)),
                  lambda t, c: (up(t, c), down(t)))


def experts(nc, x3, z3, router, w1, b1, w2, b2, gamma, beta, out):
    EPS = 1e-6
    KC = C // P
    M = 4
    TURNS = NODES // (M * P)
    E, _, F = w1.shape
    FC = F // P
    with ExitStack() as ctx:
        def sb(name, shape, dt=F32):
            return ctx.enter_context(nc.sbuf_tensor("m_" + name, shape, dt))

        def ps(name, shape, dt=F32):
            return ctx.enter_context(nc.psum_tensor("m_" + name, shape, dt))

        used = []

        def sem(name):
            used.append(ctx.enter_context(nc.semaphore("ms_" + name)))
            return used[-1]

        def sems(n, *names):
            return [[sem(f"{name}_{i}") for i in range(n)] for name in names]

        w1_sb, w2_sb = sb("w1", [P, E, KC, F]), sb("w2", [P, E, FC, C])
        gamma_sb, b2_sb = sb("gamma", [P, E, C]), sb("b2", [P, E, C])
        b1_sb, beta_sb, router_sb = sb("b1", [P, E, FC]), sb("beta", [E, C]), sb("router", [P, KC, E])
        ones, ident, eps, iota_e = sb("ones", [P, P]), sb("ident", [P, P]), sb("eps", [P, 1]), sb("iota_e", [P, E])
        z3t = sb("z3", [P, 2, M, C])
        acc = sb("acc", [P, 2, M, C])
        zT = sb("zT", [P, 2, KC, M * P])
        hT = sb("hT", [P, 2, FC, M * P])
        res = sb("res", [P, M, C])
        y = sb("y", [P, 2, M, C])
        logits = sb("logits", [P, M, E])
        top = sb("top", [P, M, 8])
        top_i = sb("top_i", [P, M, 8], mybir.dt.uint32)
        top_f = sb("top_f", [P, M, 2])
        below, ratio, g1, g2 = (sb(n, [P, M]) for n in ("below", "ratio", "g1", "g2"))
        pick = sb("pick", [P, 2, M, E])
        gate = sb("gate", [P, 2, M, E])
        gateT = sb("gateT", [E, M * P])
        stats, mean_var = sb("stats", [P, M, 6]), sb("mv", [P, M, 2])
        root = sb("root", [P, M])
        slope, offset = sb("slope", [P, 2, M]), sb("offset", [P, 2, M])
        turned = [ps(f"turned{b}", [P, C]) for b in range(2)]
        up_ps = [ps(f"up{b}", [P, M * P]) for b in range(2)]
        down_ps = [ps(f"down{m}", [P, C]) for m in range(M)]
        route_ps = turned[1][:, 0:M * E]

        s_w, s_c, s_cut, s_r, s_e, s_passed = (sem(n) for n in ("w", "c", "cut", "r", "e", "passed"))
        s_logits, s_low, s_ratio, s_gate, s_gateturn, s_gateT, s_var, s_root, s_line = (
            sem(n) for n in ("logits", "low", "ratio", "gate", "gateturn", "gateT", "var", "root", "line"))
        s_z, s_x, s_put = ([[sem(f"{n}{b}_{m}") for m in range(M)] for b in range(2)] for n in ("z", "x", "put"))
        s_turn, s_zT, s_beta, s_acc = sems(M, "turn", "zT", "beta", "acc")
        s_res, s_down, s_y, s_norm, s_gain, s_add = sems(M, "res", "down", "y", "norm", "gain", "add")
        s_up, s_h = sems(FC, "up", "h")
        block = open_block(nc, ctx, used)

        def rows(a, t, m):
            n = t * M + m
            v = a.rearrange("(n p) c -> n p c", p=P)
            return v[n, :, :] if isinstance(n, int) else v[bass.ds(n, 1), :, :].rearrange("a p c -> (a p) c")

        def turns(eng, begin, body):
            begin()
            with eng.Fori(0, TURNS // 2 - 1) as j:
                for c in range(2):
                    body(j * 2 + c, c, j, True)
            body(TURNS - 2, 0, TURNS // 2 - 1, True)
            body(TURNS - 1, 1, TURNS // 2 - 1, False)

        @block.sync
        def _(eng):
            def load(t, b, k):
                for m in range(M):
                    eng.wait_ge(s_put[b][m], k * 16)
                    eng.dma_start(z3t[:, b, m, :], rows(z3, t, m)).then_inc(s_z[b][m], 16)
                    eng.dma_start(acc[:, b, m, :], rows(x3, t, m)).then_inc(s_x[b][m], 16)

            def begin():
                load(0, 0, 0)
                eng.dma_start(router_sb[:, :, :], router.rearrange("(k p) e -> p k e", p=P)).then_inc(s_c, 16)
                eng.dma_start(beta_sb[:, :], beta).then_inc(s_c, 16)
                eng.dma_start(b1_sb[:, :, :], b1).then_inc(s_c, 16)
                eng.dma_start(w1_sb[:, :, :, :], w1.rearrange("e (k p) f -> p e k f", p=P)).then_inc(s_w, 16)
                eng.dma_start(b2_sb[:, :, :].rearrange("p e c -> p (e c)"),
                              b2.rearrange("e c -> (e c)").partition_broadcast(P)).then_inc(s_w, 16)
                eng.dma_start(w2_sb[:, :, :, :], w2.rearrange("e (k p) c -> p e k c", p=P)).then_inc(s_w, 16)
                eng.dma_start(gamma_sb[:, :, :].rearrange("p e c -> p (e c)"),
                              gamma.rearrange("e c -> (e c)").partition_broadcast(P)).then_inc(s_w, 16)

            def body(t, b, k, more):
                if more:
                    load(t + 1, 1 - b, k + b)
                for m in range(M):
                    eng.wait_ge(s_acc[m], t + 1)
                    eng.dma_start(rows(out, t, m), acc[:, b, m, :]).then_inc(s_put[b][m], 16)

            turns(eng, begin, body)
            for b in range(2):
                for m in range(M):
                    eng.wait_ge(s_put[b][m], 16 * (TURNS // 2))

        @block.gpsimd
        def _(eng):
            eng.memset(ones[:, :], 1.0).then_inc(s_cut, 1)
            eng.memset(eps[:, :], EPS).then_inc(s_cut, 1)
            eng.iota(iota_e[:, :], pattern=[[1, E]], base=0, channel_multiplier=0,
                     allow_small_or_imprecise_dtypes=True).then_inc(s_cut, 1)
            eng.wait_ge(s_cut, 3)
            eng.affine_select(out=ident[:, :], in_=ones[:, :], compare_op=ALU.is_equal, fill=0.0, base=0,
                              pattern=[[1, P]], channel_multiplier=-1).then_inc(s_cut, 1)
            eng.wait_ge(s_w, 64)

            def residual(t, b, k, e):
                for m in range(M):
                    if e == 0:
                        eng.wait_ge(s_z[b][m], k * 16 + 16)
                    eng.wait_ge(s_y[m], t * E + e)
                    eng.tensor_tensor(res[:, m, :], z3t[:, b, m, :], b2_sb[:, e, :], ALU.add).then_inc(s_res[m], 1)

            def body(t, b, k, more):
                for e in range(E):
                    if e < E - 1:
                        residual(t, b, k, e + 1)
                    elif more:
                        residual(t + 1, 1 - b, k + b, 0)
                    for m in range(M):
                        eng.wait_ge(s_norm[m], t * E + e + 1)
                        eng.tensor_tensor(y[:, e % 2, m, :], y[:, e % 2, m, :], gamma_sb[:, e, :], ALU.mult
                                          ).then_inc(s_gain[m], 1)

            turns(eng, lambda: residual(0, 0, 0, 0), body)

        @block.vector
        def _(eng):
            def route(t, b, k):
                st = Steps(eng, s_r, t, 2 * M + 9)
                eng.wait_ge(s_logits, t + 1)
                st.link(nc.vector.tensor_copy(logits[:, :, :], route_ps.rearrange("p (m e) -> p m e", e=E)))
                for m in range(M):
                    eng.sem_inc(s_passed, 1)
                    st.link(nc.vector.max(top[:, m, :], logits[:, m, :]))
                    eng.sem_inc(s_passed, 1)
                    st.link(nc.vector.max_index(top_i[:, m, :], top[:, m, :], logits[:, m, :]))
                st.link(nc.vector.tensor_copy(top_f[:, :, :], top_i[:, :, 0:2]))
                nc.vector.tensor_tensor(below[:, :], top[:, :, 1], top[:, :, 0], ALU.subtract).then_inc(s_low, 1)
                eng.wait_ge(s_ratio, t + 1)
                st.link(nc.vector.tensor_scalar(g1[:, :], ratio[:, :], 1.0, None, ALU.add))
                st.link(nc.vector.reciprocal(g1[:, :], g1[:, :]))
                st.link(nc.vector.tensor_tensor(g2[:, :], g1[:, :], ratio[:, :], ALU.mult))
                for n, g in ((0, g1), (1, g2)):
                    st.link(nc.vector.tensor_tensor(pick[:, n, :, :], iota_e[:, :].unsqueeze(1).broadcast_to([P, M, E]),
                                                    top_f[:, :, n:n + 1].broadcast_to([P, M, E]), ALU.is_equal))
                    st.link(nc.vector.tensor_tensor(pick[:, n, :, :], pick[:, n, :, :],
                                                    g[:, :].unsqueeze(2).broadcast_to([P, M, E]), ALU.mult))
                nc.vector.tensor_tensor(gate[:, b, :, :], pick[:, 0, :, :], pick[:, 1, :, :], ALU.add).then_inc(s_gate, 1)
                assert st.n == 2 * M + 9

            def start_sum(t, b, k):
                for m in range(M):
                    eng.wait_ge(s_beta[m], t + 1)
                    eng.wait_ge(s_x[b][m], k * 16 + 16)
                    nc.vector.tensor_tensor(acc[:, b, m, :], down_ps[m][:, :], acc[:, b, m, :], ALU.add
                                            ).then_inc(s_add[m], 1)

            def body(t, b, k, more):
                def norm(e):
                    st = Steps(eng, s_e, t * E + e, M + 2)
                    n = t * E + e
                    for m in range(M):
                        eng.wait_ge(s_down[m], n + 1)
                        eng.wait_ge(s_res[m], n + 1)
                        if e == 1:
                            eng.wait_ge(s_acc[m], t)
                        else:
                            eng.wait_ge(s_add[m], n)
                        nc.vector.tensor_tensor(y[:, e % 2, m, :], down_ps[m][:, :], res[:, m, :], ALU.add
                                                ).then_inc(s_y[m], 1)
                        eng.wait_ge(s_y[m], n + 1)
                        st.link(nc.vector.bn_stats(stats[:, m, :], y[:, e % 2, m, :]))
                        eng.sem_inc(s_passed, 1)
                        last = nc.vector.bn_aggr(mean_var[:, m, :], stats[:, m, :])
                    last.then_inc(s_var, 1)
                    eng.wait_ge(s_root, n + 1)
                    st.link(nc.vector.reciprocal(root[:, :], root[:, :]))
                    st.link(nc.vector.tensor_tensor(slope[:, e % 2, :], root[:, :], gate[:, b, :, e], ALU.mult))
                    nc.vector.scalar_tensor_tensor(offset[:, e % 2, :], mean_var[:, :, 0], -1.0, slope[:, e % 2, :],
                                                   ALU.mult, ALU.mult).then_inc(s_line, 1)
                    assert st.n == M + 2

                def add(e):
                    n = t * E + e
                    for m in range(M):
                        eng.wait_ge(s_gain[m], n + 1)
                        eng.wait_ge(s_add[m], t * E + e + 1)
                        last = nc.vector.tensor_tensor(acc[:, b, m, :], acc[:, b, m, :], y[:, e % 2, m, :], ALU.add)
                        last.then_inc(s_add[m], 1) if e < E - 1 else last.then_inc(s_acc[m], 1)

                norm(0)
                for e in range(1, E):
                    norm(e)
                    add(e - 1)
                    if e == E // 2 and more:
                        route(t + 1, 1 - b, k + b)
                if more:
                    start_sum(t + 1, 1 - b, k + b)
                add(E - 1)

            eng.wait_ge(s_cut, 3)
            turns(eng, lambda: (route(0, 0, 0), start_sum(0, 0, 0)), body)

        @block.scalar
        def _(eng):
            eng.wait_ge(s_cut, 3)
            eng.wait_ge(s_c, 48)

            def columns(t, b, tiles):
                for m in tiles:
                    eng.wait_ge(s_turn[m], t + 1)
                    nc.scalar.copy(zT[:, b, :, m * P:(m + 1) * P],
                                   turned[m % 2][:, :].rearrange("p (k r) -> p k r", r=P)).then_inc(s_zT[m], 1)

            def second_gate(t):
                eng.wait_ge(s_low, t + 1)
                nc.scalar.activation(ratio[:, :], below[:, :], ACT.Exp).then_inc(s_ratio, 1)

            def gate_columns(t):
                eng.wait_ge(s_gateturn, t + 1)
                nc.scalar.copy(gateT[:, :], turned[0][0:E, :]).then_inc(s_gateT, 1)

            def hidden(t, e):
                for f in range(FC):
                    eng.wait_ge(s_up[f], t * E + e + 1)
                    nc.scalar.activation(hT[:, e % 2, f, :], up_ps[f][:, :], ACT.Relu, bias=b1_sb[:, e, f:f + 1]
                                         ).then_inc(s_h[f], 1)

            def norm(t, e):
                n = t * E + e
                eng.wait_ge(s_var, n + 1)
                nc.scalar.activation(root[:, :], mean_var[:, :, 1], ACT.Sqrt, bias=eps[:, :]).then_inc(s_root, 1)
                eng.wait_ge(s_line, n + 1)
                for m in range(M):
                    nc.scalar.activation(y[:, e % 2, m, :], y[:, e % 2, m, :], ACT.Identity,
                                         bias=offset[:, e % 2, m:m + 1], scale=slope[:, e % 2, m:m + 1]
                                         ).then_inc(s_norm[m], 1)

            def body(t, b, k, more):
                for e in range(E):
                    if e < E - 1:
                        hidden(t, e + 1)
                    elif more:
                        hidden(t + 1, 0)
                    if e == E // 2 - 1 and more:
                        columns(t + 1, 1 - b, (0, 1))
                        norm(t, e)
                        columns(t + 1, 1 - b, (2, 3))
                    else:
                        norm(t, e)
                    if e == E // 2 and more:
                        second_gate(t + 1)
                    if e == E // 2 + 1 and more:
                        gate_columns(t + 1)

            turns(eng, lambda: (columns(0, 0, range(M)), second_gate(0), gate_columns(0), hidden(0, 0)), body)

        @block.tensor
        def _(eng):
            eng.wait_ge(s_cut, 4)
            eng.wait_ge(s_c, 48)

            def turn(t, b, k, tiles):
                for m in tiles:
                    eng.wait_ge(s_z[b][m], k * 16 + 16)
                    if m >= 2:
                        eng.wait_ge(s_zT[m - 2], t + 1)
                    else:
                        eng.wait_ge(s_zT[m + 2], t)
                    if m == 0:
                        eng.wait_ge(s_gateT, t)
                    for kc in range(KC):
                        last = nc.tensor.transpose(turned[m % 2][:, kc * P:(kc + 1) * P],
                                                   z3t[:, b, m, kc * P:(kc + 1) * P], ident[:, :])
                    last.then_inc(s_turn[m], 1)

            def route(t, b):
                eng.wait_ge(s_zT[M - 1], t + 1)
                for m in range(M):
                    for kc in range(KC):
                        last = nc.tensor.matmul(route_ps[:, m * E:(m + 1) * E], zT[:, b, kc, m * P:(m + 1) * P],
                                                router_sb[:, kc, :], start=(kc == 0), stop=(kc == KC - 1))
                last.then_inc(s_logits, 1)

            def turn_gates(t, b):
                eng.wait_ge(s_gate, t + 1)
                for m in range(M):
                    last = nc.tensor.transpose(turned[0][0:E, m * P:(m + 1) * P], gate[:, b, m, :], ident[:, :])
                last.then_inc(s_gateturn, 1)

            def start_sum(t):
                eng.wait_ge(s_gateT, t + 1)
                eng.wait_ge(s_y[M - 1], t * E)
                for m in range(M):
                    nc.tensor.matmul(down_ps[m][:, :], gateT[:, m * P:(m + 1) * P], beta_sb[:, :],
                                     start=True, stop=True).then_inc(s_beta[m], 1)

            def up(t, b, e):
                eng.wait_ge(s_h[FC - 1], t * E + e)
                for f in range(FC):
                    for kc in range(KC):
                        last = nc.tensor.matmul(up_ps[f][:, :], w1_sb[:, e, kc, f * P:(f + 1) * P], zT[:, b, kc, :],
                                                start=(kc == 0), stop=(kc == KC - 1))
                    last.then_inc(s_up[f], 1)

            def down(t, e):
                n = t * E + e
                eng.wait_ge(s_h[FC - 1], n + 1)
                if e == 0:
                    eng.wait_ge(s_add[M - 1], n + 1)
                else:
                    eng.wait_ge(s_y[M - 1], n)
                for m in range(M):
                    for f in range(FC):
                        last = nc.tensor.matmul(down_ps[m][:, :], hT[:, e % 2, f, m * P:(m + 1) * P],
                                                w2_sb[:, e, f, :], start=(f == 0), stop=(f == FC - 1))
                    last.then_inc(s_down[m], 1)

            def body(t, b, k, more):
                for e in range(E):
                    if e < E - 1:
                        up(t, b, e + 1)
                    elif more:
                        up(t + 1, 1 - b, 0)
                    if e == E // 2 - 1 and more:
                        turn(t + 1, 1 - b, k + b, (0, 1))
                        down(t, e)
                        turn(t + 1, 1 - b, k + b, (2, 3))
                    else:
                        down(t, e)
                    if e == E // 2 and more:
                        route(t + 1, 1 - b)
                    if e == E // 2 + 1 and more:
                        turn_gates(t + 1, 1 - b)
                if more:
                    start_sum(t + 1)

            def begin():
                turn(0, 0, 0, range(M))
                route(0, 0)
                turn_gates(0, 0)
                start_sum(0)
                eng.wait_ge(s_w, 64)
                up(0, 0, 0)

            turns(eng, begin, body)


def graph_layer(nc, a, out):

    def scratch(name, shape, dt=F32):
        return nc.dram_tensor(name, shape, dt, kind="Internal").ap()

    with ExitStack() as ctx:
        moved = [ctx.enter_context(nc.semaphore(f"moved{n}")) for n in range(MOVES)]
        stages(nc, a, out, moved, scratch)


def stages(nc, a, out, moved, scratch):
    records = scratch("records", (P * TILES, REC))
    group_block = scratch("group_block", (-(-GROUPS // P) * P,), I32)
    z0, q, k, v, mixed, x3, z3 = (scratch(f"t_{n}", (NODES, C)) for n in ("z0", "q", "k", "v", "mixed", "x3", "z3"))
    project_qkv(nc, a["x"], a["L0_gnn_ln1_g"], a["L0_gnn_ln1_b"], a["L0_gnn_Wq"], a["L0_gnn_bq"], a["L0_gnn_Wk"],
                a["L0_gnn_bk"], a["L0_gnn_Wv"], a["L0_gnn_bv"], z0, q, k, v)
    sort_edges(nc, moved, a["src_t"], a["src"], a["dst_t"], a["bias_t"], records, group_block)
    attention(nc, moved, 16 * (EDGES // P) // MOVES, records, group_block, q, k, v, mixed)
    out_and_ffn(nc, mixed, z0, a["x"], a["L0_gnn_Wo"], a["L0_gnn_bo"], a["L0_gnn_ln2_g"], a["L0_gnn_ln2_b"],
                a["L0_gnn_W1"], a["b1_t"], a["L0_gnn_W2"], a["L0_gnn_b2"], x3, z3)
    experts(nc, x3, z3, a["L0_ffn_router_w"], a["L0_ffn_w1"], a["moe_b1_t"], a["L0_ffn_w2"], a["L0_ffn_b2"],
            a["L0_ffn_gamma"], a["L0_ffn_beta"], out)


_PLAIN = ["x", "src", "L0_gnn_Wq", "L0_gnn_bq", "L0_gnn_Wk", "L0_gnn_bk", "L0_gnn_Wv", "L0_gnn_bv", "L0_gnn_Wo",
          "L0_gnn_bo", "L0_gnn_ln1_g", "L0_gnn_ln1_b", "L0_gnn_ln2_g", "L0_gnn_ln2_b", "L0_gnn_W1", "L0_gnn_W2",
          "L0_gnn_b2", "L0_ffn_router_w", "L0_ffn_w1", "L0_ffn_w2", "L0_ffn_b2", "L0_ffn_gamma", "L0_ffn_beta"]


def kernel(**inputs):
    import numpy as _np
    import concourse.bacc as _bacc
    from concourse import mybir as _mybir
    from concourse.bass_utils import run_bass_kernel_spmd as _run

    given = {name: _np.asarray(inputs[name]) for name in inputs}
    laid = {name: given[name] for name in _PLAIN}
    laid["src_t"] = given["src"].reshape(IN_TILES, P).T
    laid["dst_t"] = given["dst"].reshape(IN_TILES, P).T
    laid["bias_t"] = given["edge_attr_8"].reshape(IN_TILES, P, HEADS).transpose(1, 0, 2).reshape(P, IN_TILES * HEADS)
    laid["b1_t"] = given["L0_gnn_b1"].reshape(-1, P).T
    laid["moe_b1_t"] = given["L0_ffn_b1"].reshape(given["L0_ffn_b1"].shape[0], -1, P).transpose(2, 0, 1)

    nc = _bacc.Bacc("TRN2", target_bir_lowering=False, num_devices=1)
    arrays, args = {}, {}
    for name, a in laid.items():
        arrays[f"in_{name}"] = _np.ascontiguousarray(a)
        args[name] = nc.dram_tensor(f"in_{name}", a.shape, _mybir.dt.from_np(a.dtype), kind="ExternalInput").ap()
    out = nc.dram_tensor("out", (NODES, C), F32, kind="ExternalOutput").ap()
    graph_layer(nc, args, out)
    r = _run(nc, [arrays], core_ids=[0])
    return r.results[0]["out"]
```

```python
import concourse.bass as bass
import concourse.mybir as mybir
from contextlib import ExitStack

F32, BF16, I32 = mybir.dt.float32, mybir.dt.bfloat16, mybir.dt.int32
F32R = mybir.dt.float32r
ALU = mybir.AluOpType
ACT = mybir.ActivationFunctionType
AX = mybir.AxisListType

P = 128
NODES, C, HEADS = 4096, 512, 8
D = C // HEADS
EDGES = 69632
BLOCKS = NODES // P
IN_TILES = EDGES // P
GROUP = 2
SPAN = GROUP * P
GROUPS = -(-EDGES // SPAN) + BLOCKS
TILES = GROUPS * GROUP
RANGES = 16
RANGE_TILES = TILES // RANGES
REC = 2 + HEADS
PAD_ROW = -1.0


class Steps:

    def __init__(self, eng, sem, turn=None, per=0, base=0):
        self.eng, self.sem, self.turn, self.per, self.base, self.n = eng, sem, turn, per, base, 0

    def value(self):
        n = self.base + self.n
        return n if self.turn is None else self.turn * self.per + n

    def link(self, ins):
        self.n += 1
        ins.then_inc(self.sem, 1)
        self.eng.wait_ge(self.sem, self.value())


class Ring:

    def __init__(self, sems, tiles, unit=1):
        self.sems, self.n, self.per, self.unit = sems, len(sems), tiles // len(sems), unit

    def start(self, eng):
        for s in self.sems:
            eng.sem_inc(s, self.per * self.unit)

    def sem(self, u):
        return self.sems[u % self.n]

    def value(self, i, u):
        return i * (self.per * self.unit) + (self.per + u // self.n + 1) * self.unit

    def wait(self, eng, i, u):
        eng.wait_ge(self.sem(u), self.value(i, u))


MOVES = 32


def open_block(nc, ctx, used):
    def clear():
        for s in used:
            nc.gpsimd.sem_clear(s)
        nc.all_engine_barrier()

    ctx.callback(clear)
    return ctx.enter_context(nc.Block())


def norm_scale(nc, eng, st, passed, s_var, s_root, value, x, stats, mean_var, root, out):
    st.link(nc.vector.bn_stats(stats, x))
    eng.sem_inc(passed, 1)
    nc.vector.bn_aggr(mean_var, stats).then_inc(s_var, 1)
    eng.wait_ge(s_root, value)
    st.link(nc.vector.reciprocal(root, root))
    return nc.vector.tensor_scalar(out, x, mean_var[:, 0:1], root, ALU.subtract, ALU.mult)


def sort_and_project(nc, moved, src_t, src_row, dst_t, bias_t, low_row, records, group_block,
                     x, ln_g, ln_b, wq, bq, wk, bk, wv, bv, z0, q, k, v):
    EPS = 1e-5
    KC = C // P
    B = 16
    TURNS = IN_TILES // (2 * B)
    ROW_TURNS = NODES // P // 2
    assert ROW_TURNS < TURNS
    ACT_TILES = 4
    DVE_TILES = B - ACT_TILES
    ACT_BLOCKS = 14
    GC = -(-GROUPS // P)
    PIECE = TILES // MOVES
    with ExitStack() as ctx:
        def sb(name, shape, dt=F32):
            return ctx.enter_context(nc.sbuf_tensor(name, shape, dt))

        def ps(name, shape, dt=F32):
            return ctx.enter_context(nc.psum_tensor(name, shape, dt))

        used = []

        def sem(name):
            used.append(ctx.enter_context(nc.semaphore(name)))
            return used[-1]

        def ring(name, unit=1):
            return Ring([sem(f"{name}{b}") for b in range(2)], 2, unit)

        row_i = sb("row_i", [P, IN_TILES], I32)
        col_i = sb("col_i", [P, IN_TILES], I32)
        row_f = sb("row_f", [P, IN_TILES])
        part_i = sb("part_i", [P, IN_TILES], I32)
        blk_b = sb("blk_b", [P, IN_TILES], BF16)
        low_b = sb("low_b", [P, IN_TILES], BF16)
        away = sb("away_all", [P, 2, ACT_TILES, P], BF16)
        iota_b = sb("iota_b", [P, P], BF16)
        iota_p = sb("iota_p", [P, 1])
        earlier = sb("earlier", [P, P])
        earlier_b = sb("earlier_b", [P, P], BF16)
        ones_f = sb("ones_f", [P, P])
        ones_b = sb("ones_b", [P, 1], BF16)
        zeros_f = sb("zeros_f", [P, IN_TILES])
        counts = sb("counts", [P, BLOCKS, IN_TILES + 1])
        start = sb("start", [P, BLOCKS])
        total = sb("total", [P, BLOCKS])
        fill_i = sb("fill_i", [P, BLOCKS], I32)
        fill_s = sb("fill_s", [P, BLOCKS], I32)
        fill_f = sb("fill_f", [P, BLOCKS])
        ends = sb("ends", [P, BLOCKS])
        group_at = sb("group_at", [P, GC])
        passed = sb("passed", [P, GC, BLOCKS])
        group_f = sb("group_f", [P, GC])
        group_i = sb("group_i", [P, GC], I32)
        hots = sb("hots", [P, 2, B, P], BF16)
        blk_hot = sb("blk_hot", [P, 2, B, BLOCKS], BF16)
        row_bc = sb("row_bc", [P, 2, B * P], I32)
        low_bc = sb("low_bc", [P, 2, B * P], BF16)
        low_x = sb("low_x", [P, IN_TILES], BF16)
        low_hot_t = sb("low_hot_t", [P, 2, B * P])
        picked = sb("picked", [P, B, BLOCKS])
        before = sb("before", [P, B])
        place = sb("place", [P, B], I32)
        tile_of = sb("tile_of", [P, B], I32)
        part_of = sb("part_of", [P, B], I32)
        address = sb("address", [P, 2, B], I32)
        bias_sb = sb("bias_sb", [P, 2, B * HEADS])
        staged = sb("staged", [P, 2, B, REC])
        blank = sb("blank", [P, PIECE, REC])
        ranks = [ps(f"ranks{b}", [P, B * BLOCKS]) for b in range(2)]
        within = [ps(f"within{b}", [P, B]) for b in range(2)]

        w = sb("qkv_w", [P, 3, KC, C])
        bias = sb("qkv_bias", [P, 3, C])
        gain, shift = sb("qkv_gain", [P, C]), sb("qkv_shift", [P, C])
        ident = sb("qkv_ident", [P, P])
        eps = sb("qkv_eps", [P, 1])
        xt = sb("qkv_x", [P, 2, C])
        z0t = sb("qkv_z0", [P, 2, C])
        zn = sb("qkv_zn", [P, C])
        zt = sb("qkv_z", [P, 2, C])
        zT = sb("qkv_zT", [P, 2, C])
        out = sb("qkv_out", [P, 2, 3, C])
        stats, mean_var, root = sb("qkv_stats", [P, 6]), sb("qkv_mv", [P, 2]), sb("qkv_root", [P, 1])
        turned = ps("qkv_turned", [P, C])
        small = turned[:, 0:2 * BLOCKS]
        prod = [ps(f"qkv_prod{n}", [P, C]) for n in range(3)]

        s_rows, s_cols, s_blank, s_group, s_const, s_cut, s_dve, s_pass2, s_parts = (
            sem(f"s_{n}") for n in ("rows", "cols", "blank", "group", "const", "cut", "dve", "pass2", "parts"))
        s_total, s_small, s_start, s_groups, s_waited = (
            sem(f"s_{n}") for n in ("total", "small", "start", "groups", "waited"))
        s_away, s_begun, r_act_hot = sem("s_away"), sem("s_begun"), ring("s_act_hot")
        r_hot, r_hist, r_kept = ring("s_hot"), ring("s_hist"), ring("s_kept")
        s_linear, s_low_x, s_low_row = (sem(f"s_{n}") for n in ("linear", "low_x", "low_row"))
        s_low_bc = [sem(f"s_low_bc{b}") for b in range(2)]
        s_bc, s_bias = [sem(f"s_bc{b}") for b in range(2)], [sem(f"s_bias{b}") for b in range(2)]
        r_same, r_low, r_ranks, r_addr, r_staged = (ring(f"s_{n}") for n in ("same", "low", "ranks", "addr", "staged"))
        put = [moved[b * B:(b + 1) * B] for b in range(2)]

        s_w, s_b, s_norm, s_bn, s_var, s_root = (sem(f"q_{n}") for n in ("w", "b", "norm", "bn", "var", "root"))
        s_x = [sem(f"q_x{b}") for b in range(2)]
        r_z0, r_z, r_turn, r_zT = (ring(f"q_{n}") for n in ("z0", "z", "turn", "zT"))
        r_stored_z0 = ring("q_stored_z0", 16)
        r_prod, r_out = ([ring(f"q_{n}{m}_") for m in range(3)] for n in ("prod", "out"))
        r_stored = [ring(f"q_stored{m}_", 16) for m in range(3)]
        block = open_block(nc, ctx, used)

        def batch(i, b):
            return bass.ds(i * 2 * B + b * B, B)

        def tile_rows(a, j, c):
            return a.rearrange("(n p) c -> n p c", p=P)[bass.ds(j * 2 + c, 1), :, :].rearrange("a p c -> (a p) c")

        @block.sync
        def _(eng):
            for r in (r_stored_z0, *r_stored):
                r.start(eng)
            eng.dma_start(row_i[:, :], src_t).then_inc(s_rows, 16)
            eng.dma_start(col_i[:, :], dst_t).then_inc(s_cols, 16)
            for c in range(2):
                eng.dma_start(xt[:, c, :], x[c * P:(c + 1) * P, :]).then_inc(s_x[c], 16)
            for n, a in enumerate((bq, bk, bv)):
                eng.dma_start(bias[:, n, :], a.partition_broadcast(P)).then_inc(s_b, 16)
            for dst, a in ((gain, ln_g), (shift, ln_b)):
                eng.dma_start(dst[:, :], a.partition_broadcast(P)).then_inc(s_b, 16)
            for n, a in enumerate((wq, wk, wv)):
                eng.dma_start(w[:, n, :, :], a.rearrange("(k p) n -> p k n", p=P)).then_inc(s_w, 16)
            eng.wait_ge(s_parts, 2)
            eng.dma_start(row_i[:, :], src_row.rearrange("(p n) -> p n", p=P)).then_inc(s_linear, 16)
            eng.wait_ge(s_low_x, 1)
            eng.dma_start(low_row.rearrange("(p n) -> p n", p=P), low_x[:, :]).then_inc(s_low_row, 16)
            eng.wait_ge(s_low_row, 16)
            rows, lows = (a.rearrange("(n w) -> n w", w=B * P) for a in (src_row, low_row))

            def load_rows(i, b):
                r_low.wait(eng, i, b - 2)
                for dst, a, done in ((row_bc, rows, s_bc), (low_bc, lows, s_low_bc)):
                    eng.dma_start(dst[:, b % 2, :],
                                  a[bass.ds(i * 2 + b, 1), :].rearrange("a w -> (a w)").partition_broadcast(P)
                                  ).then_inc(done[b % 2], 16)

            def load_bias(i, b):
                r_staged.wait(eng, i, b - 2)
                eng.dma_start(bias_sb[:, b, :], bias_t[:, bass.ds((i * 2 + b) * B * HEADS, B * HEADS)]
                              ).then_inc(s_bias[b], 16)

            def load_x(j, c):
                r_z0.wait(eng, j, c - 2)
                eng.dma_start(xt[:, c % 2, :], tile_rows(x, j, c)).then_inc(s_x[c % 2], 16)

            def store(j, c):
                r_z0.wait(eng, j, c)
                eng.dma_start(tile_rows(z0, j, c), z0t[:, c, :]).then_inc(r_stored_z0.sem(c), 16)
                for n, a in enumerate((q, k, v)):
                    r_out[n].wait(eng, j, c)
                    eng.dma_start(tile_rows(a, j, c), out[:, c, n, :]).then_inc(r_stored[n].sem(c), 16)

            for b in range(2):
                load_rows(0, b)
                load_bias(0, b)
            load_rows(0, 2)
            with eng.Fori(0, ROW_TURNS - 1) as j:
                for c in range(2):
                    load_rows(j, c + 3)
                    load_bias(j + 1, c)
                    load_x(j, c + 2)
                    store(j, c)
            load_rows(ROW_TURNS - 1, 3)
            for b in range(2):
                load_bias(ROW_TURNS, b)
                store(ROW_TURNS - 1, b)
            eng.wait_ge(s_groups, 1)
            eng.dma_start(group_block.rearrange("(c p) -> p c", p=P), group_i[:, :],
                          allow_slow_non_contiguous=True).then_inc(s_group, 16)
            eng.wait_ge(s_group, 16)
            for r in (r_stored_z0, *r_stored):
                for c in range(2):
                    r.wait(eng, ROW_TURNS - 1, c)

        @block.gpsimd
        def _(eng):
            eng.memset(blank[:, :, :], 0.0).then_inc(s_blank, 1)
            eng.wait_ge(s_blank, 1)
            eng.memset(blank[:, :, 1:2], PAD_ROW).then_inc(s_blank, 1)
            eng.iota(iota_b[:, :], pattern=[[1, P]], base=0, channel_multiplier=0,
                     allow_small_or_imprecise_dtypes=True).then_inc(s_const, 1)
            eng.iota(iota_p[:, :], pattern=[[1, 1]], base=0, channel_multiplier=1,
                     allow_small_or_imprecise_dtypes=True).then_inc(s_const, 1)
            eng.iota(group_at[:, :], pattern=[[P, GC]], base=0, channel_multiplier=1,
                     allow_small_or_imprecise_dtypes=True).then_inc(s_const, 1)
            eng.memset(ones_f[:, :], 1.0).then_inc(s_const, 1)
            eng.memset(ones_b[:, :], 1.0).then_inc(s_const, 1)
            eng.memset(zeros_f[:, :], 0.0).then_inc(s_const, 1)
            eng.memset(eps[:, :], EPS).then_inc(s_const, 1)
            eng.wait_ge(s_const, 7)
            for m, op in ((earlier, ALU.is_gt), (earlier_b, ALU.is_gt), (ident, ALU.is_equal)):
                eng.affine_select(out=m[:, :], in_=ones_f[:, :], compare_op=op, fill=0.0, base=0,
                                  pattern=[[1, P]], channel_multiplier=-1).then_inc(s_cut, 1)
            eng.wait_ge(s_blank, 2)
            pieces = records.rearrange("(p m t) w -> p m (t w)", p=P, m=MOVES)
            for n in range(MOVES):
                eng.dma_start(pieces[:, n, :], blank[:, :, :].rearrange("p t w -> p (t w)")).then_inc(moved[n], 16)
            for n in range(MOVES):
                eng.wait_ge(moved[n], 16)
            with eng.Fori(0, TURNS) as i:
                for b in range(2):
                    r_addr.wait(eng, i, b)
                    r_staged.wait(eng, i, b)
                    eng.sem_inc(s_waited, 1)
                    for u in range(B):
                        eng.indirect_dma_start(
                            records, bass.IndirectOffsetOnAxis(address[:, b, u:u + 1], 0), staged[:, b, u, :], None,
                        ).then_inc(put[b][u], 16)
            for n in range(MOVES):
                eng.wait_ge(moved[n], 16 * (TURNS + 1))

        @block.scalar
        def _(eng):
            for r in (r_kept, r_act_hot, r_staged, r_zT):
                r.start(eng)
            eng.wait_ge(s_const, 7)
            eng.wait_ge(s_parts, 1)

            def one_hots(i, b):
                r_act_hot.wait(eng, i, b - 2)
                for n in range(ACT_TILES):
                    last = nc.scalar.activation(away[:, b % 2, n, :], iota_b[:, :], ACT.Abs,
                                                scale=-1.0,
                                                bias=low_b[:, bass.ds((i * 2 + b) * B + (DVE_TILES + n), 1)])
                last.then_inc(s_away, 1)
                r_hist.wait(eng, i, b - 2)
                eng.wait_ge(s_away, i * 2 + (b + 1))
                nc.scalar.activation(hots[:, b % 2, DVE_TILES:, :], away[:, b % 2, :, :], ACT.Relu, bias=1.0, scale=-1.0
                                     ).then_inc(r_act_hot.sem(b), 1)

            def keep_counts(i, b):
                r_hist.wait(eng, i, b)
                nc.scalar.copy(counts[:, :, bass.ds((i * 2 + b) * B + 1, B)].rearrange("p h t -> p t h"),
                               ranks[b][:, :].rearrange("p (t h) -> p t h", h=BLOCKS)).then_inc(r_kept.sem(b), 1)

            one_hots(0, 0)
            with eng.Fori(0, TURNS - 1) as i:
                for b in range(2):
                    one_hots(i, b + 1)
                    keep_counts(i, b)
            one_hots(TURNS - 1, 1)
            for b in range(2):
                keep_counts(TURNS - 1, b)
            eng.wait_ge(s_begun, 1)
            for h in range(BLOCKS - ACT_BLOCKS, BLOCKS):
                last = nc.scalar.activation(counts[:, h, 0:IN_TILES], counts[:, h, 0:IN_TILES], ACT.Identity,
                                            bias=start[:, h:h + 1])
            last.then_inc(s_start, 1)
            eng.wait_ge(s_parts, 2)
            eng.wait_ge(s_cols, 16)

            def stage(i, b):
                for u in range(B):
                    eng.wait_ge(put[b][u], i * 16 + 16)
                eng.wait_ge(s_bias[b], i * 16 + 16)
                nc.scalar.copy(staged[:, b, :, 2:REC], bias_sb[:, b, :].rearrange("p (t h) -> p t h", h=HEADS))
                nc.scalar.copy(staged[:, b, :, 0], col_i[:, batch(i, b)])
                nc.scalar.copy(staged[:, b, :, 1], row_f[:, batch(i, b)]).then_inc(r_staged.sem(b), 1)

            def roots(done):
                for n in range(2):
                    eng.wait_ge(s_var, done + n + 1)
                    nc.scalar.activation(root[:, :], mean_var[:, 1:2], ACT.Sqrt, bias=eps[:, :]).then_inc(s_root, 1)

            def keep(j, c):
                r_turn.wait(eng, j, c)
                r_prod[2].wait(eng, j, c - 2)
                nc.scalar.copy(zT[:, c % 2, :], turned[:, :]).then_inc(r_zT.sem(c), 1)

            roots(0)
            with eng.Fori(0, ROW_TURNS - 1) as j:
                for c in range(2):
                    keep(j, c)
                    roots(j * 4 + 2 * (c + 1))
                    stage(j, c)
            last = ROW_TURNS - 1
            keep(last, 0)
            roots(last * 4 + 2)
            stage(last, 0)
            keep(last, 1)
            stage(last, 1)
            for b in range(2):
                stage(TURNS - 1, b)

        @block.vector
        def _(eng):
            for r in (r_hot, r_same, r_low, r_addr, r_z0, r_z, *r_out):
                r.start(eng)
            st = Steps(eng, s_dve)
            eng.wait_ge(s_rows, 16)
            st.link(nc.vector.tensor_scalar(part_i[:, :], row_i[:, :], 7, None, ALU.arith_shift_right))
            st.link(nc.vector.tensor_copy(blk_b[:, :], part_i[:, :]))
            st.link(nc.vector.tensor_scalar(part_i[:, :], row_i[:, :], P - 1, None, ALU.bitwise_and))
            nc.vector.tensor_copy(low_b[:, :], part_i[:, :]).then_inc(s_parts, 1)
            nc.vector.tensor_copy(row_f[:, :], row_i[:, :]).then_inc(s_parts, 1)
            eng.wait_ge(s_parts, 2)
            eng.wait_ge(s_const, 7)

            def hot_block(i, b):
                return nc.vector.tensor_tensor(
                    blk_hot[:, b, :, :], iota_b[:, 0:BLOCKS].unsqueeze(1).broadcast_to([P, B, BLOCKS]),
                    blk_b[:, batch(i, b)].unsqueeze(2).broadcast_to([P, B, BLOCKS]), ALU.is_equal)

            with eng.Fori(0, TURNS) as i:
                for b in range(2):
                    r_hist.wait(eng, i, b - 2)
                    hot_block(i, b)
                    nc.vector.tensor_tensor(
                        hots[:, b, 0:DVE_TILES, :], iota_b[:, :].unsqueeze(1).broadcast_to([P, DVE_TILES, P]),
                        low_b[:, bass.ds((i * 2 + b) * B, DVE_TILES)].unsqueeze(2).broadcast_to([P, DVE_TILES, P]),
                        ALU.is_equal).then_inc(r_hot.sem(b), 1)
            eng.wait_ge(s_linear, 16)
            st.link(nc.vector.tensor_scalar(row_i[:, :], row_i[:, :], P - 1, None, ALU.bitwise_and))
            nc.vector.tensor_copy(low_x[:, :], row_i[:, :]).then_inc(s_low_x, 1)
            for b in range(2):
                r_kept.wait(eng, TURNS - 1, b)
            st.link(nc.vector.memset(counts[:, :, 0:1], 0.0))
            for h in range(BLOCKS):
                last = nc.vector.tensor_tensor_scan(counts[:, h, 1:], zeros_f[:, :], counts[:, h, 1:], 0.0,
                                                    ALU.add, ALU.add)
            st.link(last)
            nc.vector.tensor_copy(total[:, :], counts[:, :, IN_TILES]).then_inc(s_total, 1)
            eng.wait_ge(s_small, 1)
            st.link(nc.vector.tensor_scalar(fill_i[:, :], small[:, 0:BLOCKS], float(SPAN - 1), None, ALU.add))
            st.link(nc.vector.tensor_scalar(fill_s[:, :], fill_i[:, :], SPAN.bit_length() - 1, None, ALU.arith_shift_right))
            st.link(nc.vector.tensor_scalar(fill_f[:, :], fill_s[:, :], float(SPAN), None, ALU.mult))
            st.link(nc.vector.tensor_tensor_scan(ends[:, :], zeros_f[:, 0:BLOCKS], fill_f[:, :], 0.0, ALU.add, ALU.add))
            st.link(nc.vector.tensor_tensor(start[:, :], ends[:, :], fill_f[:, :], ALU.subtract))
            nc.vector.tensor_tensor(start[:, :], small[:, BLOCKS:], start[:, :], ALU.add).then_inc(s_begun, 1)
            eng.wait_ge(s_begun, 1)
            mine = slice(0, BLOCKS - ACT_BLOCKS)
            nc.vector.tensor_tensor(counts[:, mine, 0:IN_TILES], counts[:, mine, 0:IN_TILES],
                                    start[:, mine].unsqueeze(2).broadcast_to([P, BLOCKS - ACT_BLOCKS, IN_TILES]),
                                    ALU.add).then_inc(s_start, 1)
            st.link(nc.vector.tensor_scalar(group_at[:, :], group_at[:, :], float(SPAN), None, ALU.mult))
            st.link(nc.vector.tensor_tensor(passed[:, :, :], group_at[:, :].unsqueeze(2).broadcast_to([P, GC, BLOCKS]),
                                            ends[:, :].unsqueeze(1).broadcast_to([P, GC, BLOCKS]), ALU.is_ge))
            st.link(nc.vector.tensor_reduce(group_f[:, :], passed[:, :, :], AX.X, ALU.add))
            nc.vector.tensor_scalar(group_i[:, :], group_f[:, :], float(BLOCKS - 1), None, ALU.min).then_inc(s_groups, 1)
            eng.wait_ge(s_cut, 3)

            def compare(i, b):
                eng.wait_ge(s_bc[b], i * 16 + 16)
                r_ranks.wait(eng, i, b - 2)
                for u in range(B):
                    last = nc.vector.scalar_tensor_tensor(
                        hots[:, b, u, :], row_bc[:, b, u * P:(u + 1) * P],
                        row_f[:, bass.ds(i * 2 * B + b * B + u, 1)], earlier_b[:, :], ALU.is_equal, ALU.mult)
                last.then_inc(r_same.sem(b), 1)
                eng.wait_ge(s_low_bc[b], i * 16 + 16)
                nc.vector.tensor_scalar(low_hot_t[:, b, :], low_bc[:, b, :], iota_p[:, :], None,
                                        ALU.is_equal).then_inc(r_low.sem(b), 1)

            def place_edges(i, b):
                st2 = Steps(eng, s_pass2, i, 10, b * 5)
                hot_block(i, b).then_inc(s_pass2, 1)
                st2.n = 1
                r_ranks.wait(eng, i, b)
                eng.wait_ge(s_pass2, st2.value())
                st2.link(nc.vector.tensor_tensor(picked[:, :, :], ranks[b][:, :].rearrange("p (t h) -> p t h", h=BLOCKS),
                                                 blk_hot[:, b, :, :], ALU.mult))
                st2.link(nc.vector.tensor_reduce(before[:, :], picked[:, :, :], AX.X, ALU.add))
                st2.link(nc.vector.tensor_tensor(place[:, :], within[b][:, :], before[:, :], ALU.add))
                nc.vector.tensor_scalar(tile_of[:, :], place[:, :], 7, None, ALU.arith_shift_right)
                st2.link(nc.vector.tensor_scalar(part_of[:, :], place[:, :], P - 1, None, ALU.bitwise_and))
                for u in range(B):
                    eng.wait_ge(put[b][u], i * 16 + 16)
                nc.vector.scalar_tensor_tensor(address[:, b, :], part_of[:, :], float(TILES),
                                               tile_of[:, :], ALU.mult, ALU.add).then_inc(r_addr.sem(b), 1)
                assert st2.n == 5

            def norms(st, j, c):
                done = j * 4 + 2 * c
                eng.wait_ge(s_x[c % 2], j * 16 + (16 + c // 2 * 16))
                r_stored_z0.wait(eng, j, c - 2)
                norm_scale(nc, eng, st, s_bn, s_var, s_root, done + 1, xt[:, c % 2, :], stats[:, :], mean_var[:, :],
                           root[:, :], z0t[:, c % 2, :]).then_inc(r_z0.sem(c), 1)
                r_z0.wait(eng, j, c)
                st.link(norm_scale(nc, eng, st, s_bn, s_var, s_root, done + 2, z0t[:, c % 2, :], stats[:, :],
                                   mean_var[:, :], root[:, :], zn[:, :]))
                st.link(nc.vector.tensor_tensor(zn[:, :], zn[:, :], gain[:, :], ALU.mult))
                r_turn.wait(eng, j, c - 2)
                nc.vector.tensor_tensor(zt[:, c % 2, :], zn[:, :], shift[:, :], ALU.add).then_inc(r_z.sem(c), 1)

            def leave(j, c):
                for n in range(3):
                    r_prod[n].wait(eng, j, c)
                    r_stored[n].wait(eng, j, c - 2)
                    nc.vector.scalar_tensor_tensor(out[:, c, n, :], prod[n][:, :], float(D) ** -0.5 if n == 0 else 1.0,
                                                   bias[:, n, :], ALU.mult, ALU.add).then_inc(r_out[n].sem(c), 1)

            STEPS = 6
            eng.wait_ge(s_b, 80)
            pre = Steps(eng, s_norm)
            pre.link(nc.vector.tensor_scalar(bias[:, 0, :], bias[:, 0, :], float(D) ** -0.5, None, ALU.mult))
            compare(0, 0)
            norms(pre, 0, 0)
            compare(0, 1)
            assert pre.n == STEPS + 1
            with eng.Fori(0, ROW_TURNS - 1) as j:
                st = Steps(eng, s_norm, j, 2 * STEPS, STEPS + 1)
                for c in range(2):
                    place_edges(j, c)
                    norms(st, j, c + 1)
                    compare(j + 1, c)
                    leave(j, c)
            last = ROW_TURNS - 1
            post = Steps(eng, s_norm, None, 0, STEPS + 1 + last * 2 * STEPS)
            place_edges(last, 0)
            norms(post, last, 1)
            compare(TURNS - 1, 0)
            leave(last, 0)
            place_edges(last, 1)
            compare(TURNS - 1, 1)
            leave(last, 1)
            for b in range(2):
                place_edges(TURNS - 1, b)

        @block.tensor
        def _(eng):
            for r in (r_hist, r_ranks, r_turn, *r_prod):
                r.start(eng)
            with eng.Fori(0, TURNS) as i:
                for b in range(2):
                    r_hot.wait(eng, i, b)
                    r_act_hot.wait(eng, i, b)
                    r_kept.wait(eng, i, b - 2)
                    for u in range(B):
                        last = nc.tensor.matmul(ranks[b][:, u * BLOCKS:(u + 1) * BLOCKS], hots[:, b, u, :],
                                                blk_hot[:, b, u, :], start=True, stop=True)
                    last.then_inc(r_hist.sem(b), 1)
            eng.wait_ge(s_total, 1)
            eng.wait_ge(s_cut, 3)
            nc.tensor.matmul(small[:, 0:BLOCKS], ones_f[:, :], total[:, :], start=True, stop=True)
            nc.tensor.matmul(small[:, BLOCKS:], earlier[:, :], total[:, :], start=True, stop=True).then_inc(s_small, 1)
            eng.wait_ge(s_start, 2)
            eng.wait_ge(s_w, 48)

            def rank(i, b):
                r_low.wait(eng, i, b)
                r_addr.wait(eng, i, b - 2)
                for u in range(B):
                    nc.tensor.matmul(ranks[b % 2][:, u * BLOCKS:(u + 1) * BLOCKS], low_hot_t[:, b % 2, u * P:(u + 1) * P],
                                     counts[:, :, bass.ds(i * 2 * B + b * B + u, 1)].rearrange("p h a -> p (h a)"),
                                     start=True, stop=True)
                for u in range(B):
                    last = nc.tensor.matmul(within[b % 2][:, u:u + 1], hots[:, b % 2, u, :], ones_b[:, :],
                                            start=True, stop=True)
                last.then_inc(r_ranks.sem(b), 1)

            def turn(j, c):
                r_z.wait(eng, j, c)
                for n in range(KC):
                    last = nc.tensor.transpose(turned[:, n * P:(n + 1) * P], zt[:, c, n * P:(n + 1) * P], ident[:, :])
                last.then_inc(r_turn.sem(c), 1)

            def project(j, c):
                r_zT.wait(eng, j, c)
                r_out[2].wait(eng, j, c - 1)
                for n in range(3):
                    for kc in range(KC):
                        last = nc.tensor.matmul(prod[n][:, :], zT[:, c, kc * P:(kc + 1) * P], w[:, n, kc, :],
                                                start=(kc == 0), stop=(kc == KC - 1))
                    last.then_inc(r_prod[n].sem(c), 1)

            rank(0, 0)
            with eng.Fori(0, ROW_TURNS - 1) as j:
                for c in range(2):
                    turn(j, c)
                    rank(j, c + 1)
                    project(j, c)
            for c in range(2):
                turn(ROW_TURNS - 1, c)
                rank(ROW_TURNS - 1, c + 1)
                project(ROW_TURNS - 1, c)
            rank(TURNS - 1, 1)


def attention(nc, moved, count, records, group_block, q, k, v, mixed):
    SLOTS = 16
    U = SLOTS // 2
    TURN = 2 * SLOTS
    TURNS = TILES // TURN
    assert TILES % TURN == 0
    BIG = 3.0e38
    DVE_HEADS = HEADS - 1
    k_from = count
    v_from = count + 16 * (TILES // SLOTS)
    LANE = RANGE_TILES * P
    with ExitStack() as ctx:
        def sb(name, shape, dt, on=ctx):
            return on.enter_context(nc.sbuf_tensor(name, shape, dt))

        def ps(name, shape, dt=F32, on=ctx):
            return on.enter_context(nc.psum_tensor(name, shape, dt))

        def sem(name, on=ctx):
            used.append(on.enter_context(nc.semaphore(name)))
            return used[-1]

        rec = sb("at_rec", [P, TILES, REC], F32)
        groups = sb("groups", [1, 1 + GROUPS], I32)
        low_neg = sb("low_neg", [P, TILES + 5], F32)
        weight = sb("weight", [P, TILES, HEADS], F32)
        iota_f = sb("iota_f", [P, P], F32)
        ident = sb("ident", [P, P], F32)
        ident_b = sb("ident_b", [P, P], BF16)
        ones = sb("ones", [P, P], F32)

        fetched = sb("fetched", [P, SLOTS, C], F32)
        index = sb("at_index", [P, 2, U], I32)

        def fetches(i, n):
            return i * (16 * (TURN // SLOTS)) + 16 * n

        used = []
        with ExitStack() as part:
            q_sb = sb("q_sb", [P, BLOCKS, C], F32, part)
            row_i = sb("at_row_i", [P, TILES], I32, part)
            low_f = sb("at_low_f", [P, TILES], F32, part)
            padded = sb("padded", [P, TILES], F32, part)
            away = sb("away", [P, 4, P], F32, part)
            hot = sb("hot", [P, 4, P], BF16, part)
            hot_t = sb("hot_t", [P, 4, P], F32, part)
            product = sb("product", [P, 4, C], F32, part)
            turned = [ps(f"turned{b}", [P, P], BF16, part) for b in range(4)]
            q_edge = [ps(f"q_edge{b}", [P, C], F32, part) for b in range(4)]
            s_const, s_cut = sem("a_const", part), sem("a_cut", part)
            s_rec, s_grp, s_q = sem("a_rec", part), sem("a_grp", part), sem("a_q", part)
            s_dve, s_low, s_index, s_passed = (sem(n, part) for n in ("a_dve", "a_low", "a_index", "a_passed"))
            s_k = moved[:SLOTS]
            r_away, r_hot, r_turned, r_hot_t, r_edge, r_product, r_score, r_last = (
                Ring([sem(f"{n}{b}", part) for b in range(4)], TURN)
                for n in ("a_away", "a_hot", "a_turned", "a_hot_t", "a_edge", "a_product", "a_score", "a_last"))
            block = open_block(nc, part, used)

            @block.sync
            def _(eng):
                eng.dma_start(rec[:, :, :], records.rearrange("(p t) w -> p t w", p=P)).then_inc(s_rec, 16)
                eng.dma_start(groups[0:1, 1:], group_block[0:GROUPS].unsqueeze(0)).then_inc(s_grp, 16)
                eng.dma_start(q_sb[:, :, :], q.rearrange("(b p) c -> p b c", p=P)).then_inc(s_q, 16)

            @block.gpsimd
            def _(eng):
                eng.memset(ones[:, :], 1.0).then_inc(s_const, 1)
                eng.iota(iota_f[:, :], pattern=[[1, P]], base=0, channel_multiplier=0,
                         allow_small_or_imprecise_dtypes=True).then_inc(s_const, 1)
                eng.memset(low_neg[:, TILES:], 0.0).then_inc(s_const, 1)
                eng.memset(groups[0:1, 0:1], 0).then_inc(s_const, 1)
                eng.wait_ge(s_const, 4)
                for m in (ident, ident_b):
                    eng.affine_select(out=m[:, :], in_=ones[:, :], compare_op=ALU.is_equal, fill=0.0, base=0,
                                      pattern=[[1, P]], channel_multiplier=-1).then_inc(s_cut, 1)
                eng.wait_ge(s_rec, 16)
                with eng.Fori(0, TURNS) as i:
                    for portion in range(TURN // U):
                        half = portion % 2
                        for n in range(U):
                            eng.wait_ge(s_k[half * U + n], fetches(i, portion // 2) + k_from)
                        eng.tensor_copy(index[:, half, :], rec[:, bass.ds(i * TURN + portion * U, U), 0]
                                        ).then_inc(s_index, 1)
                        eng.wait_ge(s_index, i * (TURN // U) + portion + 1)
                        for n in range(U):
                            u = portion * U + n
                            r_product.wait(eng, i, u - SLOTS)
                            eng.sem_inc(s_passed, 1)
                            eng.indirect_dma_start(fetched[:, u % SLOTS, :], None, k,
                                                   bass.IndirectOffsetOnAxis(index[:, half, n:n + 1], 0)
                                                   ).then_inc(s_k[u % SLOTS], 16)

            @block.vector
            def _(eng):
                st = Steps(eng, s_dve)
                r_product.start(eng)
                r_score.start(eng)
                eng.wait_ge(s_rec, 16)
                row = rec[:, :, 1]
                st.link(nc.vector.tensor_copy(row_i[:, :], row))
                st.link(nc.vector.tensor_scalar(row_i[:, :], row_i[:, :], P - 1, None, ALU.bitwise_and))
                st.link(nc.vector.tensor_copy(low_f[:, :], row_i[:, :]))
                st.link(nc.vector.tensor_scalar(padded[:, :], row, 0.0, float(4 * P), ALU.is_lt, ALU.mult))
                st.link(nc.vector.tensor_tensor(low_f[:, :], low_f[:, :], padded[:, :], ALU.add))
                nc.vector.tensor_scalar(low_neg[:, 0:TILES], low_f[:, :], -1.0, None, ALU.mult).then_inc(s_low, 1)
                with eng.Fori(0, TURNS) as i:
                    def reduce(u):
                        r_product.wait(eng, i, u)
                        nc.vector.tensor_reduce(weight[:, bass.ds(i * TURN + u, 1), 0:DVE_HEADS].rearrange("p a h -> p (a h)"),
                                                product[:, u % 4, 0:DVE_HEADS * D].rearrange("p (h d) -> p h d", d=D), AX.X,
                                                ALU.add).then_inc(r_score.sem(u), 1)

                    for u in range(TURN):
                        eng.wait_ge(s_k[u % SLOTS], fetches(i, u // SLOTS + 1) + k_from)
                        r_edge.wait(eng, i, u)
                        r_score.wait(eng, i, u - 4)
                        r_last.wait(eng, i, u - 4)
                        nc.vector.tensor_tensor(product[:, u % 4, :], q_edge[u % 4][:, :], fetched[:, u % SLOTS, :],
                                                ALU.mult).then_inc(r_product.sem(u), 1)
                        if u:
                            reduce(u - 1)
                    reduce(TURN - 1)

            @block.scalar
            def _(eng):
                for r in (r_away, r_hot, r_hot_t, r_last):
                    r.start(eng)
                eng.wait_ge(s_low, 1)
                eng.wait_ge(s_const, 4)

                def distance(i, u):
                    r_hot.wait(eng, i, u - 4)
                    nc.scalar.activation(away[:, u % 4, :], iota_f[:, :], ACT.Abs, bias=low_neg[:, bass.ds(i * TURN + u, 1)]
                                         ).then_inc(r_away.sem(u), 1)

                def one_hot(i, u):
                    r_away.wait(eng, i, u)
                    r_turned.wait(eng, i, u - 4)
                    nc.scalar.activation(hot[:, u % 4, :], away[:, u % 4, :], ACT.Relu, bias=1.0, scale=-1.0
                                         ).then_inc(r_hot.sem(u), 1)

                def transposed(i, u):
                    r_turned.wait(eng, i, u)
                    r_edge.wait(eng, i, u - 4)
                    nc.scalar.copy(hot_t[:, u % 4, :], turned[u % 4][:, :]).then_inc(r_hot_t.sem(u), 1)

                def last_heads(i, u):
                    r_product.wait(eng, i, u)
                    for h in range(DVE_HEADS, HEADS):
                        mine = product[:, u % 4, h * D:(h + 1) * D]
                        ins = nc.scalar.activation(mine, mine, ACT.Copy, accum_out=weight[:, bass.ds(i * TURN + u, 1), h])
                    ins.then_inc(r_last.sem(u), 1)

                for u in range(3):
                    distance(0, u)
                for u in range(2):
                    one_hot(0, u)
                for u in range(2):
                    distance(0, u + 3)
                    one_hot(0, u + 2)
                    transposed(0, u)
                with eng.Fori(0, TURNS) as i:
                    for u in range(TURN):
                        distance(i, u + 5)
                        one_hot(i, u + 4)
                        transposed(i, u + 2)
                        last_heads(i, u)

            @block.tensor
            def _(eng):
                r_turned.start(eng)
                r_edge.start(eng)
                eng.wait_ge(s_cut, 2)
                eng.wait_ge(s_grp, 16)
                eng.wait_ge(s_q, 16)

                def turn(i, u):
                    r_hot.wait(eng, i, u)
                    r_hot_t.wait(eng, i, u - 4)
                    nc.tensor.transpose(turned[u % 4][:, :], hot[:, u % 4, :], ident_b[:, :]).then_inc(r_turned.sem(u), 1)

                turn(0, 0)
                turn(0, 1)
                with eng.Fori(0, TURNS) as i:
                    for u in range(TURN):
                        if u % GROUP == 0:
                            at = eng.value_load(groups[0:1, bass.ds(i * (TURN // GROUP) + u // GROUP + 1, 1)],
                                                min_val=0, max_val=BLOCKS - 1)
                        turn(i, u + 2)
                        r_hot_t.wait(eng, i, u)
                        r_product.wait(eng, i, u - 4)
                        nc.tensor.matmul(q_edge[u % 4][:, :], hot_t[:, u % 4, :],
                                         q_sb[:, bass.ds(at, 1), :].rearrange("p a c -> p (a c)"),
                                         start=True, stop=True).then_inc(r_edge.sem(u), 1)

        used = []
        with ExitStack() as part:
            PAIR = 2
            LOOPS = (RANGE_TILES // PAIR - 1) // 2
            assert RANGE_TILES == PAIR * (2 * LOOPS + 1)
            stage_s = sb("stage_s", [P, 2, PAIR, RANGES, HEADS], F32, part)
            stage_k = sb("stage_k", [P, 2, PAIR, RANGES, HEADS], F32, part)
            stage_p = sb("stage_p", [P, 2, PAIR * P], F32, part)
            keys = sb("keys", [P, LANE], F32, part)
            score = sb("score", [P, LANE], F32, part)
            cont = sb("cont", [P, LANE + 1], F32, part)
            ahead = sb("ahead", [P, LANE], F32, part)
            back = sb("back", [P, LANE], F32, part)
            row4 = sb("row4", [1, 4, HEADS, RANGES], F32, part)
            linked = sb("linked", [1, HEADS, RANGES + 1], F32, part)
            whole = sb("whole", [1, HEADS, RANGES], F32, part)
            pass_f = sb("pass_f", [1, HEADS, RANGES], F32, part)
            pass_b = sb("pass_b", [1, HEADS, RANGES], F32, part)
            state = sb("state", [1, 2, HEADS, RANGES], F32, part)
            carry = sb("carry", [1, 2, RANGES, HEADS], F32, part)
            carried = sb("carried", [P, 2], F32, part)
            turn_s = [ps(f"turn_s{b}", [P, PAIR * P], F32, part) for b in range(2)]
            turn_k = [ps(f"turn_k{b}", [P, PAIR * P], F32, part) for b in range(2)]
            ends4 = ps("ends4", [1, 4 * P], F32, part)
            carry_ps = ps("carry_ps", [P, 2], F32, part)
            s_dve, s_loc, s_ends, s_carry, s_carried, s_sub, s_index = (
                sem(n, part) for n in ("m_dve", "m_loc", "m_ends", "m_carry", "m_carried", "m_sub", "m_index"))
            r_sum, r_row, r_turn, r_keep_s, r_keep_k, r_exp, r_back, r_keep = (
                Ring([sem(f"m_{n}", part)], 2)
                for n in ("sum", "row", "turn", "keep_s", "keep_k", "exp", "back", "keep"))
            block = open_block(nc, part, used)

            def pairs(eng, body, ahead=None):
                if ahead:
                    ahead(0, 0)
                with eng.Fori(0, LOOPS) as i:
                    for b in range(2):
                        if ahead:
                            ahead(i, b + 1)
                        body(i, b)
                body(LOOPS, 0)

            def tiles_of(i, b):
                return bass.ds((i * 2 + b) * PAIR, PAIR)

            def places_of(i, b):
                return bass.ds((i * 2 + b) * PAIR * P, PAIR * P)

            def by_range(x):
                return x.rearrange("p (c j) h -> p c j h", c=RANGES)

            rec_range = by_range(rec[:, :, :])

            @block.gpsimd
            def _(eng):
                for half in range(2):
                    for n in range(U):
                        eng.wait_ge(moved[half * U + n], v_from)
                    eng.tensor_copy(index[:, half, :], rec[:, half * U:(half + 1) * U, 0]).then_inc(s_index, 1)
                    eng.wait_ge(s_index, half + 1)
                    for n in range(U):
                        u = half * U + n
                        eng.indirect_dma_start(fetched[:, u, :], None, v,
                                               bass.IndirectOffsetOnAxis(index[:, half, n:n + 1], 0)
                                               ).then_inc(moved[u], 16)

            @block.tensor
            def _(eng):
                for r in (r_turn, r_back):
                    r.start(eng)

                def turn(i, b):
                    r_sum.wait(eng, i, b)
                    r_row.wait(eng, i, b)
                    r_keep_s.wait(eng, i, b - 2)
                    r_keep_k.wait(eng, i, b - 2)
                    for to, of in ((turn_s, stage_s), (turn_k, stage_k)):
                        for n in range(PAIR):
                            last = nc.tensor.transpose(to[b][:, n * P:(n + 1) * P],
                                                       of[:, b, n, :, :].rearrange("p c h -> p (c h)"), ident[:, :])
                    last.then_inc(r_turn.sem(b), 1)

                pairs(eng, turn)
                eng.wait_ge(s_loc, 2)
                for n, x in enumerate((ahead[:, LANE - 1:LANE], back[:, 0:1], keys[:, 0:1], keys[:, LANE - 1:LANE])):
                    last = nc.tensor.transpose(ends4[0:1, n * P:(n + 1) * P], x, ident[:, :])
                last.then_inc(s_ends, 1)
                eng.wait_ge(s_carry, 1)
                for n in range(2):
                    last = nc.tensor.matmul(carry_ps[:, n:n + 1], carry[0:1, n, :, :].rearrange("p c h -> p (c h)"),
                                            ones[0:1, 0:1], start=True, stop=True)
                last.then_inc(s_carried, 1)

                def back_turn(i, b):
                    r_exp.wait(eng, i, b)
                    r_keep.wait(eng, i, b - 2)
                    for n in range(PAIR):
                        last = nc.tensor.transpose(turn_s[b][:, n * P:(n + 1) * P], stage_p[:, b, n * P:(n + 1) * P],
                                                   ident[:, :])
                    last.then_inc(r_back.sem(b), 1)

                pairs(eng, back_turn)

            @block.scalar
            def _(eng):
                for r in (r_row, r_keep_k, r_exp):
                    r.start(eng)

                def rows_of(i, b):
                    r_turn.wait(eng, i, b - 2)
                    nc.scalar.copy(stage_k[:, b % 2, :, :, :].rearrange("p n c h -> p c n h"),
                                   rec_range[:, :, tiles_of(i, b), 1:2].broadcast_to([P, RANGES, PAIR, HEADS])
                                   ).then_inc(r_row.sem(b), 1)

                def keep_rows(i, b):
                    r_turn.wait(eng, i, b)
                    nc.scalar.copy(keys[:, places_of(i, b)], turn_k[b][:, :]).then_inc(r_keep_k.sem(b), 1)

                pairs(eng, keep_rows, rows_of)
                eng.wait_ge(s_sub, 1)

                def exponentials(i, b):
                    r_back.wait(eng, i, b - 2)
                    nc.scalar.activation(stage_p[:, b, :], score[:, places_of(i, b)], ACT.Exp).then_inc(r_exp.sem(b), 1)

                pairs(eng, exponentials)

            @block.vector
            def _(eng):
                st = Steps(eng, s_dve)
                for r in (r_sum, r_keep_s, r_keep):
                    r.start(eng)

                def add_bias(i, b):
                    r_turn.wait(eng, i, b - 2)
                    nc.vector.tensor_tensor(stage_s[:, b % 2, :, :, :].rearrange("p n c h -> p c n h"),
                                            by_range(weight[:, :, :])[:, :, tiles_of(i, b), :],
                                            rec_range[:, :, tiles_of(i, b), 2:REC], ALU.add).then_inc(r_sum.sem(b), 1)

                def keep_scores(i, b):
                    r_turn.wait(eng, i, b)
                    nc.vector.tensor_copy(score[:, places_of(i, b)], turn_s[b][:, :]).then_inc(r_keep_s.sem(b), 1)

                pairs(eng, keep_scores, add_bias)
                r_keep_k.wait(eng, LOOPS, 0)
                r_keep_s.wait(eng, LOOPS, 0)
                st.link(nc.vector.memset(cont[:, :], 1.0))
                st.link(nc.vector.tensor_tensor(cont[:, 1:LANE], keys[:, 1:], keys[:, 0:LANE - 1], ALU.is_equal))
                st.link(nc.vector.tensor_scalar(cont[:, :], cont[:, :], 1.0, BIG, ALU.subtract, ALU.mult))
                nc.vector.tensor_tensor_scan(ahead[:, :], cont[:, 0:LANE], score[:, :], -BIG, ALU.add, ALU.max).then_inc(s_loc, 1)
                nc.vector.tensor_tensor_scan(back[:, ::-1], cont[:, LANE:0:-1], score[:, ::-1], -BIG, ALU.add, ALU.max).then_inc(s_loc, 1)
                eng.wait_ge(s_ends, 1)
                st.link(nc.vector.tensor_copy(row4[:, :, :, :], ends4[0:1, :].rearrange("p (n c h) -> p n h c", n=4, c=RANGES)))
                first, last = row4[0:1, 2, :, :], row4[0:1, 3, :, :]
                st.link(nc.vector.memset(linked[:, :, :], 0.0))
                st.link(nc.vector.tensor_tensor(linked[:, :, 1:RANGES], first[:, :, 1:], last[:, :, 0:RANGES - 1], ALU.is_equal))
                st.link(nc.vector.tensor_tensor(whole[:, :, :], first, last, ALU.is_equal))
                for to, at in ((pass_f, linked[:, :, 0:RANGES]), (pass_b, linked[:, :, 1:])):
                    st.link(nc.vector.tensor_tensor(to[:, :, :], whole[:, :, :], at, ALU.mult))
                    st.link(nc.vector.tensor_scalar(to[:, :, :], to[:, :, :], 1.0, BIG, ALU.subtract, ALU.mult))
                st.link(nc.vector.tensor_scalar(linked[:, :, :], linked[:, :, :], 1.0, BIG, ALU.subtract, ALU.mult))

                def flat(x):
                    return x.rearrange("p h c -> p (h c)")

                st.link(nc.vector.tensor_tensor_scan(flat(state[:, 0, :, :]), flat(pass_f[:, :, :]),
                                                     flat(row4[:, 0, :, :]), 0.0, ALU.add, ALU.max))
                st.link(nc.vector.tensor_tensor_scan(flat(state[:, 1, :, :])[:, ::-1], flat(pass_b[:, :, :])[:, ::-1],
                                                     flat(row4[:, 1, :, :])[:, ::-1], 0.0, ALU.add, ALU.max))
                st.link(nc.vector.memset(carry[:, :, :, :], -BIG))
                st.link(nc.vector.tensor_tensor(carry[:, 0, 1:, :].rearrange("p c h -> p h c"), state[:, 0, :, 0:RANGES - 1],
                                                linked[:, :, 1:RANGES], ALU.add))
                nc.vector.tensor_tensor(carry[:, 1, 0:RANGES - 1, :].rearrange("p c h -> p h c"), state[:, 1, :, 1:],
                                        linked[:, :, 1:RANGES], ALU.add).then_inc(s_carry, 1)
                eng.wait_ge(s_carried, 1)
                st.link(nc.vector.tensor_copy(carried[:, :], carry_ps[:, :]))
                st.link(nc.vector.tensor_tensor_scan(ahead[:, :], cont[:, 0:LANE], score[:, :], carried[:, 0:1], ALU.add, ALU.max))
                st.link(nc.vector.tensor_tensor_scan(back[:, ::-1], cont[:, LANE:0:-1], score[:, ::-1], carried[:, 1:2],
                                                     ALU.add, ALU.max))
                st.link(nc.vector.tensor_tensor(ahead[:, :], ahead[:, :], back[:, :], ALU.max))
                nc.vector.tensor_tensor(score[:, :], score[:, :], ahead[:, :], ALU.subtract).then_inc(s_sub, 1)

                def keep_weights(i, b):
                    r_back.wait(eng, i, b)
                    nc.vector.tensor_copy(by_range(weight[:, :, :])[:, :, tiles_of(i, b), :],
                                          turn_s[b][:, :].rearrange("p (n c h) -> p c n h", n=PAIR, c=RANGES)
                                          ).then_inc(r_keep.sem(b), 1)

                pairs(eng, keep_weights)

        used = []
        with ExitStack() as part:
            total = sb("mix_total", [P, BLOCKS, C], F32, part)
            mass = sb("mix_mass", [P, BLOCKS, HEADS], F32, part)
            scaled = sb("scaled", [P, 4, C], F32, part)
            away = sb("v_away", [P, 4, P], F32, part)
            hot = sb("v_hot", [P, 4, P], F32, part)
            mix = [ps(f"mix{b}", [P, C], F32, part) for b in range(4)]
            mass_ps = [ps(f"mass{b}", [P, HEADS], F32, part) for b in range(4)]
            s_passed, s_dve, s_zeroed, s_cleared, s_index, s_norm, s_out = (
                sem(f"v_{n}", part) for n in ("passed", "dve", "zeroed", "cleared", "index", "norm", "out"))
            s_v = moved[:SLOTS]
            r_away, r_hot, r_scaled, r_tile = (
                Ring([sem(f"{n}{b}", part) for b in range(4)], TURN) for n in ("v_away", "v_hot", "v_scaled", "v_tile"))
            G2 = TURN // GROUP
            CLEARED = BLOCKS // 2
            PARTS = 8
            r_total, r_mass = (
                Ring([sem(f"{n}{b}", part) for b in range(4)], G2) for n in ("v_total", "v_mass"))
            block = open_block(nc, part, used)

            @block.gpsimd
            def _(eng):
                eng.memset(total[:, BLOCKS - CLEARED:, :], 0.0).then_inc(s_cleared, 1)

                def refill(i, parts):
                    for portion in range(parts):
                        half = portion % 2
                        for n in range(U):
                            eng.wait_ge(s_v[half * U + n], fetches(i, portion // 2 + 1) + v_from)
                        eng.tensor_copy(index[:, half, :], rec[:, bass.ds(i * TURN + (SLOTS + portion * U), U), 0]
                                        ).then_inc(s_index, 1)
                        eng.wait_ge(s_index, i * (TURN // U) + portion + 1)
                        for n in range(U):
                            u = portion * U + n
                            r_scaled.wait(eng, i, u)
                            eng.sem_inc(s_passed, 1)
                            eng.indirect_dma_start(fetched[:, u % SLOTS, :], None, v,
                                                   bass.IndirectOffsetOnAxis(index[:, half, n:n + 1], 0)
                                                   ).then_inc(s_v[u % SLOTS], 16)

                with eng.Fori(0, TURNS - 1) as i:
                    refill(i, TURN // U)
                refill(TURNS - 1, (TURN - SLOTS) // U)

            @block.scalar
            def _(eng):
                r_away.start(eng)
                r_hot.start(eng)

                def distance(i, u):
                    r_hot.wait(eng, i, u - 4)
                    nc.scalar.activation(away[:, u % 4, :], iota_f[:, :], ACT.Abs, bias=low_neg[:, bass.ds(i * TURN + u, 1)]
                                         ).then_inc(r_away.sem(u), 1)

                distance(0, 0)
                with eng.Fori(0, TURNS) as i:
                    for u in range(TURN):
                        distance(i, u + 1)
                        r_away.wait(eng, i, u)
                        r_tile.wait(eng, i, u - 4)
                        nc.scalar.activation(hot[:, u % 4, :], away[:, u % 4, :], ACT.Relu, bias=1.0, scale=-1.0
                                             ).then_inc(r_hot.sem(u), 1)

            @block.vector
            def _(eng):
                r_scaled.start(eng)
                st = Steps(eng, s_dve)
                st.link(nc.vector.memset(total[:, 0:BLOCKS - CLEARED, :], 0.0))
                st.link(nc.vector.memset(mass[:, :, :], 0.0))
                for ring in (r_total, r_mass):
                    for n, s in enumerate(ring.sems):
                        eng.sem_inc(s, ring.per - (n == 3))
                eng.wait_ge(s_zeroed, 1)
                eng.wait_ge(s_cleared, 1)

                def add(i, g):
                    at = eng.value_load(groups[0:1, bass.ds(i * G2 + g + 1, 1)], min_val=0, max_val=BLOCKS - 1)
                    r_tile.wait(eng, i, (g + 1) * GROUP - 1)
                    for ring, to, of in ((r_mass, mass, mass_ps), (r_total, total, mix)):
                        ring.wait(eng, i, g - 1)
                        t = to[:, bass.ds(at, 1), :].rearrange("p a c -> p (a c)")
                        nc.vector.tensor_tensor(t, of[g % 4][:, :], t, ALU.add).then_inc(ring.sem(g), 1)

                with eng.Fori(0, TURNS) as i:
                    for u in range(TURN):
                        eng.wait_ge(s_v[u % SLOTS], fetches(i, u // SLOTS + 1) + v_from)
                        r_tile.wait(eng, i, u - 4)
                        nc.vector.tensor_tensor(
                            scaled[:, u % 4, :].rearrange("p (h d) -> p h d", d=D),
                            fetched[:, u % SLOTS, :].rearrange("p (h d) -> p h d", d=D),
                            weight[:, bass.ds(i * TURN + u, 1), :].rearrange("p a h -> p (a h)").unsqueeze(2)
                            .broadcast_to([P, HEADS, D]), ALU.mult).then_inc(r_scaled.sem(u), 1)
                        if u % GROUP == GROUP - 1:
                            add(i, u // GROUP - 1)
                add(TURNS - 1, G2 - 1)
                r_total.wait(eng, TURNS - 1, G2 - 1)
                r_mass.wait(eng, TURNS - 1, G2 - 1)
                st.link(nc.vector.tensor_scalar(mass[:, :, :], mass[:, :, :], 1e-30, None, ALU.max))
                st.link(nc.vector.reciprocal(mass[:, :, :], mass[:, :, :]))
                for n in range(PARTS):
                    bl = slice(n * BLOCKS // PARTS, (n + 1) * BLOCKS // PARTS)
                    t = total[:, bl, :].rearrange("p b (h d) -> p (b h) d", d=D)
                    nc.vector.tensor_tensor(
                        t, t, mass[:, bl, :].rearrange("p b h -> p (b h)").unsqueeze(2)
                        .broadcast_to([P, BLOCKS // PARTS * HEADS, D]), ALU.mult).then_inc(s_norm, 1)

            @block.tensor
            def _(eng):
                eng.wait_ge(s_dve, 2)
                nc.tensor.matmul(mass_ps[3][:, :], total[:, 0, 0:P], total[:, 0, 0:HEADS], start=True, stop=True)
                nc.tensor.matmul(mix[3][:, :], total[:, 0, 0:P], total[:, 0, :], start=True, stop=True).then_inc(s_zeroed, 1)
                r_tile.start(eng)
                with eng.Fori(0, TURNS) as i:
                    for u in range(TURN):
                        g, first, last = u // GROUP, u % GROUP == 0, u % GROUP == GROUP - 1
                        r_hot.wait(eng, i, u)
                        if first:
                            r_mass.wait(eng, i, g - 4)
                            r_total.wait(eng, i, g - 4)
                        nc.tensor.matmul(mass_ps[g % 4][:, :], hot[:, u % 4, :],
                                         weight[:, bass.ds(i * TURN + u, 1), :].rearrange("p a h -> p (a h)"),
                                         start=first, stop=last)
                        r_scaled.wait(eng, i, u)
                        nc.tensor.matmul(mix[g % 4][:, :], hot[:, u % 4, :], scaled[:, u % 4, :],
                                         start=first, stop=last).then_inc(r_tile.sem(u), 1)

            @block.sync
            def _(eng):
                for n in range(PARTS):
                    eng.wait_ge(s_norm, n + 1)
                    bl = slice(n * BLOCKS // PARTS, (n + 1) * BLOCKS // PARTS)
                    eng.dma_start(mixed.rearrange("(b p) c -> p b c", p=P)[:, bl, :], total[:, bl, :]).then_inc(s_out, 16)
                eng.wait_ge(s_out, 16 * PARTS)


def out_and_ffn(nc, mixed, z0, x, wo, bo, ln_g, ln_b, w1, b1, w2, b2, x3, z3):
    EPS = 1e-5
    KC = C // P
    M = 2
    TURNS = NODES // (M * P)
    HIDDEN = w1.shape[1]
    FC = HIDDEN // P
    LARGE, SMALL = 0, 1
    PIECE = 2 * C
    STORES = 4
    with ExitStack() as ctx:
        def sb(name, shape, dt=F32):
            return ctx.enter_context(nc.sbuf_tensor("f_" + name, shape, dt))

        def ps(name, shape, dt=F32):
            return ctx.enter_context(nc.psum_tensor("f_" + name, shape, dt))

        used = []

        def sem(name):
            used.append(ctx.enter_context(nc.semaphore("fs_" + name)))
            return used[-1]

        def by_tile(*names):
            return [Ring([sem(n)], M) for n in names]

        def moves(*names):
            return [Ring([sem(f"{n}{m}") for m in range(M)], M, 16) for n in names]

        wo_sb, w1_sb, w2_sb = (sb(n, s, F32R) for n, s in (("wo", [P, 2, KC, C]), ("w1", [P, 2, KC, HIDDEN]), ("w2", [P, 2, FC, C])))
        raw = sb("raw", [P, STORES, PIECE])
        bo_sb, b2_sb, gain, shift = sb("bo", [P, C]), sb("b2", [P, C]), sb("gain", [P, C]), sb("shift", [P, C])
        b1_sb = sb("b1", [P, FC])
        ones, ident, eps = sb("ones", [P, P]), sb("ident", [P, P]), sb("eps", [P, 1])
        mixt, z0t, xt = sb("mix", [P, M, C]), sb("z0", [P, M, C]), sb("x", [P, M, C])
        mixT = sb("mixT", [P, 2, M, C], F32R)
        x1 = sb("x1", [P, M, C])
        zn = sb("zn", [P, C])
        z = sb("z", [P, M, C])
        zT = sb("zT", [P, 2, KC, M * P], F32R)
        base = sb("base", [P, 2, M, C])
        h = sb("h", [P, FC, M * P])
        hT = sb("hT", [P, 2, FC, M * P], F32R)
        x3t, z3t = sb("x3", [P, M, C]), sb("z3", [P, M, C])
        stats, mean_var, root = sb("stats", [P, 2, M, 6]), sb("mv", [P, 2, M, 2]), sb("root", [P, 2, M])
        turned = [ps(f"turned{b}", [P, C]) for b in range(2)]
        o_ps = [ps(f"o{b}", [P, C]) for b in range(2)]
        up_ps = [ps(f"up{b}", [P, 2, M * P]) for b in range(2)]
        down_ps = [ps(f"down{b}", [P, C]) for b in range(2)]

        s_b, s_c, s_cut, s_a, s_e, s_passed = (sem(n) for n in ("b", "c", "cut", "a", "e", "passed"))
        s_raw = [sem(f"raw{n}") for n in range(STORES)]
        s_w_large, s_w_small = sem("w_large"), sem("w_small")
        got_mix, got_z0, got_x, put_x3, put_z3 = moves("got_mix", "got_z0", "got_x", "put_x3", "put_z3")
        (r_res, r_mixturn, r_mix_large, r_mix_small, r_o, r_x1, r_z, r_zturn, r_z_large, r_z_small, r_part, r_base, r_down,
         r_x3, r_z3) = by_tile("res", "mixturn", "mix_large", "mix_small", "o", "x1", "z", "zturn", "z_large", "z_small",
                               "part", "base", "down", "x3", "z3")
        r_up, r_h, r_h_large, r_h_small = (Ring([sem(n)], FC) for n in ("up", "h", "h_large", "h_small"))
        s_var_a, s_root_a, s_var_e, s_root_e = (sem(n) for n in ("var_a", "root_a", "var_e", "root_e"))
        block = open_block(nc, ctx, used)

        def rows(a, t, m):
            return a.rearrange("(n p) c -> n p c", p=P)[bass.ds(t * M + m, 1), :, :].rearrange("a p c -> (a p) c")

        def turns(begin, body, end, eng):
            begin()
            with eng.Fori(0, (TURNS - 2) // 2) as j:
                for c in range(2):
                    body(j * 2 + c, c)
            body(TURNS - 2, 0)
            end(TURNS - 1, 1)

        wo_rows, w1_rows, w2_rows = (a.rearrange("(k p) n -> p k n", p=P) for a in (wo, w1, w2))
        per = PIECE // C
        pieces = ([(wo_rows[:, k:k + per, :], wo_sb, slice(k, k + per)) for k in range(0, KC, per)]
                  + [(w1_rows[:, k:k + 1, :], w1_sb, slice(k, k + 1)) for k in range(KC)]
                  + [(w2_rows[:, k:k + per, :], w2_sb, slice(k, k + per)) for k in range(0, FC, per)])
        assert HIDDEN == PIECE
        WO_PIECES = KC // per
        W1_PIECES = WO_PIECES + KC

        def raw_piece(n):
            k = pieces[n][2].stop - pieces[n][2].start
            return raw[:, n % STORES, :].rearrange("p (k c) -> p k c", k=k)

        @block.sync
        def _(eng):
            for r in (put_x3, put_z3):
                r.start(eng)

            def load(t, m):
                r_mixturn.wait(eng, t, m - M)
                eng.dma_start(mixt[:, m, :], rows(mixed, t, m)).then_inc(got_mix.sem(m), 16)
                r_x1.wait(eng, t, m - M)
                eng.dma_start(z0t[:, m, :], rows(z0, t, m)).then_inc(got_z0.sem(m), 16)
                r_part.wait(eng, t, m - M)
                eng.dma_start(xt[:, m, :], rows(x, t, m)).then_inc(got_x.sem(m), 16)

            def store(t, m):
                r_x3.wait(eng, t, m)
                eng.dma_start(rows(x3, t, m), x3t[:, m, :]).then_inc(put_x3.sem(m), 16)
                r_z3.wait(eng, t, m)
                eng.dma_start(rows(z3, t, m), z3t[:, m, :]).then_inc(put_z3.sem(m), 16)

            def load_piece(n):
                if n >= STORES:
                    eng.wait_ge(s_w_small, n - STORES + 1)
                eng.dma_start(raw_piece(n), pieces[n][0]).then_inc(s_raw[n % STORES], 16)

            def begin():
                for n in range(WO_PIECES):
                    load_piece(n)
                load(0, 0)
                for dst, a in ((bo_sb, bo), (gain, ln_g), (shift, ln_b), (b2_sb, b2)):
                    eng.dma_start(dst[:, :], a.partition_broadcast(P)).then_inc(s_b, 16)
                eng.dma_start(b1_sb[:, :], b1).then_inc(s_b, 16)
                for m in range(1, M):
                    load(0, m)
                for n in range(WO_PIECES, len(pieces)):
                    load_piece(n)
                for m in range(M):
                    load(1, m)

            def body(t, c):
                if not (isinstance(t, int) and t == TURNS - 2):
                    for m in range(M):
                        load(t + 2, m)
                for m in range(M):
                    store(t, m)

            def end(t, c):
                for m in range(M):
                    store(t, m)

            turns(begin, body, end, eng)
            for m in range(M):
                put_x3.wait(eng, TURNS - 1, m)
                put_z3.wait(eng, TURNS - 1, m)

        @block.gpsimd
        def _(eng):
            for r in (r_res, r_part, r_base):
                r.start(eng)
            eng.memset(ones[:, :], 1.0).then_inc(s_c, 1)
            eng.memset(eps[:, :], EPS).then_inc(s_c, 1)
            eng.wait_ge(s_c, 2)
            eng.affine_select(out=ident[:, :], in_=ones[:, :], compare_op=ALU.is_equal, fill=0.0, base=0,
                              pattern=[[1, P]], channel_multiplier=-1).then_inc(s_cut, 1)
            eng.wait_ge(s_b, 80)

            def sums(t, c):
                for m in range(M):
                    eng.wait_ge(got_z0.sem(m), t * 16 + 16)
                    eng.tensor_tensor(z0t[:, m, :], z0t[:, m, :], bo_sb[:, :], ALU.add).then_inc(r_res.sem(m), 1)
                for m in range(M):
                    r_x1.wait(eng, t, m)
                    eng.wait_ge(got_x.sem(m), t * 16 + 16)
                    eng.tensor_tensor(base[:, c, m, :], x1[:, m, :], xt[:, m, :], ALU.add).then_inc(r_part.sem(m), 1)
                    r_part.wait(eng, t, m)
                    eng.tensor_tensor(base[:, c, m, :], base[:, c, m, :], b2_sb[:, :], ALU.add).then_inc(r_base.sem(m), 1)

            turns(lambda: sums(0, 0), lambda t, c: sums(t + 1, 1 - c), lambda t, c: None, eng)

        @block.vector
        def _(eng):
            for r in (r_mix_small, r_x1, r_z, r_z_small, r_h_small, r_x3, r_z3):
                r.start(eng)

            def split(whole, halves):
                return nc.vector.tensor_tensor(halves[1], whole, halves[0], ALU.subtract)

            def weights(those):
                for n in those:
                    _, dst, k = pieces[n]
                    eng.wait_ge(s_w_large, n + 1)
                    split(raw_piece(n), (dst[:, LARGE, k, :], dst[:, SMALL, k, :])).then_inc(s_w_small, 1)

            def mix_small(t):
                for m in range(M):
                    r_mix_large.wait(eng, t, m)
                    split(turned[m][:, :], (mixT[:, LARGE, m, :], mixT[:, SMALL, m, :])).then_inc(r_mix_small.sem(m), 1)

            def spread(st, n, m, whole, s_var):
                st.link(nc.vector.bn_stats(stats[:, n, m, :], whole))
                eng.sem_inc(s_passed, 1)
                nc.vector.bn_aggr(mean_var[:, n, m, :], stats[:, n, m, :]).then_inc(s_var, 1)

            def scaled(st, n, m, whole, s_root, value, out):
                eng.wait_ge(s_root, value)
                st.link(nc.vector.reciprocal(root[:, n, m:m + 1], root[:, n, m:m + 1]))
                return nc.vector.tensor_scalar(out, whole, mean_var[:, n, m, 0:1], root[:, n, m:m + 1], ALU.subtract, ALU.mult)

            def attended(t):
                st = Steps(eng, s_a, t, 4 * M)
                for m in range(M):
                    r_o.wait(eng, t, m)
                    r_res.wait(eng, t, m)
                    r_base.wait(eng, t, m - M)
                    nc.vector.tensor_tensor(x1[:, m, :], o_ps[m][:, :], z0t[:, m, :], ALU.add).then_inc(r_x1.sem(m), 1)
                    r_x1.wait(eng, t, m)
                    spread(st, 0, m, x1[:, m, :], s_var_a)
                for m in range(M):
                    st.link(scaled(st, 0, m, x1[:, m, :], s_root_a, t * M + m + 1, zn[:, :]))
                    st.link(nc.vector.tensor_tensor(zn[:, :], zn[:, :], gain[:, :], ALU.mult))
                    r_zturn.wait(eng, t, m - M)
                    nc.vector.tensor_tensor(z[:, m, :], zn[:, :], shift[:, :], ALU.add).then_inc(r_z.sem(m), 1)
                assert st.n == 4 * M

            def hidden_small(t):
                for f in range(FC):
                    r_h_large.wait(eng, t, f)
                    split(h[:, f, :], (hT[:, LARGE, f, :], hT[:, SMALL, f, :])).then_inc(r_h_small.sem(f), 1)

            def z_small(t):
                for m in range(M):
                    r_z_large.wait(eng, t, m)
                    mine = slice(m * P, (m + 1) * P)
                    split(turned[m][:, :].rearrange("p (k r) -> p k r", r=P),
                          (zT[:, LARGE, :, mine], zT[:, SMALL, :, mine])).then_inc(r_z_small.sem(m), 1)

            def ended(t, c):
                for m in range(M):
                    st = Steps(eng, s_e, t, 2 * M, 2 * m)
                    r_down.wait(eng, t, m)
                    r_base.wait(eng, t, m)
                    put_x3.wait(eng, t, m - M)
                    nc.vector.tensor_tensor(x3t[:, m, :], down_ps[m][:, :], base[:, c, m, :], ALU.add).then_inc(r_x3.sem(m), 1)
                    r_x3.wait(eng, t, m)
                    put_z3.wait(eng, t, m - M)
                    spread(st, 1, m, x3t[:, m, :], s_var_e)
                    scaled(st, 1, m, x3t[:, m, :], s_root_e, t * M + m + 1, z3t[:, m, :]).then_inc(r_z3.sem(m), 1)
                    assert st.n == 2

            def begin():
                weights(range(WO_PIECES))
                eng.wait_ge(s_b, 80)
                mix_small(0)
                weights(range(WO_PIECES, W1_PIECES))
                attended(0)
                z_small(0)
                weights(range(W1_PIECES, len(pieces)))

            def body(t, c):
                mix_small(t + 1)
                hidden_small(t)
                attended(t + 1)
                z_small(t + 1)
                ended(t, c)

            turns(begin, body, lambda t, c: (hidden_small(t), ended(t, c)), eng)

        @block.scalar
        def _(eng):
            for r in (r_mix_large, r_z_large, r_h, r_h_large):
                r.start(eng)

            def weights(those):
                for n in those:
                    _, dst, k = pieces[n]
                    eng.wait_ge(s_raw[n % STORES], n // STORES * 16 + 16)
                    nc.scalar.copy(dst[:, LARGE, k, :], raw_piece(n)).then_inc(s_w_large, 1)

            def mix_large(t):
                for m in range(M):
                    r_mixturn.wait(eng, t, m)
                    r_o.wait(eng, t, m - M)
                    nc.scalar.copy(mixT[:, LARGE, m, :], turned[m][:, :]).then_inc(r_mix_large.sem(m), 1)

            def roots(t, n, s_var, s_root):
                for m in range(M):
                    eng.wait_ge(s_var, t * M + m + 1)
                    nc.scalar.activation(root[:, n, m:m + 1], mean_var[:, n, m, 1:2], ACT.Sqrt, bias=eps[:, :]
                                         ).then_inc(s_root, 1)

            def hidden(t):
                for f in range(FC):
                    if f % 2 == 0:
                        r_up.wait(eng, t, f + 1)
                    r_h_small.wait(eng, t, f - FC)
                    nc.scalar.activation(h[:, f, :], up_ps[f // 2 % 2][:, f % 2, :], ACT.Silu, bias=b1_sb[:, f:f + 1]).then_inc(r_h.sem(f), 1)
                    r_h.wait(eng, t, f)
                    r_down.wait(eng, t, -1)
                    nc.scalar.copy(hT[:, LARGE, f, :], h[:, f, :]).then_inc(r_h_large.sem(f), 1)

            def columns(t):
                for m in range(M):
                    r_zturn.wait(eng, t, m)
                    nc.scalar.copy(zT[:, LARGE, :, m * P:(m + 1) * P],
                                   turned[m][:, :].rearrange("p (k r) -> p k r", r=P)).then_inc(r_z_large.sem(m), 1)

            def begin():
                weights(range(WO_PIECES))
                eng.wait_ge(s_c, 2)
                eng.wait_ge(s_b, 80)
                mix_large(0)
                weights(range(WO_PIECES, W1_PIECES))
                roots(0, 0, s_var_a, s_root_a)
                columns(0)
                weights(range(W1_PIECES, len(pieces)))

            def body(t, c):
                mix_large(t + 1)
                hidden(t)
                roots(t + 1, 0, s_var_a, s_root_a)
                columns(t + 1)
                roots(t, 1, s_var_e, s_root_e)

            turns(begin, body, lambda t, c: (hidden(t), roots(t, 1, s_var_e, s_root_e)), eng)

        @block.tensor
        def _(eng):
            for r in (r_mixturn, r_o, r_zturn, r_up, r_down):
                r.start(eng)
            eng.wait_ge(s_cut, 1)
            PASSES = ((LARGE, LARGE), (LARGE, SMALL), (SMALL, LARGE))

            def product(out, stationary, moving, chunks):
                for k in range(chunks):
                    for n, (a, b) in enumerate(PASSES):
                        last = nc.tensor.matmul(out, stationary(a, k), moving(b, k), start=(k == 0 and n == 0),
                                                stop=(k == chunks - 1 and n == len(PASSES) - 1))
                return last

            def turn(src, m, done):
                for kc in range(KC):
                    last = nc.tensor.transpose(turned[m][:, kc * P:(kc + 1) * P], src[:, m, kc * P:(kc + 1) * P], ident[:, :])
                last.then_inc(done.sem(m), 1)

            def turn_mixed(t):
                for m in range(M):
                    eng.wait_ge(got_mix.sem(m), t * 16 + 16)
                    r_z_small.wait(eng, t, m - M)
                    turn(mixt, m, r_mixturn)

            def attended(t):
                for m in range(M):
                    r_mix_small.wait(eng, t, m)
                    product(o_ps[m][:, :], lambda a, k: mixT[:, a, m, k * P:(k + 1) * P],
                            lambda b, k: wo_sb[:, b, k, :], KC).then_inc(r_o.sem(m), 1)

            def up(t):
                r_z_small.wait(eng, t, M - 1)
                for f in range(FC):
                    if f % 2 == 0:
                        r_h.wait(eng, t, f - 3)
                    product(up_ps[f // 2 % 2][:, f % 2, :], lambda a, k: w1_sb[:, a, k, f * P:(f + 1) * P],
                            lambda b, k: zT[:, b, k, :], KC).then_inc(r_up.sem(f), 1)

            def turn_z(t):
                for m in range(M):
                    r_z.wait(eng, t, m)
                    turn(z, m, r_zturn)

            def down(t, m):
                if m == 0:
                    eng.wait_ge(s_w_small, len(pieces))
                    r_h_small.wait(eng, t, FC - 1)
                r_x3.wait(eng, t, m - M)
                product(down_ps[m][:, :], lambda a, k: hT[:, a, k, m * P:(m + 1) * P],
                        lambda b, k: w2_sb[:, b, k, :], FC).then_inc(r_down.sem(m), 1)

            def begin():
                eng.wait_ge(s_w_small, WO_PIECES)
                turn_mixed(0)
                attended(0)
                turn_z(0)
                eng.wait_ge(s_w_small, W1_PIECES)

            def body(t, c):
                turn_mixed(t + 1)
                up(t)
                attended(t + 1)
                down(t, 0)
                turn_z(t + 1)
                down(t, 1)

            turns(begin, body, lambda t, c: (up(t), down(t, 0), down(t, 1)), eng)


def experts(nc, moved, count, x3, z3, router, w1, b1, w2, b2, gamma, beta, by_slot, out):
    EPS = 1e-6
    BIG = 3.0e38
    KC = C // P
    T = NODES // P
    E, _, F = w1.shape
    FC = F // P
    TOP = 2
    SLOTS = TOP * T + E
    TURN = 8
    TURNS = SLOTS // TURN
    assert SLOTS % TURN == 0
    HALF = 4
    SUM_TURNS = T // HALF
    LIST_TURNS = 4
    CHUNK = T // LIST_TURNS
    with ExitStack() as ctx:
        def sb(name, shape, dt=F32):
            return ctx.enter_context(nc.sbuf_tensor("m_" + name, shape, dt))

        def ps(name, shape, dt=F32):
            return ctx.enter_context(nc.psum_tensor("m_" + name, shape, dt))

        used = []

        def sem(name):
            used.append(ctx.enter_context(nc.semaphore("ms_" + name)))
            return used[-1]

        w1_sb, w2_sb = sb("w1", [P, E, KC, F]), sb("w2", [P, E, FC, C])
        gamma_sb, beta_sb, b2_sb = sb("gamma", [P, E, C]), sb("beta", [P, E, C]), sb("b2", [P, E, C])
        b1_sb, router_sb = sb("b1", [P, E, FC]), sb("router", [P, KC, E])
        ones, ident, earlier = sb("ones", [P, P]), sb("ident", [P, P]), sb("earlier", [P, P])
        zeros, eps = sb("zeros", [P, P]), sb("eps", [P, 1])
        falling = sb("falling", [P, E])
        iota_p = sb("iota_p", [P, P])
        row_id = sb("row_id", [P, T])
        slot_at = sb("slot_at", [1, SLOTS])
        rows_sb = sb("rows", [P, TURN, C])
        zT = sb("zT", [P, 2, C])
        z_cols = sb("z_cols", [P, 2, KC, HALF * P])
        route_sb = sb("route", [E, 2, HALF * P])
        h_sb = sb("h", [P, 2, F])
        hT = sb("hT", [P, 2, FC, P])
        res = sb("res", [P, 2, C])
        y = sb("y", [P, 4, C])
        acc = sb("acc", [P, 4, C])
        stats, mean_var, root = sb("stats", [P, 6]), sb("mv", [P, 2]), sb("root", [P, 1])
        logits = sb("logits", [P, T, E])
        first = sb("first", [P, T, E])
        one = sb("one", [P, TOP, T, E])
        top = sb("top", [P, TOP, T])
        rank = sb("rank", [P, T])
        both = sb("both", [P, T, E])
        ratio = sb("ratio", [P, T])
        gate = sb("gate", [P, TOP, T])
        begun = sb("begun", [P, T + 1, E])
        filled_i = sb("filled_i", [P, E], I32)
        filled = sb("filled", [P, E])
        ends = sb("ends", [P, E])
        start = sb("start", [P, E])
        slot = sb("slot", [P, T, E])
        place = sb("place", [P, TOP, T])
        place_i = sb("place_i", [P, TOP, T], I32)
        part_i = sb("part_i", [P, TOP, T], I32)
        tile_f, part_f = sb("tile_f", [P, TOP, T]), sb("part_f", [P, TOP, T])
        part_hot = sb("part_hot", [P, TOP, CHUNK, P], mybir.dt.float32r)
        tile_hot = sb("tile_hot", [P, CHUNK, SLOTS])
        tile_id = sb("tile_id", [P, TOP, CHUNK, SLOTS], mybir.dt.float32r)
        passed_at = sb("passed_at", [1, SLOTS, E])
        expert_f = sb("expert_f", [1, SLOTS])
        expert_of = sb("expert_of", [1, SLOTS], I32)
        row_of = sb("row_of", [P, SLOTS], I32)
        index = sb("index", [P, 2, HALF], I32)
        turned = [ps(f"turned{b}", [P, C]) for b in range(2)]
        up_ps = [ps(f"up{b}", [P, F]) for b in range(2)]
        h_turned = [ps(f"h_turned{b}", [P, F]) for b in range(2)]
        down_ps = [ps(f"down{b}", [P, C]) for b in range(2)]
        route_ps = [p[0:E, :] for p in down_ps]
        route_turned = [p[:, 0:HALF * E] for p in up_ps]
        within = down_ps[0][:, 0:T * E]
        total = down_ps[0][:, T * E:]
        list_ps = down_ps[1][:, 0:SLOTS]

        s_w, s_c, s_cut, s_dve, s_low, s_ratio = (sem(n) for n in ("w", "c", "cut", "dve", "low", "ratio"))
        s_both, s_counted, s_open, s_list, s_ready = (sem(n) for n in ("both", "counted", "open", "list", "ready"))
        s_norm, s_passed, s_passed_v, s_passed_pe, s_sum = (sem(n) for n in ("norm", "passed", "passed_v", "passed_pe", "sum"))
        r_load = Ring([sem(f"load{b}") for b in range(TURN)], TURN, 16)
        r_turn, r_zT = (Ring([sem(n)], TURN) for n in ("turn", "zT"))
        r_route, r_route_sb, r_route_turned, r_kept = (Ring([sem(n)], 2) for n in ("route", "route_sb", "route_turned", "kept"))
        r_hot, r_listed = (Ring([sem(n)], TOP) for n in ("hot", "listed"))
        names = ("e_turn", "e_zT", "e_up", "e_h", "e_hturn", "e_hT", "e_down", "e_res", "e_y", "e_var", "e_root",
                 "e_norm", "e_gain", "e_done", "e_index")
        (e_turn, e_zT, e_up, e_h, e_hturn, e_hT, e_down, e_res, e_y, e_var, e_root, e_norm, e_gain, e_done) = (
            Ring([sem(n)], TURN) for n in names[:-1])
        e_index = Ring([sem("e_index")], 2)
        e_put = Ring([sem(f"e_put{b}") for b in range(4)], TURN, 16)
        got = moved[16:16 + TURN]
        got_y = moved[24:24 + TOP * HALF]
        c_index, c_sum = Ring([sem("c_index")], 2), Ring([sem("c_sum")], HALF)
        c_x3, c_out = (Ring([sem(f"{n}{b}") for b in range(HALF)], HALF, 16) for n in ("c_x3", "c_out"))
        block = open_block(nc, ctx, used)

        def tile_rows(a, i, per, u):
            v = a.rearrange("(n p) c -> n p c", p=P)
            return v[bass.ds(i * per + u, 1), :, :].rearrange("a p c -> (a p) c")

        def by_turn(eng, turns, body):
            with eng.Fori(0, turns - 1) as i:
                body(i, True)
            body(turns - 1, False)

        def expert(eng, i, u):
            return bass.ds(eng.value_load(expert_of[0:1, bass.ds(i * TURN + u, 1)], min_val=0, max_val=E - 1), 1)

        def flat(x):
            return x.rearrange("p a c -> p (a c)")

        @block.sync
        def _(eng):
            for r in (e_put, c_out):
                r.start(eng)
            eng.dma_start(router_sb[:, :, :], router.rearrange("(k p) e -> p k e", p=P)).then_inc(s_c, 16)
            for u in range(TURN):
                eng.dma_start(rows_sb[:, u, :], z3[u * P:(u + 1) * P, :]).then_inc(r_load.sem(u), 16)

            def load(i, more):
                if more:
                    for u in range(TURN):
                        r_turn.wait(eng, i, u)
                        eng.dma_start(rows_sb[:, u, :], tile_rows(z3, i + 1, TURN, u)).then_inc(r_load.sem(u), 16)

            by_turn(eng, T // TURN, load)
            eng.dma_start(b1_sb[:, :, :], b1).then_inc(s_w, 16)
            eng.dma_start(w1_sb[:, :, :, :], w1.rearrange("e (k p) f -> p e k f", p=P)).then_inc(s_w, 16)
            eng.dma_start(w2_sb[:, :, :, :], w2.rearrange("e (k p) c -> p e k c", p=P)).then_inc(s_w, 16)
            for dst, a in ((b2_sb, b2), (gamma_sb, gamma), (beta_sb, beta)):
                eng.dma_start(flat(dst[:, :, :]), a.rearrange("e c -> (e c)").partition_broadcast(P)).then_inc(s_w, 16)
            for u in range(HALF):
                eng.dma_start(acc[:, u, :], x3[u * P:(u + 1) * P, :]).then_inc(c_x3.sem(u), 16)

            def store(i, more):
                for u in range(TURN):
                    e_done.wait(eng, i, u)
                    eng.dma_start(tile_rows(by_slot, i, TURN, u), y[:, u % 4, :]).then_inc(e_put.sem(u), 16)

            by_turn(eng, TURNS, store)

            with eng.Fori(0, SUM_TURNS) as i:
                for u in range(HALF):
                    c_sum.wait(eng, i, u)
                    eng.dma_start(tile_rows(out, i, HALF, u), acc[:, u, :]).then_inc(c_out.sem(u), 16)
            for u in range(HALF):
                c_out.wait(eng, SUM_TURNS - 1, u)

        @block.gpsimd
        def _(eng):
            for r in (e_res, e_gain):
                r.start(eng)
            for a, value in ((ones, 1.0), (zeros, 0.0), (eps, EPS)):
                eng.memset(a[:, :], value).then_inc(s_cut, 1)
            for a, step, n, down, base in ((falling, -1, E, 0, E), (iota_p, 1, P, 0, 0), (row_id, P, T, 1, 0),
                                           (slot_at, P, SLOTS, 0, 0)):
                eng.iota(a[:, :], pattern=[[step, n]], base=base, channel_multiplier=down,
                         allow_small_or_imprecise_dtypes=True).then_inc(s_cut, 1)
            eng.wait_ge(s_cut, 7)
            for m, op in ((ident, ALU.is_equal), (earlier, ALU.is_gt)):
                eng.affine_select(out=m[:, :], in_=ones[:, :], compare_op=op, fill=0.0, base=0,
                                  pattern=[[1, P]], channel_multiplier=-1).then_inc(s_cut, 1)

            def lay_out(i, half):
                for n in range(HALF):
                    eng.wait_ge(got[half * HALF + n], i * 16 + count)
                eng.tensor_copy(index[:, half, :], row_of[:, bass.ds(i * TURN + half * HALF, HALF)]
                                ).then_inc(e_index.sem(half), 1)
                e_index.wait(eng, i, half)

            def gather(i, u):
                e_turn.wait(eng, i, u - TURN)
                e_res.wait(eng, i, u - TURN)
                eng.sem_inc(s_passed, 1)
                eng.indirect_dma_start(rows_sb[:, u, :], None, z3,
                                       bass.IndirectOffsetOnAxis(index[:, u // HALF, u % HALF:u % HALF + 1], 0)
                                       ).then_inc(got[u], 16)

            def residual(i, u):
                e = expert(eng, i, u)
                e_y.wait(eng, i, u - 2)
                eng.wait_ge(got[u % TURN], i * 16 + (count + 16 + u // TURN * 16))
                eng.tensor_tensor(res[:, u % 2, :], rows_sb[:, u % TURN, :], flat(b2_sb[:, e, :]),
                                  ALU.add).then_inc(e_res.sem(u), 1)

            def body(i, more):
                for u in range(TURN):
                    if u == 0:
                        lay_out(i, 1)
                    if u < HALF:
                        gather(i, u + HALF)
                    elif more:
                        if u == HALF:
                            lay_out(i + 1, 0)
                        gather(i + 1, u - HALF)
                    if u < TURN - 1 or more:
                        residual(i, u + 1)
                    e = expert(eng, i, u)
                    e_norm.wait(eng, i, u)
                    eng.tensor_tensor(y[:, u % 4, :], y[:, u % 4, :], flat(gamma_sb[:, e, :]),
                                      ALU.mult).then_inc(e_gain.sem(u), 1)

            e_index.start(eng)
            c_index.start(eng)
            eng.wait_ge(s_ready, 1)
            eng.wait_ge(s_w, 96)
            lay_out(0, 0)
            for u in range(HALF):
                gather(0, u)
            residual(0, 0)
            by_turn(eng, TURNS, body)
            for u in range(4):
                e_put.wait(eng, TURNS - 1, TURN - 4 + u)
            with eng.Fori(0, SUM_TURNS) as i:
                for half in range(2):
                    mine = range(half * 2, half * 2 + 2)
                    for n in range(4):
                        eng.wait_ge(got_y[half * 4 + n], i * 16 + count)
                    eng.tensor_copy(index[:, half, :].rearrange("p (n c) -> p c n", c=TOP),
                                    place_i[:, :, bass.ds(i * HALF + half * 2, 2)]).then_inc(c_index.sem(half), 1)
                    c_index.wait(eng, i, half)
                    for u in mine:
                        c_sum.wait(eng, i, u - HALF)
                        eng.sem_inc(s_passed, 1)
                        for c in range(TOP):
                            n = u * TOP + c
                            eng.indirect_dma_start(rows_sb[:, n, :], None, by_slot,
                                                   bass.IndirectOffsetOnAxis(index[:, half, n % 4:n % 4 + 1], 0)
                                                   ).then_inc(got_y[n], 16)

        @block.scalar
        def _(eng):
            for r in (r_zT, e_zT, e_h, e_hT):
                r.start(eng)
            eng.wait_ge(s_cut, 9)
            with eng.Fori(0, T // TURN) as i:
                for u in range(TURN):
                    m, half = u % HALF, u // HALF
                    r_turn.wait(eng, i, u)
                    if m == 0:
                        r_route.wait(eng, i, half - 2)
                    nc.scalar.copy(z_cols[:, half, :, m * P:(m + 1) * P],
                                   turned[u % 2][:, :].rearrange("p (k r) -> p k r", r=P)).then_inc(r_zT.sem(u), 1)
            eng.wait_ge(s_low, 1)
            nc.scalar.activation(ratio[:, :], ratio[:, :], ACT.Exp).then_inc(s_ratio, 1)
            eng.wait_ge(s_ready, 1)
            eng.wait_ge(s_w, 96)

            def columns(i, u):
                e_turn.wait(eng, i, u)
                e_up.wait(eng, i, u - 2)
                nc.scalar.copy(zT[:, u % 2, :], turned[u % 2][:, :]).then_inc(e_zT.sem(u), 1)

            def hidden(i, u):
                e_up.wait(eng, i, u)
                e_hturn.wait(eng, i, u - 2)
                nc.scalar.copy(h_sb[:, u % 2, :], up_ps[u % 2][:, :]).then_inc(e_h.sem(u), 1)

            def hidden_columns(i, u):
                e = expert(eng, i, u)
                e_hturn.wait(eng, i, u)
                e_down.wait(eng, i, u - 2)
                for f in range(FC):
                    last = nc.scalar.activation(hT[:, u % 2, f, :], h_turned[u % 2][:, f * P:(f + 1) * P], ACT.Relu,
                                                bias=flat(b1_sb[:, e, f:f + 1]))
                last.then_inc(e_hT.sem(u), 1)

            columns(0, 0)
            columns(0, 1)
            hidden(0, 0)
            hidden_columns(0, 0)

            def body(i, more):
                for u in range(TURN):
                    if u < TURN - 2 or more:
                        columns(i, u + 2)
                    if u < TURN - 1 or more:
                        hidden(i, u + 1)
                        hidden_columns(i, u + 1)
                    e_var.wait(eng, i, u)
                    nc.scalar.activation(root[:, :], mean_var[:, 1:2], ACT.Sqrt, bias=eps[:, :]).then_inc(e_root.sem(u), 1)

            e_root.start(eng)
            by_turn(eng, TURNS, body)
            with eng.Fori(0, SUM_TURNS - 1) as i:
                for u in range(HALF):
                    c_out.wait(eng, i, u)
                    eng.dma_start(acc[:, u, :], tile_rows(x3, i + 1, HALF, u)).then_inc(c_x3.sem(u), 16)

        @block.vector
        def _(eng):
            for r in (r_route_sb, r_kept, r_hot, e_y, e_var, e_norm, e_done, c_sum):
                r.start(eng)
            st = Steps(eng, s_dve)
            with eng.Fori(0, T // TURN) as i:
                for half in range(2):
                    r_route.wait(eng, i, half)
                    r_route_turned.wait(eng, i, half - 2)
                    nc.vector.tensor_copy(route_sb[:, half, :], route_ps[half]).then_inc(r_route_sb.sem(half), 1)
                    r_route_turned.wait(eng, i, half)
                    nc.vector.tensor_copy(logits[:, bass.ds(i * TURN + half * HALF, HALF), :],
                                          route_turned[half].rearrange("p (m e) -> p m e", e=E)).then_inc(r_kept.sem(half), 1)
            r_kept.wait(eng, T // TURN - 1, 1)
            eng.wait_ge(s_cut, 9)

            def over_experts(x):
                return x.unsqueeze(2).broadcast_to([P, T, E])

            order = falling[:, :].unsqueeze(1).broadcast_to([P, T, E])
            for c in range(TOP):
                st.link(nc.vector.tensor_reduce(top[:, c, :], logits[:, :, :], AX.X, ALU.max))
                st.link(nc.vector.tensor_tensor(first[:, :, :], logits[:, :, :], over_experts(top[:, c, :]), ALU.is_equal))
                st.link(nc.vector.tensor_tensor(first[:, :, :], first[:, :, :], order, ALU.mult))
                st.link(nc.vector.tensor_reduce(rank[:, :], first[:, :, :], AX.X, ALU.max))
                st.link(nc.vector.tensor_tensor(one[:, c, :, :], order, over_experts(rank[:, :]), ALU.is_equal))
                if c == 0:
                    st.link(nc.vector.scalar_tensor_tensor(logits[:, :, :], one[:, c, :, :], -BIG, logits[:, :, :],
                                                           ALU.mult, ALU.add))
            nc.vector.tensor_tensor(both[:, :, :], one[:, 0, :, :], one[:, 1, :, :], ALU.add).then_inc(s_both, 1)
            nc.vector.tensor_tensor(ratio[:, :], top[:, 1, :], top[:, 0, :], ALU.subtract).then_inc(s_low, 1)
            eng.wait_ge(s_counted, 1)
            st.link(nc.vector.memset(begun[:, 0, :], 0.0))
            for e in range(E):
                last = nc.vector.tensor_tensor_scan(begun[:, 1:, e], zeros[:, 0:T],
                                                    total.rearrange("p (t e) -> p t e", e=E)[:, :, e], 0.0,
                                                    ALU.add, ALU.add)
            st.link(last)
            st.link(nc.vector.tensor_scalar(filled_i[:, :], begun[:, T, :], float(P - 1), None, ALU.add))
            st.link(nc.vector.tensor_scalar(filled_i[:, :], filled_i[:, :], P.bit_length() - 1, None, ALU.arith_shift_right))
            st.link(nc.vector.tensor_scalar(filled[:, :], filled_i[:, :], float(P), None, ALU.mult))
            st.link(nc.vector.tensor_tensor_scan(ends[:, :], zeros[:, 0:E], filled[:, :], 0.0, ALU.add, ALU.add))
            st.link(nc.vector.tensor_tensor(start[:, :], ends[:, :], filled[:, :], ALU.subtract))
            st.link(nc.vector.tensor_tensor(slot[:, :, :], begun[:, 0:T, :], within.rearrange("p (t e) -> p t e", e=E), ALU.add))
            st.link(nc.vector.tensor_tensor(slot[:, :, :], slot[:, :, :],
                                            start[:, :].unsqueeze(1).broadcast_to([P, T, E]), ALU.add))
            for c in range(TOP):
                st.link(nc.vector.tensor_tensor(first[:, :, :], slot[:, :, :], one[:, c, :, :], ALU.mult))
                st.link(nc.vector.tensor_reduce(place[:, c, :], first[:, :, :], AX.X, ALU.add))
            st.link(nc.vector.tensor_copy(place_i[:, :, :], place[:, :, :]))
            st.link(nc.vector.tensor_scalar(part_i[:, :, :], place_i[:, :, :], 7, None, ALU.arith_shift_right))
            st.link(nc.vector.tensor_copy(tile_f[:, :, :], part_i[:, :, :]))
            st.link(nc.vector.tensor_scalar(part_i[:, :, :], place_i[:, :, :], P - 1, None, ALU.bitwise_and))
            st.link(nc.vector.tensor_copy(part_f[:, :, :], part_i[:, :, :]))
            st.link(nc.vector.tensor_tensor(passed_at[:, :, :], slot_at[:, :].unsqueeze(2).broadcast_to([1, SLOTS, E]),
                                            ends[0:1, :].unsqueeze(1).broadcast_to([1, SLOTS, E]), ALU.is_ge))
            st.link(nc.vector.tensor_reduce(expert_f[:, :], passed_at[:, :, :], AX.X, ALU.add))
            st.link(nc.vector.tensor_scalar(expert_of[:, :], expert_f[:, :], float(E - 1), None, ALU.min))
            eng.wait_ge(s_ratio, 1)
            st.link(nc.vector.tensor_scalar(gate[:, 0, :], ratio[:, :], 1.0, None, ALU.add))
            st.link(nc.vector.reciprocal(gate[:, 0, :], gate[:, 0, :]))
            st.link(nc.vector.tensor_tensor(gate[:, 1, :], gate[:, 0, :], ratio[:, :], ALU.mult))
            with eng.Fori(0, LIST_TURNS) as i:
                for c in range(TOP):
                    r_listed.wait(eng, i, c - TOP)
                    r_hot.wait(eng, i, c - 1)
                    mine = bass.ds(i * CHUNK, CHUNK)
                    st2 = Steps(eng, s_list, i, TOP, c)
                    nc.vector.tensor_tensor(part_hot[:, c, :, :], iota_p[:, :].unsqueeze(1).broadcast_to([P, CHUNK, P]),
                                            part_f[:, c, mine].unsqueeze(2).broadcast_to([P, CHUNK, P]), ALU.is_equal)
                    st2.link(nc.vector.tensor_tensor(
                        tile_hot[:, :, :], iota_p[:, 0:SLOTS].unsqueeze(1).broadcast_to([P, CHUNK, SLOTS]),
                        tile_f[:, c, mine].unsqueeze(2).broadcast_to([P, CHUNK, SLOTS]), ALU.is_equal))
                    nc.vector.tensor_tensor(tile_id[:, c, :, :], tile_hot[:, :, :],
                                            row_id[:, mine].unsqueeze(2).broadcast_to([P, CHUNK, SLOTS]), ALU.mult
                                            ).then_inc(r_hot.sem(c), 1)
            eng.wait_ge(s_open, 2)
            nc.vector.tensor_copy(row_of[:, :], list_ps).then_inc(s_ready, 1)
            eng.wait_ge(s_w, 96)

            def norm(i, u):
                per = Steps(eng, s_norm, i, 2 * TURN, 2 * u)
                mine = y[:, u % 4, :]
                e_down.wait(eng, i, u)
                e_res.wait(eng, i, u)
                e_put.wait(eng, i, u - 4)
                nc.vector.tensor_tensor(mine, down_ps[u % 2][:, :], res[:, u % 2, :], ALU.add).then_inc(e_y.sem(u), 1)
                e_y.wait(eng, i, u)
                per.link(nc.vector.bn_stats(stats[:, :], mine))
                eng.sem_inc(s_passed_v, 1)
                nc.vector.bn_aggr(mean_var[:, :], stats[:, :]).then_inc(e_var.sem(u), 1)
                e_root.wait(eng, i, u)
                per.link(nc.vector.reciprocal(root[:, :], root[:, :]))
                nc.vector.tensor_scalar(mine, mine, mean_var[:, 0:1], root[:, :], ALU.subtract, ALU.mult
                                        ).then_inc(e_norm.sem(u), 1)

            def shift(i, u):
                e = expert(eng, i, u)
                e_gain.wait(eng, i, u)
                nc.vector.tensor_tensor(y[:, u % 4, :], y[:, u % 4, :], flat(beta_sb[:, e, :]),
                                        ALU.add).then_inc(e_done.sem(u), 1)

            with eng.Fori(0, TURNS) as i:
                for u in range(TURN):
                    norm(i, u)
                    if u:
                        shift(i, u - 1)
                shift(i, TURN - 1)
            with eng.Fori(0, SUM_TURNS) as i:
                for u in range(HALF):
                    per = Steps(eng, s_sum, i, HALF, u)
                    eng.wait_ge(c_x3.sem(u), i * 16 + 16)
                    for c in range(TOP):
                        eng.wait_ge(got_y[u * TOP + c], i * 16 + (count + 16))
                    n = bass.ds(i * HALF + u, 1)
                    per.link(nc.vector.scalar_tensor_tensor(acc[:, u, :], rows_sb[:, u * TOP, :], gate[:, 0, n],
                                                            acc[:, u, :], ALU.mult, ALU.add))
                    nc.vector.scalar_tensor_tensor(acc[:, u, :], rows_sb[:, u * TOP + 1, :], gate[:, 1, n],
                                                   acc[:, u, :], ALU.mult, ALU.add).then_inc(c_sum.sem(u), 1)

        @block.tensor
        def _(eng):
            for r in (r_turn, r_route, r_route_turned, r_listed, e_turn, e_up, e_hturn, e_down):
                r.start(eng)
            eng.wait_ge(s_cut, 9)
            eng.wait_ge(s_c, 16)

            def turn(u, ring):
                for kc in range(KC):
                    last = nc.tensor.transpose(turned[u % 2][:, kc * P:(kc + 1) * P], rows_sb[:, u % TURN, kc * P:(kc + 1) * P],
                                               ident[:, :])
                last.then_inc(ring.sem(u), 1)

            def rows_turned(i, u):
                eng.wait_ge(r_load.sem(u), i * 16 + 16)
                r_zT.wait(eng, i, u - 2)
                turn(u, r_turn)

            def route(i, half):
                r_zT.wait(eng, i, half * HALF + HALF - 1)
                r_route_sb.wait(eng, i, half - 2)
                for kc in range(KC):
                    last = nc.tensor.matmul(route_ps[half], router_sb[:, kc, :], z_cols[:, half, kc, :],
                                            start=(kc == 0), stop=(kc == KC - 1))
                last.then_inc(r_route.sem(half), 1)

            def turn_route(i, half):
                r_route_sb.wait(eng, i, half)
                r_kept.wait(eng, i, half - 2)
                eng.sem_inc(s_passed_pe, 1)
                for m in range(HALF):
                    last = nc.tensor.transpose(route_turned[half][:, m * E:(m + 1) * E],
                                               route_sb[:, half, m * P:(m + 1) * P], ident[0:E, 0:E])
                last.then_inc(r_route_turned.sem(half), 1)

            with eng.Fori(0, T // TURN) as i:
                for half in range(2):
                    for m in range(HALF):
                        rows_turned(i, half * HALF + m)
                    if half == 1:
                        turn_route(i, 0)
                    route(i, half)
                turn_route(i, 1)
            eng.wait_ge(s_both, 1)
            nc.tensor.matmul(within, earlier[:, :], flat(both[:, :, :]), start=True, stop=True)
            nc.tensor.matmul(total, ones[:, :], flat(both[:, :, :]), start=True, stop=True).then_inc(s_counted, 1)
            nc.tensor.matmul(list_ps, zeros[:, :], iota_p[:, 0:SLOTS], start=True, stop=False).then_inc(s_open, 1)
            with eng.Fori(0, LIST_TURNS) as i:
                for c in range(TOP):
                    r_hot.wait(eng, i, c)
                    for m in range(CHUNK):
                        last = nc.tensor.matmul(list_ps, part_hot[:, c, m, :], tile_id[:, c, m, :], start=False, stop=False)
                    last.then_inc(r_listed.sem(c), 1)
            nc.tensor.matmul(list_ps, zeros[:, :], iota_p[:, 0:SLOTS], start=False, stop=True).then_inc(s_open, 1)
            eng.wait_ge(s_ready, 1)
            eng.wait_ge(s_w, 96)

            def turn_rows(i, u):
                eng.wait_ge(got[u % TURN], i * 16 + (count + 16 + u // TURN * 16))
                turn(u, e_turn)

            def up(i, u, e):
                e_zT.wait(eng, i, u)
                for kc in range(KC):
                    last = nc.tensor.matmul(up_ps[u % 2][:, :], zT[:, u % 2, kc * P:(kc + 1) * P], flat(w1_sb[:, e, kc, :]),
                                            start=(kc == 0), stop=(kc == KC - 1))
                last.then_inc(e_up.sem(u), 1)

            def turn_hidden(i, u):
                e_h.wait(eng, i, u)
                for f in range(FC):
                    last = nc.tensor.transpose(h_turned[u % 2][:, f * P:(f + 1) * P], h_sb[:, u % 2, f * P:(f + 1) * P],
                                               ident[:, :])
                last.then_inc(e_hturn.sem(u), 1)

            def down(i, u, e):
                e_hT.wait(eng, i, u)
                e_y.wait(eng, i, u - 2)
                for f in range(FC):
                    last = nc.tensor.matmul(down_ps[u % 2][:, :], hT[:, u % 2, f, :], flat(w2_sb[:, e, f, :]),
                                            start=(f == 0), stop=(f == FC - 1))
                last.then_inc(e_down.sem(u), 1)

            turn_rows(0, 0)
            turn_rows(0, 1)
            up(0, 0, expert(eng, 0, 0))
            turn_hidden(0, 0)

            def body(i, more):
                e = expert(eng, i, 0)
                for u in range(TURN):
                    this = e
                    if u < TURN - 2 or more:
                        turn_rows(i, u + 2)
                    if u < TURN - 1 or more:
                        e = expert(eng, i, u + 1)
                        up(i, u + 1, e)
                    down(i, u, this)
                    if u < TURN - 1 or more:
                        turn_hidden(i, u + 1)

            by_turn(eng, TURNS, body)


def graph_layer(nc, a, out):

    def scratch(name, shape, dt=F32):
        return nc.dram_tensor(name, shape, dt, kind="Internal").ap()

    with ExitStack() as ctx:
        moved = [ctx.enter_context(nc.semaphore(f"moved{n}")) for n in range(MOVES)]
        stages(nc, a, out, moved, scratch)


def stages(nc, a, out, moved, scratch):
    records = scratch("records", (P * TILES, REC))
    group_block = scratch("group_block", (-(-GROUPS // P) * P,), I32)
    low_row = scratch("low_row", (EDGES,), BF16)
    z0, q, k, v, mixed, x3, z3 = (scratch(f"t_{n}", (NODES, C)) for n in ("z0", "q", "k", "v", "mixed", "x3", "z3"))
    sort_and_project(nc, moved, a["src_t"], a["src"], a["dst_t"], a["bias_t"], low_row, records, group_block,
                     a["x"], a["L0_gnn_ln1_g"], a["L0_gnn_ln1_b"], a["L0_gnn_Wq"], a["L0_gnn_bq"], a["L0_gnn_Wk"],
                     a["L0_gnn_bk"], a["L0_gnn_Wv"], a["L0_gnn_bv"], z0, q, k, v)
    prep_count = 16 * (EDGES // P // MOVES + 1)
    attention(nc, moved, prep_count, records, group_block, q, k, v, mixed)
    out_and_ffn(nc, mixed, z0, a["x"], a["L0_gnn_Wo"], a["L0_gnn_bo"], a["L0_gnn_ln2_g"], a["L0_gnn_ln2_b"],
                a["L0_gnn_W1"], a["b1_t"], a["L0_gnn_W2"], a["L0_gnn_b2"], x3, z3)
    by_slot = scratch("by_slot", ((2 * NODES // P + a["L0_ffn_w1"].shape[0]) * P, C))
    experts(nc, moved, prep_count, x3, z3, a["L0_ffn_router_w"], a["L0_ffn_w1"], a["moe_b1_t"], a["L0_ffn_w2"],
            a["L0_ffn_b2"], a["L0_ffn_gamma"], a["L0_ffn_beta"], by_slot, out)


_PLAIN = ["x", "src", "L0_gnn_Wq", "L0_gnn_bq", "L0_gnn_Wk", "L0_gnn_bk", "L0_gnn_Wv", "L0_gnn_bv", "L0_gnn_Wo",
          "L0_gnn_bo", "L0_gnn_ln1_g", "L0_gnn_ln1_b", "L0_gnn_ln2_g", "L0_gnn_ln2_b", "L0_gnn_W1", "L0_gnn_W2",
          "L0_gnn_b2", "L0_ffn_router_w", "L0_ffn_w1", "L0_ffn_w2", "L0_ffn_b2", "L0_ffn_gamma", "L0_ffn_beta"]


def kernel(**inputs):
    import numpy as _np
    import concourse.bacc as _bacc
    from concourse import mybir as _mybir
    from concourse.bass_utils import run_bass_kernel_spmd as _run

    given = {name: _np.asarray(inputs[name]) for name in inputs}
    laid = {name: given[name] for name in _PLAIN}
    laid["src_t"] = given["src"].reshape(IN_TILES, P).T
    laid["dst_t"] = given["dst"].reshape(IN_TILES, P).T
    laid["bias_t"] = given["edge_attr_8"].reshape(IN_TILES, P, HEADS).transpose(1, 0, 2).reshape(P, IN_TILES * HEADS)
    laid["b1_t"] = given["L0_gnn_b1"].reshape(-1, P).T
    laid["moe_b1_t"] = given["L0_ffn_b1"].reshape(given["L0_ffn_b1"].shape[0], -1, P).transpose(2, 0, 1)

    nc = _bacc.Bacc("TRN2", target_bir_lowering=False, num_devices=1)
    arrays, args = {}, {}
    for name, a in laid.items():
        arrays[f"in_{name}"] = _np.ascontiguousarray(a)
        args[name] = nc.dram_tensor(f"in_{name}", a.shape, _mybir.dt.from_np(a.dtype), kind="ExternalInput").ap()
    out = nc.dram_tensor("out", (NODES, C), F32, kind="ExternalOutput").ap()
    graph_layer(nc, args, out)
    r = _run(nc, [arrays], core_ids=[0])
    return r.results[0]["out"]
```
